# Optimizing a Trainium2 kernel written in Bass

```python
import numpy as np
import jax
import jax.numpy as jnp

def _softmax(x, axis=-1):
    return jax.nn.softmax(x, axis=axis)

def _gelu(x):
    return jax.nn.gelu(x, approximate=True)

def _silu(x):
    return jax.nn.silu(x)

def _sigmoid(x):
    return jax.nn.sigmoid(x)

def _layernorm(x, axis=-1, eps=1e-05):
    m = jnp.mean(x, axis=axis, keepdims=True)
    v = jnp.var(x, axis=axis, keepdims=True)
    return (x - m) / jnp.sqrt(v + eps)

def _scatter_add(tgt, idx, src, axis=0):
    return tgt.at[idx].add(src)

def _segment_sum(src, seg, n):
    return jax.ops.segment_sum(src, seg, n)
kernel_name = 'mk_early_fusion_d1_tok_img768_r4_460766'

def setup_inputs(seed: int=0):
    np.random.seed(seed)
    _w = jnp.asarray

    def _rec_inputs():
        import jax
        import jax.numpy as jnp
        _rk = jax.random.key(seed)
        x = -0.000356955 + 1 * jax.random.normal(jax.random.fold_in(_rk, 1), (16, 3, 224, 224), jnp.float32)
        txt = -0.000682618 + 1.23071 * jax.random.normal(jax.random.fold_in(_rk, 2), (16, 128, 192), jnp.float32)
        return (x, txt)
    x, txt = _rec_inputs()

    def _L0_tok_setup():
        import jax, jax.numpy as jnp
        import numpy as np
        P = 16
        PW = P // 2 + 1
        EMBED = 192
        C_IN = 3
        NUM_PATCHES = 196
        key = jax.random.key(seed)
        ks = jax.random.split(key, 7)
        B, H, W = (128, 224, 224)
        in_feat = C_IN * P * PW
        return {'x': jax.random.normal(ks[0], (B, C_IN, H, W), dtype=jnp.float32), 'freq_weight_h': jnp.ones((P,), dtype=jnp.float32), 'freq_weight_w': jnp.ones((PW,), dtype=jnp.float32), 'proj_w': jax.random.normal(ks[1], (EMBED, in_feat), dtype=jnp.float32) / np.sqrt(in_feat), 'proj_b': jnp.zeros((EMBED,), dtype=jnp.float32), 'cls_token': jax.random.normal(ks[2], (1, 1, EMBED), dtype=jnp.float32), 'position_embeddings': jax.random.normal(ks[3], (1, NUM_PATCHES + 1, EMBED), dtype=jnp.float32)}
    _L0_tok_all = _L0_tok_setup()
    _L0_tok_in = {k: v for k, v in _L0_tok_all.items() if k in ('freq_weight_h', 'freq_weight_w', 'proj_w', 'proj_b', 'cls_token', 'position_embeddings')}
    del _L0_tok_all

    def _L0_attn_setup():
        import jax, jax.numpy as jnp
        import numpy as np
        B, L, D, H = (2, 512, 192, 12)
        HD = D // H
        ROPE_BASE = 10000.0

        def apply_rope(x):
            d = x.shape[-1]
            pos = jnp.arange(x.shape[2], dtype=jnp.float32)
            inv_freq = 1.0 / ROPE_BASE ** (jnp.arange(0, d, 2, dtype=jnp.float32) / d)
            ang = pos[:, None] * inv_freq[None, :]
            cos = jnp.concatenate([jnp.cos(ang), jnp.cos(ang)], axis=-1)
            sin = jnp.concatenate([jnp.sin(ang), jnp.sin(ang)], axis=-1)
            x1, x2 = jnp.split(x, 2, axis=-1)
            rot = jnp.concatenate([-x2, x1], axis=-1)
            return x * cos[None, None, :, :].astype(x.dtype) + rot * sin[None, None, :, :].astype(x.dtype)
        key = jax.random.key(seed)
        ks = jax.random.split(key, 9)
        s = 1.0 / np.sqrt(D)
        return {'query': jax.random.normal(ks[0], (B, L, D), dtype=jnp.float32), 'Wq': jax.random.uniform(ks[1], (D, D), jnp.float32, -s, s), 'bq': jax.random.uniform(ks[2], (D,), jnp.float32, -s, s), 'Wk': jax.random.uniform(ks[3], (D, D), jnp.float32, -s, s), 'bk': jax.random.uniform(ks[4], (D,), jnp.float32, -s, s), 'Wv': jax.random.uniform(ks[5], (D, D), jnp.float32, -s, s), 'bv': jax.random.uniform(ks[6], (D,), jnp.float32, -s, s), 'Wo': jax.random.uniform(ks[7], (D, D), jnp.float32, -s, s), 'bo': jax.random.uniform(ks[8], (D,), jnp.float32, -s, s)}
    _L0_attn_all = _L0_attn_setup()
    _L0_attn_in = {k: v for k, v in _L0_attn_all.items() if k in ('Wq', 'bq', 'Wk', 'bk', 'Wv', 'bv', 'Wo', 'bo')}
    del _L0_attn_all

    def _L0_ffn_setup():
        import jax, jax.numpy as jnp
        import numpy as np
        EPS_NORM = 1e-06
        EPS_LN = 1e-05

        def _layernorm(x, g, b):
            mu = jnp.mean(x, axis=-1, keepdims=True)
            var = jnp.mean(jnp.square(x - mu), axis=-1, keepdims=True)
            return (x - mu) * jax.lax.rsqrt(var + EPS_LN) * g + b
        key = jax.random.key(seed)
        ks = jax.random.split(key, 6)
        b, m, d = (8, 256, 192)
        n, p = (64, 16)
        h = 2 * d
        x = jax.random.normal(ks[0], (b, m, d), dtype=jnp.float32)
        phi = jax.random.normal(ks[1], (n, p, d), dtype=jnp.float32)
        ln_g = jnp.ones((n, d), dtype=jnp.float32)
        ln_b = jnp.zeros((n, d), dtype=jnp.float32)
        w1 = jax.random.normal(ks[2], (n, d, h), dtype=jnp.float32) * (1.0 / np.sqrt(d))
        b1 = jax.random.normal(ks[3], (n, h), dtype=jnp.float32) * 0.01
        w2 = jax.random.normal(ks[4], (n, h, d), dtype=jnp.float32) * (1.0 / np.sqrt(h))
        b2 = jax.random.normal(ks[5], (n, d), dtype=jnp.float32) * 0.01
        return {'x': x, 'phi': phi, 'ln_g': ln_g, 'ln_b': ln_b, 'w1': w1, 'b1': b1, 'w2': w2, 'b2': b2}
    _L0_ffn_all = _L0_ffn_setup()
    _L0_ffn_in = {k: v for k, v in _L0_ffn_all.items() if k in ('phi', 'ln_g', 'ln_b', 'w1', 'b1', 'w2', 'b2')}
    del _L0_ffn_all
    return {'x': x, 'txt': txt, 'L0_tok_freq_weight_h': _L0_tok_in['freq_weight_h'], 'L0_tok_freq_weight_w': _L0_tok_in['freq_weight_w'], 'L0_tok_proj_w': _L0_tok_in['proj_w'], 'L0_tok_proj_b': _L0_tok_in['proj_b'], 'L0_tok_cls_token': _L0_tok_in['cls_token'], 'L0_tok_position_embeddings': _L0_tok_in['position_embeddings'], 'L0_attn_Wq': _L0_attn_in['Wq'], 'L0_attn_bq': _L0_attn_in['bq'], 'L0_attn_Wk': _L0_attn_in['Wk'], 'L0_attn_bk': _L0_attn_in['bk'], 'L0_attn_Wv': _L0_attn_in['Wv'], 'L0_attn_bv': _L0_attn_in['bv'], 'L0_attn_Wo': _L0_attn_in['Wo'], 'L0_attn_bo': _L0_attn_in['bo'], 'L0_ffn_phi': _L0_ffn_in['phi'], 'L0_ffn_ln_g': _L0_ffn_in['ln_g'], 'L0_ffn_ln_b': _L0_ffn_in['ln_b'], 'L0_ffn_w1': _L0_ffn_in['w1'], 'L0_ffn_b1': _L0_ffn_in['b1'], 'L0_ffn_w2': _L0_ffn_in['w2'], 'L0_ffn_b2': _L0_ffn_in['b2']}

def reference(x, txt, L0_tok_freq_weight_h, L0_tok_freq_weight_w, L0_tok_proj_w, L0_tok_proj_b, L0_tok_cls_token, L0_tok_position_embeddings, L0_attn_Wq, L0_attn_bq, L0_attn_Wk, L0_attn_bk, L0_attn_Wv, L0_attn_bv, L0_attn_Wo, L0_attn_bo, L0_ffn_phi, L0_ffn_ln_g, L0_ffn_ln_b, L0_ffn_w1, L0_ffn_b1, L0_ffn_w2, L0_ffn_b2):
    import jax
    import jax.numpy as jnp

    def _L0_tok_ref(x, freq_weight_h, freq_weight_w, proj_w, proj_b, cls_token, position_embeddings):
        import jax, jax.numpy as jnp
        import numpy as np
        P = 16
        PW = P // 2 + 1
        EMBED = 192
        C_IN = 3
        NUM_PATCHES = 196
        B, C, H, W = x.shape
        nH, nW = (H // P, W // P)
        N = nH * nW
        xp = x.reshape(B, C, nH, P, nW, P).transpose(0, 1, 2, 4, 3, 5).reshape(B, C, N, P, P)
        xf = jnp.fft.rfft2(xp, norm='ortho').real
        xf = xf * freq_weight_h[:, None] * freq_weight_w[None, :]
        xf = xf.transpose(0, 2, 1, 3, 4).reshape(B, N, C * P * PW)
        x_proj = xf @ proj_w.T + proj_b
        cls = jnp.broadcast_to(cls_token, (B, 1, EMBED))
        out = jnp.concatenate([cls, x_proj], axis=1) + position_embeddings
        return out

    def _L0_attn_ref(query, Wq, bq, Wk, bk, Wv, bv, Wo, bo):
        import jax, jax.numpy as jnp
        import numpy as np
        B, L, D, H = (2, 512, 192, 12)
        HD = D // H
        ROPE_BASE = 10000.0

        def apply_rope(x):
            d = x.shape[-1]
            pos = jnp.arange(x.shape[2], dtype=jnp.float32)
            inv_freq = 1.0 / ROPE_BASE ** (jnp.arange(0, d, 2, dtype=jnp.float32) / d)
            ang = pos[:, None] * inv_freq[None, :]
            cos = jnp.concatenate([jnp.cos(ang), jnp.cos(ang)], axis=-1)
            sin = jnp.concatenate([jnp.sin(ang), jnp.sin(ang)], axis=-1)
            x1, x2 = jnp.split(x, 2, axis=-1)
            rot = jnp.concatenate([-x2, x1], axis=-1)
            return x * cos[None, None, :, :].astype(x.dtype) + rot * sin[None, None, :, :].astype(x.dtype)
        b, l, _ = query.shape
        q = (query @ Wq.T + bq).reshape(b, l, H, HD).transpose(0, 2, 1, 3)
        k = (query @ Wk.T + bk).reshape(b, l, H, HD).transpose(0, 2, 1, 3)
        v = (query @ Wv.T + bv).reshape(b, l, H, HD).transpose(0, 2, 1, 3)
        q = apply_rope(q)
        k = apply_rope(k)
        scores = jnp.einsum('bhqd,bhkd->bhqk', q, k) / np.sqrt(HD).astype(np.float32)
        causal = jnp.triu(jnp.ones((l, l), dtype=bool), k=1)
        scores = jnp.where(causal[None, None, :, :], -jnp.inf, scores)
        attn = jax.nn.softmax(scores, axis=-1)
        out = jnp.einsum('bhqk,bhkd->bhqd', attn, v)
        out = out.transpose(0, 2, 1, 3).reshape(b, l, D)
        return out @ Wo.T + bo

    def _L0_ffn_ref(x, phi, ln_g, ln_b, w1, b1, w2, b2):
        import jax, jax.numpy as jnp
        import numpy as np
        EPS_NORM = 1e-06
        EPS_LN = 1e-05

        def _layernorm(x, g, b):
            mu = jnp.mean(x, axis=-1, keepdims=True)
            var = jnp.mean(jnp.square(x - mu), axis=-1, keepdims=True)
            return (x - mu) * jax.lax.rsqrt(var + EPS_LN) * g + b
        phi_n = phi * jax.lax.rsqrt(jnp.sum(jnp.square(phi), axis=0, keepdims=True) + EPS_NORM)
        bsz, m, d = x.shape
        n, p, _ = phi_n.shape
        logits = jnp.einsum('bmd,npd->bmnp', x, phi_n)
        D = jax.nn.softmax(logits, axis=1)
        C = jax.nn.softmax(logits.reshape(bsz, m, n * p), axis=-1)
        Xs = jnp.einsum('bmd,bmnp->bnpd', x, D)
        hdn = _layernorm(Xs, ln_g[:, None, :], ln_b[:, None, :])
        hdn = jnp.einsum('bnpd,ndh->bnph', hdn, w1) + b1[:, None, :]
        hdn = jax.nn.gelu(hdn, approximate=False)
        Ys = jnp.einsum('bnph,nhd->bnpd', hdn, w2) + b2[:, None, :]
        Ys = Ys.reshape(bsz, n * p, d)
        Y = jnp.einsum('bsd,bms->bmd', Ys, C)
        return Y
    h = _L0_tok_ref(x, L0_tok_freq_weight_h, L0_tok_freq_weight_w, L0_tok_proj_w, L0_tok_proj_b, L0_tok_cls_token, L0_tok_position_embeddings)
    h = jnp.concatenate([h, txt], axis=1)
    h = h + _L0_attn_ref(_layernorm(h, axis=-1), L0_attn_Wq, L0_attn_bq, L0_attn_Wk, L0_attn_bk, L0_attn_Wv, L0_attn_bv, L0_attn_Wo, L0_attn_bo)
    h = h + _L0_ffn_ref(_layernorm(h, axis=-1), L0_ffn_phi, L0_ffn_ln_g, L0_ffn_ln_b, L0_ffn_w1, L0_ffn_b1, L0_ffn_w2, L0_ffn_b2)
    return h

_drawn_inputs = setup_inputs


def setup_inputs(seed=0):
    import zlib

    import numpy as np

    out = dict(_drawn_inputs(seed))
    spreads = {'L0_tok_freq_weight_h': (1.0, 0.2),
     'L0_tok_freq_weight_w': (1.0, 0.2),
     'L0_tok_proj_b': (0.0, 0.1),
     'L0_ffn_ln_g': (1.0, 0.6),
     'L0_ffn_ln_b': (0.0, 0.8)}
    factors = {'L0_attn_Wq': 3.274,
     'L0_attn_bq': 8.0,
     'L0_attn_Wk': 3.793,
     'L0_attn_bk': 8.0,
     'L0_attn_bv': 2.749,
     'L0_ffn_b1': 64.0,
     'L0_ffn_b2': 42.949}
    for name, (base, spread) in spreads.items():
        noise = np.random.default_rng([zlib.crc32(name.encode()), seed]).standard_normal(out[name].shape)
        drawn = base * np.exp(spread * noise) if base else spread * noise
        out[name] = jnp.asarray(drawn.astype(out[name].dtype))
    for name, factor in factors.items():
        out[name] = (out[name] * factor).astype(out[name].dtype)
    return out
```

```python
from contextlib import ExitStack

import numpy as np

import concourse.bass as bass
from concourse import mybir

F32 = mybir.dt.float32
F32R = mybir.dt.float32r
BF16 = mybir.dt.bfloat16
ALU = mybir.AluOpType
ACT = mybir.ActivationFunctionType
AX = mybir.AxisListType

P = 128
D = 192
DB = D - P
B = 16
C_IN, IMG, PATCH = 3, 224, 16
NH = IMG // PATCH
NPATCH = NH * NH
TXT = 128
L = 1 + NPATCH + TXT
QT = 3
LAST = L - 2 * P
LE = L + L % 2
LASTE = LE - 2 * P
LP = QT * P
HEADS, HD = 12, 16
N_EXP, SLOTS_PER = 64, 16
S = N_EXP * SLOTS_PER
ST = S // P
EPT = P // SLOTS_PER
HID = 2 * D
HT = HID // P
KW = PATCH // 2 + 1
NF = PATCH * KW
FT = 4
FR = C_IN * NF // FT
SHIFTS = 2
PWS = PATCH // SHIFTS
ROWS = SHIFTS * C_IN * PATCH
NROW = NH // 2
PTOK = NROW * NH
LN_EPS = 1e-5
PHI_EPS = 1e-6
MASKED = -1e30
PRIME = 2
RING = 4


def shape_constants():
    k = np.arange(C_IN * NF)
    c, kh, kw = k // NF, (k % NF) // KW, k % KW
    ph = np.arange(PATCH)
    dft = np.zeros((C_IN * NF, PWS, SHIFTS, C_IN, PATCH), np.float64)
    for s in range(SHIFTS):
        for p in range(PWS):
            pw = p + PWS * s
            ang = 2 * np.pi * ((kh[:, None] * ph[None, :] + kw[:, None] * pw) % PATCH) / PATCH
            dft[k, p, s, c, :] = np.cos(ang) / PATCH
    dft = dft.reshape(FT, FR, PWS, ROWS).transpose(1, 0, 2, 3)
    sel_h = (np.arange(PATCH)[:, None] == kh[None, :]).astype(np.float32)
    sel_w = (np.arange(KW)[:, None] == kw[None, :]).astype(np.float32)
    inv = (1.0 / 10000.0 ** (np.arange(0, HD, 2, dtype=np.float32) / np.float32(HD))).astype(np.float32)
    ang = (np.arange(LP, dtype=np.float32)[:, None] * inv[None, :]).astype(np.float32)
    cos, sin = np.cos(ang.astype(np.float64)), np.sin(ang.astype(np.float64))
    rope = np.concatenate([cos, cos, -sin, sin], 1).reshape(QT, P, 4 * (HD // 2)).transpose(1, 0, 2)
    i = np.arange(P)
    return {
        "c_dft": np.ascontiguousarray(dft.astype(np.float32)),
        "c_selh": sel_h,
        "c_selw": sel_w,
        "c_rope": np.ascontiguousarray(rope.astype(np.float32)),
        "c_ident": np.eye(P, dtype=np.float32),
        "c_mask": np.where(i[None, :] > i[:, None], MASKED, 0.0).astype(np.float32),
        "c_maskT": np.where(i[:, None] > i[None, :], MASKED, 0.0).astype(np.float32),
    }


class Pool_:

    def __init__(self, nc, ctx, tag):
        self.nc, self.ctx, self.tag = nc, ctx, tag

    def sb(self, name, shape, dt=F32):
        return self.ctx.enter_context(self.nc.sbuf_tensor(f"{self.tag}_{name}", shape, dt))

    def bank(self, name):
        return self.ctx.enter_context(self.nc.psum_tensor(f"{self.tag}_{name}", [P, 512], F32))

    def sem(self, name):
        return self.ctx.enter_context(self.nc.semaphore(f"{self.tag}_{name}"))


def patch_phase(nc, x, txt, fh, fw, proj_w, proj_b, cls_token, pos, c_dft, c_selh, c_selw, c_ident, h_d):
    with ExitStack() as ctx:
        a = Pool_(nc, ctx, "pt")
        ident = a.sb("ident", [P, P])
        dft = a.sb("dft", [FR, FT, PWS, ROWS])
        selh = a.sb("selh", [PATCH, C_IN * NF])
        selw = a.sb("selw", [KW, C_IN * NF])
        fhc = a.sb("fhc", [PATCH, 1])
        fwc = a.sb("fwc", [KW, 1])
        pw_a = a.sb("pw_a", [P, C_IN * NF])
        pw_b = a.sb("pw_b", [DB, C_IN * NF])
        fsel = a.sb("fsel", [FR, 2 * FT])
        fcol = a.sb("fcol", [FR, FT])
        pT = a.sb("pT", [FR, FT, D])
        weff = a.sb("weff", [ROWS, PWS, D])
        ones = a.sb("ones", [1, P])
        brow = a.sb("brow", [1, D])
        clsr = a.sb("clsr", [1, D])
        pos0 = a.sb("pos0", [1, D])
        cls0 = a.sb("cls0", [1, D])
        clsb = a.sb("clsb", [B, D])
        posb = a.sb("posb", [PTOK, 2, D])
        img = [a.sb(f"img{u}", [ROWS, NH, IMG]) for u in range(2)]
        emb = [a.sb(f"emb{u}", [PTOK, 2, D]) for u in range(2)]
        bank = [a.bank(f"bank{i}") for i in range(8)]
        consts_in = a.sem("consts_in")
        ones_set = a.sem("ones_set")
        projT_done = a.sem("projT_done")
        fsel_done = a.sem("fsel_done")
        fsel_copied = a.sem("fsel_copied")
        fcol_done = a.sem("fcol_done")
        pT_ready = a.sem("pT_ready")
        weff_mm = a.sem("weff_mm")
        weff_ready = a.sem("weff_ready")
        bias_mm = a.sem("bias_mm")
        posb_ready = a.sem("posb_ready")
        cls0_ready = a.sem("cls0_ready")
        cls_mm = a.sem("cls_mm")
        clsb_ready = a.sem("clsb_ready")
        img_in = [a.sem(f"img_in{u}") for u in range(2)]
        emb_mm = a.sem("emb_mm")
        emb_ready = a.sem("emb_ready")
        emb_stored = [a.sem(f"emb_stored{u}") for u in range(2)]
        stored = a.sem("stored")
        N_CONST = 12
        block = ctx.enter_context(nc.Block())

        @block.sync
        def _(sp):
            sp.dma_start(h_d[:, 1 + NPATCH:L, :], txt).then_inc(stored, 16)
            for dst, src in (
                (ident[:], c_ident), (dft[:], c_dft), (selh[:], c_selh), (selw[:], c_selw),
                (fhc[:], fh.rearrange("(a b) -> a b", b=1)), (fwc[:], fw.rearrange("(a b) -> a b", b=1)),
                (pw_a[:], proj_w[0:P, :]), (pw_b[:], proj_w[P:D, :]),
                (brow[:], proj_b.rearrange("(a b) -> a b", a=1)), (clsr[:], cls_token[0]),
                (pos0[:], pos[0, 0:1, :]),
                (posb[:], pos[0, 1:1 + NPATCH, :].rearrange("(t p) d -> p t d", p=PTOK)),
            ):
                sp.dma_start(dst, src).then_inc(consts_in, 16)
            with sp.Fori(0, B // 2) as i:
                for u in range(2):
                    sp.wait_ge(emb_mm, 2 * i + u + 1)
                    xb = x.rearrange("(i u) c (nh ph) w -> u i c ph nh w", u=2, ph=PATCH)[u, i]
                    for s in range(SHIFTS):
                        for c in range(C_IN):
                            r0 = (s * C_IN + c) * PATCH
                            w = IMG - PWS * s
                            sp.dma_start(img[u][r0:r0 + PATCH, :, 0:w], xb[c, :, :, PWS * s:IMG]
                                         ).then_inc(img_in[u], 16)

        @block.scalar
        def _(act):
            for u in range(2):
                act.sem_inc(emb_stored[u], 16)
            act.wait_ge(clsb_ready, 1)
            act.dma_start(h_d[:, 0, :], clsb[:]).then_inc(stored, 16)
            with act.Fori(0, B // 2) as i:
                for u in range(2):
                    act.wait_ge(emb_ready, PRIME + 2 * i + u + 1)
                    hb = h_d.rearrange("(i u) l d -> u i l d", u=2)[u, i]
                    act.dma_start(hb[1:1 + NPATCH, :].rearrange("(t p) d -> p t d", p=PTOK), emb[u][:]
                                  ).then_inc(emb_stored[u], 16)
            act.wait_ge(stored, 32)
            for u in range(2):
                act.wait_ge(emb_stored[u], 16 * (1 + B // 2))

        @block.tensor
        def _(pe):
            pe.sem_inc(emb_mm, PRIME)
            pe.wait_ge(consts_in, 16 * N_CONST)
            for t in range(FT):
                o = bank[t // 2][0:FR, (t % 2) * D:(t % 2) * D + D]
                pe.transpose(o[:, 0:P], pw_a[:, FR * t:FR * t + FR], ident[:])
                pe.transpose(o[:, P:D], pw_b[:, FR * t:FR * t + FR], ident[0:DB, 0:DB]).then_inc(projT_done, 1)
            for t in range(FT):
                pe.matmul(bank[2][0:FR, t:t + 1], selh[:, FR * t:FR * t + FR], fhc[:], start=True, stop=True)
                pe.matmul(bank[2][0:FR, FT + t:FT + t + 1], selw[:, FR * t:FR * t + FR], fwc[:],
                          start=True, stop=True).then_inc(fsel_done, 1)
            pe.wait_ge(ones_set, 1)
            pe.matmul(bank[3][0:PTOK, 0:D], ones[:, 0:PTOK], brow[:], start=True, stop=True).then_inc(bias_mm, 1)
            for p in range(PWS):
                if p == 0:
                    pe.wait_ge(pT_ready, FT)
                for t in range(FT):
                    mm = pe.matmul(bank[4 + p // 2][0:ROWS, (p % 2) * D:(p % 2) * D + D], dft[:, t, p, :], pT[:, t, :],
                                   start=(t == 0), stop=(t == FT - 1))
                mm.then_inc(weff_mm, 1)
            pe.wait_ge(cls0_ready, 1)
            pe.matmul(bank[2][0:B, 256:256 + D], ones[:, 0:B], cls0[:], start=True, stop=True).then_inc(cls_mm, 1)
            pe.wait_ge(weff_ready, PWS)
            pe.wait_ge(clsb_ready, 1)
            with pe.Fori(0, B // 2) as i:
                for u in range(2):
                    pe.wait_ge(img_in[u], 16 * SHIFTS * C_IN * (i + 1))
                    pe.wait_ge(emb_ready, 2 * i + u + 1)
                    for t in range(2):
                        for p in range(PWS):
                            px = img[u][:, t * NROW:(t + 1) * NROW, p:p + PATCH * (NH - 1) + 1:PATCH]
                            mm = pe.matmul(bank[u * 2 + t][0:PTOK, 0:D], px, weff[:, p, :],
                                           start=(p == 0), stop=(p == PWS - 1))
                    mm.then_inc(emb_mm, 1)

        @block.vector
        def _(dve):
            dve.sem_inc(emb_ready, PRIME)
            dve.memset(ones[:], 1.0).then_inc(ones_set, 1)
            dve.wait_ge(fsel_done, FT)
            dve.tensor_copy(fsel[:], bank[2][0:FR, 0:2 * FT]).then_inc(fsel_copied, 1)
            dve.wait_ge(fsel_copied, 1)
            dve.tensor_tensor(fcol[:], fsel[:, 0:FT], fsel[:, FT:2 * FT], ALU.mult).then_inc(fcol_done, 1)
            dve.wait_ge(fcol_done, 1)
            for t in range(FT):
                dve.wait_ge(projT_done, 2 * (t // 2) + 2)
                dve.tensor_scalar(pT[:, t, :], bank[t // 2][0:FR, (t % 2) * D:(t % 2) * D + D], fcol[:, t:t + 1],
                                  None, ALU.mult).then_inc(pT_ready, 1)
            dve.wait_ge(consts_in, 16 * N_CONST)
            dve.wait_ge(bias_mm, 1)
            for t in range(2):
                dve.tensor_tensor(posb[:, t, :], posb[:, t, :], bank[3][0:PTOK, 0:D], ALU.add).then_inc(posb_ready, 1)
            dve.tensor_tensor(cls0[:], clsr[:], pos0[:], ALU.add).then_inc(cls0_ready, 1)
            for p in range(PWS):
                dve.wait_ge(weff_mm, 2 * (p // 2) + 2)
                dve.tensor_copy(weff[:, p, :], bank[4 + p // 2][0:ROWS, (p % 2) * D:(p % 2) * D + D]
                                ).then_inc(weff_ready, 1)
            dve.wait_ge(cls_mm, 1)
            dve.tensor_copy(clsb[:], bank[2][0:B, 256:256 + D]).then_inc(clsb_ready, 1)
            dve.wait_ge(posb_ready, 2)
            with dve.Fori(0, B // 2) as i:
                for u in range(2):
                    dve.wait_ge(emb_mm, PRIME + 2 * i + u + 1)
                    dve.wait_ge(emb_stored[u], 16 * (i + 1))
                    for t in range(2):
                        add = dve.tensor_tensor(emb[u][:, t, :], bank[u * 2 + t][0:PTOK, 0:D], posb[:, t, :], ALU.add)
                    add.then_inc(emb_ready, 1)


class Uses:

    def __init__(self, banks, per_body):
        self.banks, self.per_body, self.n = banks, per_body, -1
        assert per_body % len(banks) == 0

    def take(self):
        self.n += 1
        return self.banks[self.n % len(self.banks)]

    def free(self, i):
        return i * self.per_body + self.n + 1

    def filled(self, i):
        return i * self.per_body + self.n + 1

    def read(self, i, n=None):
        return i * self.per_body + (self.n if n is None else n) + 1 + len(self.banks)

    def end(self):
        assert self.n + 1 == self.per_body, (self.n + 1, self.per_body)


GROUP = 4
NG = HEADS // GROUP
PAIRS = HEADS // 2
STK = 64
MROW = 3 * HD
PTC = LE + (LE - P) + LASTE
AC = LE + LASTE
BC = LE - P


def attention_phase(nc, h_d, wq, bq, wk, bk, wv, bv, wo, bo, c_rope, c_ident, c_mask, c_maskT, h2_d):
    with ExitStack() as ctx:
        a = Pool_(nc, ctx, "at")
        ident = a.sb("ident", [P, P])
        identb = a.sb("identb", [P, P], BF16)
        maskf = a.sb("maskf", [P, 2, P])
        mask = a.sb("mask", [P, 2, P], BF16)
        rope = a.sb("rope", [P, QT, 2 * HD])
        w_in = a.sb("w_in", [P, 4, 2, D])
        wa = a.sb("wa", [P, 4, D])
        wb = a.sb("wb", [DB + 1, 4, D])
        half = a.sb("half", [P, QT])
        hb = [a.sb(f"hb{u}", [P, QT, D]) for u in range(2)]
        stats = [a.sb(f"stats{u}", [P, QT, 6]) for u in range(2)]
        mv = [a.sb(f"mv{u}", [P, QT, 2]) for u in range(2)]
        var = [a.sb(f"var{u}", [P, QT]) for u in range(2)]
        rstd = [a.sb(f"rstd{u}", [P, QT]) for u in range(2)]
        xn = [a.sb(f"xn{u}", [P, QT, D]) for u in range(2)]
        xTa = [a.sb(f"xTa{u}", [P, LP]) for u in range(2)]
        xTb = [a.sb(f"xTb{u}", [DB + 1, LP]) for u in range(2)]
        rots = [a.sb(f"rot{u}", [P, 2, 2 * HEADS, HD]) for u in range(2)]
        stk = [a.sb(f"stk{u}", [P, QT, 2 * HEADS, STK]) for u in range(2)]
        vaug = [a.sb(f"vaug{u}", [P, QT, HEADS, 32]) for u in range(2)]
        qT = [a.sb(f"qT{u}", [P, PAIRS, LP]) for u in range(2)]
        kT = [a.sb(f"kT{u}", [P, PAIRS, LP]) for u in range(2)]
        mx = [a.sb(f"mx{u}", [P, QT, HEADS]) for u in range(2)]
        probs = [a.sb(f"probs{u}", [P, GROUP, PTC]) for u in range(2)]
        oT = [a.sb(f"oT{u}", [P, NG, LP]) for u in range(2)]
        rden = [a.sb(f"rden{u}", [P, QT, HEADS]) for u in range(2)]
        on = [a.sb(f"on{u}", [P, QT, D]) for u in range(2)]
        onTa = [a.sb(f"onTa{u}", [P, LP]) for u in range(2)]
        onTb = [a.sb(f"onTb{u}", [DB + 1, LP]) for u in range(2)]
        h2 = [a.sb(f"h2{u}", [P, QT, D]) for u in range(2)]
        vbank = [a.bank(f"vbank{i}") for i in range(RING)]
        sbank = [a.bank(f"sbank{i}") for i in range(RING)]

        consts_in = a.sem("consts_in")
        init_done = a.sem("init_done")
        wT_mm = a.sem("wT_mm")
        wT_ready = a.sem("wT_ready")
        v_filled, v_freed = a.sem("v_filled"), a.sem("v_freed")
        s_filled, s_freed = a.sem("s_filled"), a.sem("s_freed")
        vec_step = a.sem("vec_step")
        carried = a.sem("carried")
        h_in = [a.sem(f"h_in{u}") for u in range(2)]
        var_ready = a.sem("var_ready")
        rstd_ready = a.sem("rstd_ready")
        xn_ready = a.sem("xn_ready")
        rope_ready = a.sem("rope_ready")
        dup_ready = a.sem("dup_ready")
        max_ready = a.sem("max_ready")
        h2_stored = [a.sem(f"h2_stored{u}") for u in range(2)]
        block = ctx.enter_context(nc.Block())

        N_CONST = 16
        N_INIT = 17
        VN, SN = 80, 72
        VSTEPS = 24
        PROJECTED = (73, 80)
        MAXES = [(0, g + j, 3, P) for g in (0, 6) for j in range(2)] \
            + [(1, g + j, 2, 2 * P) for g in range(0, HEADS, 4) for j in range(2)] \
            + [(2, g, 1, LE) for g in range(HEADS)]
        PART = (0, 8, 15, len(MAXES))

        @block.sync
        def _(sp):
            for dst, src in ((ident[:], c_ident), (maskf[:, 0, :], c_mask), (maskf[:, 1, :], c_maskT), (rope[:], c_rope)):
                sp.dma_start(dst, src).then_inc(consts_in, 16)
            for j, w in enumerate((wq, wk, wv, wo)):
                sp.dma_start(w_in[:, j, 0, :], w[0:P, :]).then_inc(consts_in, 16)
                sp.dma_start(w_in[0:DB, j, 1, :], w[P:D, :]).then_inc(consts_in, 16)
            for j, w in enumerate((bq, bk, bv, bo)):
                sp.dma_start(wb[DB:DB + 1, j, :], w.rearrange("(a b) -> a b", a=1)).then_inc(consts_in, 16)
            sp.wait_ge(init_done, N_INIT)
            hd = h_d.rearrange("(i u) l d -> u i l d", u=2)
            h2d = h2_d.rearrange("(i u) l d -> u i l d", u=2)
            for u in range(2):
                sp.dma_start(hb[u][:, 0:2, :], hd[u, 0, 0:2 * P].rearrange("(t p) d -> p t d", p=P)).then_inc(h_in[u], 16)
                sp.dma_start(hb[u][0:LAST, 2, :], hd[u, 0, 2 * P:L]).then_inc(h_in[u], 16)
            with sp.Fori(0, B // 2) as i:
                for u in range(2):
                    sp.wait_ge(v_freed, RING + i * VN + PROJECTED[u])
                    sp.dma_start(h2d[u, i, 0:2 * P].rearrange("(t p) d -> p t d", p=P), h2[u][:, 0:2, :]
                                 ).then_inc(h2_stored[u], 16)
                    sp.dma_start(h2d[u, i, 2 * P:L], h2[u][0:LAST, 2, :]).then_inc(h2_stored[u], 16)
                    nxt = hd[u, (i + 1) % (B // 2)]
                    sp.dma_start(hb[u][:, 0:2, :], nxt[0:2 * P].rearrange("(t p) d -> p t d", p=P)).then_inc(h_in[u], 16)
                    sp.dma_start(hb[u][0:LAST, 2, :], nxt[2 * P:L]).then_inc(h_in[u], 16)
            for u in range(2):
                sp.wait_ge(h2_stored[u], 32 * (1 + B // 2))
                sp.wait_ge(h_in[u], 32 * (1 + B // 2))

        @block.gpsimd
        def _(pool):
            pool.memset(half[:], -0.5).then_inc(init_done, 1)
            pool.wait_ge(init_done, N_INIT)
            with pool.Fori(0, B // 2) as i:
                for u in range(2):
                    pool.wait_ge(var_ready, 2 * i + u + 1)
                    pool.tensor_tensor(rstd[u][:], var[u][:], half[:], ALU.pow).then_inc(rstd_ready, 1)
                for u in range(2):
                    for t in range(QT):
                        pool.wait_ge(rope_ready, QT * (2 * i + u) + t + 1)
                        pool.sem_inc(carried, 1)
                        pool.tensor_copy(stk[u][:, t, 0:HEADS, 2 * HD:3 * HD], stk[u][:, t, 0:HEADS, 0:HD])
                        pool.tensor_copy(stk[u][:, t, HEADS:, HD:2 * HD], stk[u][:, t, HEADS:, 0:HD]
                                         ).then_inc(dup_ready, 1)

        @block.tensor
        def _(pe):
            pe.wait_ge(consts_in, 16 * N_CONST)
            for j in range(4):
                pe.transpose(vbank[j][:, 0:P], w_in[:, j, 0, 0:P], ident[:])
                pe.transpose(vbank[j][:, P:D], w_in[0:DB, j, 1, 0:P], ident[0:DB, 0:DB])
                pe.transpose(vbank[j][0:DB, D:D + P], w_in[:, j, 0, P:D], ident[:])
                pe.transpose(vbank[j][0:DB, D + P:2 * D], w_in[0:DB, j, 1, P:D], ident[0:DB, 0:DB]).then_inc(wT_mm, 1)
            pe.wait_ge(wT_ready, 11)
            pe.wait_ge(init_done, N_INIT)
            with pe.Fori(0, B // 2) as i:
                v = Uses(vbank, VN)
                s = Uses(sbank, SN)
                at = {}

                def layer_in(u):
                    bt = 2 * i + u
                    pe.wait_ge(xn_ready, bt + 1)
                    ta = s.take()
                    pe.wait_ge(s_freed, s.free(i))
                    for t in range(QT):
                        mm = pe.transpose(ta[:, t * P:t * P + P], xn[u][:, t, 0:P], ident[:])
                    mm.then_inc(s_filled, 1)
                    tb = s.take()
                    pe.wait_ge(s_freed, s.free(i))
                    pe.sem_inc(carried, 1)
                    for t in range(QT):
                        mm = pe.transpose(tb[0:DB, t * P:t * P + P], xn[u][:, t, P:D], ident[:])
                    mm.then_inc(s_filled, 1)
                    at["xT", u] = s.n

                def qkv(u):
                    pe.wait_ge(s_freed, s.read(i, at["xT", u]))
                    for t in range(QT):
                        o = v.take()
                        pe.wait_ge(v_freed, v.free(i))
                        pe.matmul(o[:, 0:2 * D], xTa[u][:, t * P:t * P + P], wa[:, 0:2, :], start=True, stop=False)
                        pe.matmul(o[:, 0:2 * D], xTb[u][:, t * P:t * P + P], wb[:, 0:2, :], start=False, stop=True
                                  ).then_inc(v_filled, 1)
                    for ts in ((0, 1), (2,)):
                        o = s.take()
                        pe.wait_ge(s_freed, s.free(i))
                        for t in ts:
                            c = (t % 2) * D
                            pe.matmul(o[:, c:c + D], xTa[u][:, t * P:t * P + P], wa[:, 2, :], start=True, stop=False)
                            mm = pe.matmul(o[:, c:c + D], xTb[u][:, t * P:t * P + P], wb[:, 2, :], start=False, stop=True)
                        mm.then_inc(s_filled, 1)
                    at["v", u] = s.n

                def stack_T(u, first, ring, freed, filled, p):
                    o = ring.take()
                    pe.wait_ge(freed, ring.free(i))
                    for t in range(QT):
                        mm = pe.transpose(o[:, t * P:t * P + P], stk[u][:, t, first + 2 * p:first + 2 * p + 2, :], ident[:])
                    mm.then_inc(filled, 1)

                def qk_T(u):
                    pe.wait_ge(dup_ready, QT * (2 * i + u + 1))
                    for p in range(PAIRS):
                        stack_T(u, 0, v, v_freed, v_filled, p)
                        stack_T(u, HEADS, s, s_freed, s_filled, p)
                    at["q", u], at["k", u] = v.n, s.n

                def maxima(u, part):
                    if part == 0:
                        pe.wait_ge(v_freed, v.read(i, at["q", u]))
                        pe.wait_ge(s_freed, s.read(i, at["k", u]))
                    for t, h0, n, keys in MAXES[PART[part]:PART[part + 1]]:
                        o = v.take()
                        pe.wait_ge(v_freed, v.free(i))
                        ov = o[:, 0:n * keys].rearrange("p (n k) -> p n k", n=n)
                        diag = min(P, keys - t * P)
                        pe.matmul(ov[:, :, t * P:t * P + diag], identb[:],
                                  mask[:, 0:1, 0:diag].to_broadcast([P, n, diag]), start=True, stop=True)
                        for j in range(n):
                            h = h0 + 2 * j
                            r = STK * (h % 2)
                            mm = pe.matmul(ov[:, j, :], qT[u][r:r + MROW, h // 2, t * P:t * P + P].bitcast(F32R),
                                           kT[u][r:r + MROW, h // 2, 0:keys].bitcast(F32R), start=False, stop=True,
                                           skip_group_check=True)
                        mm.then_inc(v_filled, 1)

                def q_T_again(u):
                    pe.wait_ge(max_ready, 2 * i + u + 1)
                    for p in range(PAIRS):
                        stack_T(u, 0, s, s_freed, s_filled, p)
                    at["q2", u] = s.n

                def scores(u, g):
                    if g == 0:
                        pe.wait_ge(s_freed, s.read(i, at["q2", u]))
                    for j in range(2):
                        r = STK * j
                        pairs = (g * GROUP // 2, g * GROUP // 2 + 1)
                        for pr in pairs:
                            kh = kT[u][r:r + STK, pr, :].bitcast(F32R)
                            qh = qT[u][r:r + STK, pr, :].bitcast(F32R)
                            o = s.take()
                            pe.wait_ge(s_freed, s.free(i))
                            pe.matmul(o[:, 0:P], identb[:], mask[:, 1, :], start=True, stop=True, skip_group_check=True)
                            pe.matmul(o[:, LE:AC], identb[:], mask[:, 1, 0:LASTE], start=False, stop=True,
                                      skip_group_check=True)
                            pe.matmul(o[:, 0:LE], kh[:, 0:P], qh[:, 0:LE], start=False, stop=True, skip_group_check=True)
                            pe.matmul(o[:, LE:AC], kh[:, 2 * P:LP], qh[:, 2 * P:LE], start=False, stop=True,
                                      skip_group_check=True).then_inc(s_filled, 1)
                        o = s.take()
                        pe.wait_ge(s_freed, s.free(i))
                        ov = o[:, 0:2 * BC].rearrange("p (n k) -> p n k", n=2)
                        pe.matmul(ov[:, :, 0:P], identb[:], mask[:, 1:2, :].to_broadcast([P, 2, P]), start=True, stop=True,
                                  skip_group_check=True)
                        for n, pr in enumerate(pairs):
                            mm = pe.matmul(ov[:, n, :], kT[u][r:r + STK, pr, P:2 * P].bitcast(F32R),
                                           qT[u][r:r + STK, pr, P:LE].bitcast(F32R), start=False, stop=True,
                                           skip_group_check=True)
                        mm.then_inc(s_filled, 1)
                    at["probs", u, g] = s.n

                def attend(u, g):
                    pe.wait_ge(s_freed, s.read(i, at["probs", u, g]))
                    pb = probs[(NG * u + g) % 2]
                    o = v.take()
                    pe.wait_ge(v_freed, v.free(i))
                    for kt, c0, src in ((0, 0, pb[:, :, 0:LE]), (1, P, pb[:, :, AC:PTC]), (2, 2 * P, pb[:, :, LE:AC])):
                        for j in range(GROUP):
                            mm = pe.matmul(o[32 * j:32 * j + 32, c0:LE], vaug[u][:, kt, g * GROUP + j, :], src[:, j, :],
                                           start=(kt == 0), stop=(kt == 2))
                    mm.then_inc(v_filled, 1)
                    at["oT", u] = v.n

                def out_T(u):
                    pe.wait_ge(v_freed, v.read(i, at["oT", u]))
                    for t in range(QT):
                        o = v.take()
                        pe.wait_ge(v_freed, v.free(i))
                        for g in range(NG):
                            mm = pe.transpose(o[:, g * P:g * P + P], oT[u][:, g, t * P:t * P + P], ident[:])
                        mm.then_inc(v_filled, 1)
                    at["on", u] = v.n

                def norm_T(u):
                    pe.wait_ge(v_freed, v.read(i, at["on", u]))
                    ta = s.take()
                    pe.wait_ge(s_freed, s.free(i))
                    for t in range(QT):
                        mm = pe.transpose(ta[:, t * P:t * P + P], on[u][:, t, 0:P], ident[:])
                    mm.then_inc(s_filled, 1)
                    tb = s.take()
                    pe.wait_ge(s_freed, s.free(i))
                    pe.sem_inc(carried, 1)
                    for t in range(QT):
                        mm = pe.transpose(tb[0:DB, t * P:t * P + P], on[u][:, t, P:D], ident[:])
                    mm.then_inc(s_filled, 1)
                    at["onT", u] = s.n

                def project(u):
                    pe.wait_ge(s_freed, s.read(i, at["onT", u]))
                    for t in range(QT):
                        o = v.take()
                        pe.wait_ge(v_freed, v.free(i))
                        pe.matmul(o[:, 0:D], onTa[u][:, t * P:t * P + P], wa[:, 3, :], start=True, stop=False)
                        pe.matmul(o[:, 0:D], onTb[u][:, t * P:t * P + P], wb[:, 3, :], start=False, stop=True
                                  ).then_inc(v_filled, 1)

                layer_in(0)
                layer_in(1)
                qkv(0)
                qkv(1)
                qk_T(0)
                for g in range(NG):
                    maxima(0, g)
                qk_T(1)
                q_T_again(0)
                scores(0, 0)
                maxima(1, 0)
                scores(0, 1)
                attend(0, 0)
                maxima(1, 1)
                scores(0, 2)
                attend(0, 1)
                maxima(1, 2)
                attend(0, 2)
                q_T_again(1)
                scores(1, 0)
                out_T(0)
                scores(1, 1)
                attend(1, 0)
                norm_T(0)
                scores(1, 2)
                attend(1, 1)
                project(0)
                attend(1, 2)
                out_T(1)
                norm_T(1)
                project(1)
                v.end()
                s.end()

        @block.scalar
        def _(act):
            act.sem_inc(s_freed, RING)
            act.wait_ge(consts_in, 16 * N_CONST)
            act.copy(identb[:], ident[:]).then_inc(wT_ready, 1)
            act.copy(mask[:], maskf[:]).then_inc(wT_ready, 1)
            with act.Fori(0, B // 2) as i:
                s = Uses(sbank, SN)

                def two_parts(ta, tb):
                    for dst, rows in ((ta, P), (tb, DB)):
                        o = s.take()
                        act.wait_ge(s_filled, s.filled(i))
                        act.copy(dst[0:rows, :], o[0:rows, 0:LP]).then_inc(s_freed, 1)

                def values(u):
                    for t0, n in ((0, 2), (2, 1)):
                        o = s.take()
                        act.wait_ge(s_filled, s.filled(i))
                        act.copy(vaug[u][:, t0:t0 + n, :, 0:HD],
                                 o[:, 0:n * D].rearrange("p (t h d) -> p t h d", t=n, h=HEADS)).then_inc(s_freed, 1)

                def stacks(dst):
                    for p in range(PAIRS):
                        o = s.take()
                        act.wait_ge(s_filled, s.filled(i))
                        act.copy(dst[:, p, :].bitcast(F32R), o[:, 0:LP]).then_inc(s_freed, 1)

                def exps(u, g):
                    pb = probs[(NG * u + g) % 2]
                    for j in range(2):
                        for n in range(2):
                            o = s.take()
                            act.wait_ge(s_filled, s.filled(i))
                            act.activation(pb[:, 2 * n + j, 0:AC], o[:, 0:AC], ACT.Exp).then_inc(s_freed, 1)
                        o = s.take()
                        act.wait_ge(s_filled, s.filled(i))
                        act.activation(pb[:, j:j + 3:2, AC:PTC],
                                       o[:, 0:2 * BC].rearrange("p (n k) -> p n k", n=2), ACT.Exp).then_inc(s_freed, 1)

                two_parts(xTa[0], xTb[0])
                two_parts(xTa[1], xTb[1])
                values(0)
                values(1)
                stacks(kT[0])
                stacks(kT[1])
                stacks(qT[0])
                exps(0, 0)
                exps(0, 1)
                exps(0, 2)
                stacks(qT[1])
                exps(1, 0)
                exps(1, 1)
                two_parts(onTa[0], onTb[0])
                exps(1, 2)
                two_parts(onTa[1], onTb[1])
                s.end()

        @block.vector
        def _(dve):
            dve.sem_inc(v_freed, RING)
            for u in range(2):
                dve.sem_inc(h2_stored[u], 32)
            for u in range(2):
                dve.memset(hb[u][:, 2, :], 0.0).then_inc(init_done, 1)
                dve.memset(xTb[u][DB:DB + 1, :], 1.0).then_inc(init_done, 1)
                dve.memset(onTb[u][DB:DB + 1, :], 1.0).then_inc(init_done, 1)
                dve.memset(stk[u][:, :, :, MROW:STK], 0.0).then_inc(init_done, 1)
                dve.memset(vaug[u][:, :, :, HD:32], 0.0).then_inc(init_done, 1)
                dve.memset(oT[u][:, :, LE:LP], 1.0).then_inc(init_done, 1)
            dve.wait_ge(init_done, 13)
            for u in range(2):
                dve.memset(stk[u][:, :, HEADS:, MROW:MROW + 2], 1.0).then_inc(init_done, 1)
                dve.memset(vaug[u][:, :, :, HD:HD + 1], 1.0).then_inc(init_done, 1)
            dve.wait_ge(consts_in, 16 * N_CONST)
            scale = float(HD) ** -0.5
            dve.tensor_scalar(wb[DB:DB + 1, 0, :], wb[DB:DB + 1, 0, :], scale, None, ALU.mult).then_inc(wT_ready, 1)
            for j in range(4):
                dve.wait_ge(wT_mm, j + 1)
                by = scale if j == 0 else 1.0
                dve.tensor_scalar(wa[:, j, :], vbank[j][:, 0:D], by, None, ALU.mult).then_inc(wT_ready, 1)
                dve.tensor_scalar(wb[0:DB, j, :], vbank[j][0:DB, D:2 * D], by, None, ALU.mult).then_inc(wT_ready, 1)
            dve.wait_ge(init_done, N_INIT)
            with dve.Fori(0, B // 2) as i:
                v = Uses(vbank, VN)
                steps = [0]

                def link(ins):
                    steps[0] += 1
                    ins.then_inc(vec_step, 1)
                    dve.wait_ge(vec_step, i * VSTEPS + steps[0])

                def layernorm(u):
                    dve.wait_ge(h_in[u], 32 * (i + 1))
                    for t in range(QT):
                        ins = dve.bn_stats(stats[u][:, t, :], hb[u][:, t, :])
                    link(ins)
                    dve.sem_inc(carried, 1)
                    for t in range(QT):
                        ins = dve.bn_aggr(mv[u][:, t, :], stats[u][:, t, :])
                    link(ins)
                    dve.tensor_scalar(var[u][:], mv[u][:, :, 1], LN_EPS, None, ALU.add).then_inc(var_ready, 1)

                def normalize(u):
                    dve.wait_ge(rstd_ready, 2 * i + u + 1)
                    for t in range(QT):
                        ins = dve.tensor_scalar(xn[u][:, t, :], hb[u][:, t, :], mv[u][:, t, 0:1], rstd[u][:, t:t + 1],
                                                ALU.subtract, ALU.mult)
                    ins.then_inc(xn_ready, 1)

                def rotate(u):
                    for t in range(QT):
                        rot = rots[(u * QT + t) % 2]
                        o = v.take()
                        dve.wait_ge(v_filled, v.filled(i))
                        qk = o[:, 0:2 * D].rearrange("p (h d) -> p h d", d=HD)

                        def table(c0, n):
                            return rope[:, t:t + 1, c0:c0 + n].to_broadcast([P, 2 * HEADS, n])

                        dve.tensor_tensor(rot[:, 0], qk, table(0, HD), ALU.mult)
                        dve.tensor_tensor(rot[:, 1, :, 0:HD // 2], qk[:, :, HD // 2:HD], table(HD, HD // 2), ALU.mult)
                        dve.tensor_tensor(rot[:, 1, :, HD // 2:HD], qk[:, :, 0:HD // 2], table(HD + HD // 2, HD // 2),
                                          ALU.mult).then_inc(v_freed, 1)
                        dve.wait_ge(v_freed, v.read(i))
                        link(dve.tensor_tensor(rot[:, 0], rot[:, 0], rot[:, 1], ALU.add))
                        link(dve.tensor_copy(stk[u][:, t, :, 0:HD].bitcast(F32R), rot[:, 0]))
                        dve.tensor_tensor(stk[u][:, t, 0:HEADS, HD:2 * HD].bitcast(F32R), rot[:, 0, 0:HEADS],
                                          stk[u][:, t, 0:HEADS, 0:HD], ALU.subtract)
                        dve.tensor_tensor(stk[u][:, t, HEADS:, 2 * HD:3 * HD].bitcast(F32R), rot[:, 0, HEADS:],
                                          stk[u][:, t, HEADS:, 0:HD], ALU.subtract).then_inc(rope_ready, 1)

                def queries(u):
                    for p in range(PAIRS):
                        o = v.take()
                        dve.wait_ge(v_filled, v.filled(i))
                        dve.tensor_copy(qT[u][:, p, :].bitcast(F32R), o[:, 0:LP]).then_inc(v_freed, 1)

                def maxima(u, part):
                    for t, h0, n, keys in MAXES[PART[part]:PART[part + 1]]:
                        o = v.take()
                        dve.wait_ge(v_filled, v.filled(i))
                        dve.tensor_reduce(mx[u][:, t, h0:h0 + 2 * n - 1:2], o[:, 0:n * keys].rearrange("p (n k) -> p n k", n=n),
                                          AX.X, ALU.max).then_inc(v_freed, 1)

                def put_maxima(u):
                    dve.wait_ge(v_freed, v.read(i))
                    hi, lo = stk[u][:, :, 0:HEADS, MROW], stk[u][:, :, 0:HEADS, MROW + 1]
                    link(dve.tensor_scalar(hi.bitcast(F32R), mx[u][:], -1.0, None, ALU.mult))
                    dve.scalar_tensor_tensor(lo.bitcast(F32R), mx[u][:], -1.0, hi, ALU.mult, ALU.subtract
                                             ).then_inc(max_ready, 1)

                def attended(u, g):
                    o = v.take()
                    dve.wait_ge(v_filled, v.filled(i))
                    dve.tensor_copy(oT[u][:, g, 0:LE], o[:, 0:LE]).then_inc(v_freed, 1)

                def divide(u):
                    for t in range(QT):
                        o = v.take()
                        dve.wait_ge(v_filled, v.filled(i))
                        ov = o[:, 0:NG * P].rearrange("p (h d) -> p h d", d=32)
                        link(dve.reciprocal(rden[u][:, t, :], ov[:, :, HD]))
                        dve.tensor_tensor(on[u][:, t, :].rearrange("p (h d) -> p h d", d=HD), ov[:, :, 0:HD],
                                          rden[u][:, t, :].unsqueeze(2).to_broadcast([P, HEADS, HD]), ALU.mult
                                          ).then_inc(v_freed, 1)

                def residual(u):
                    dve.wait_ge(h2_stored[u], 32 * (i + 1))
                    for t in range(QT):
                        o = v.take()
                        dve.wait_ge(v_filled, v.filled(i))
                        dve.tensor_tensor(h2[u][:, t, :], o[:, 0:D], hb[u][:, t, :], ALU.add).then_inc(v_freed, 1)
                    assert v.n + 1 == PROJECTED[u], v.n + 1

                layernorm(0)
                layernorm(1)
                normalize(0)
                normalize(1)
                rotate(0)
                rotate(1)
                queries(0)
                for g in range(NG):
                    maxima(0, g)
                put_maxima(0)
                queries(1)
                maxima(1, 0)
                attended(0, 0)
                maxima(1, 1)
                attended(0, 1)
                maxima(1, 2)
                put_maxima(1)
                attended(0, 2)
                divide(0)
                attended(1, 0)
                attended(1, 1)
                residual(0)
                attended(1, 2)
                divide(1)
                residual(1)
                v.end()
                assert steps[0] == VSTEPS, steps[0]


HALF = N_EXP // 2
EC = B * SLOTS_PER
EC1 = EC + 1


def dispatch_phase(nc, xsTa, xsTb, h2_d, phi, ln_g, ln_b, c_ident, e2_d):
    with ExitStack() as ctx:
        a = Pool_(nc, ctx, "di")
        ident = a.sb("ident", [P, P])
        phiTa = a.sb("phiTa", [P, S])
        phiTb = a.sb("phiTb", [DB, S])
        gTa = a.sb("gTa", [P, N_EXP])
        gTb = a.sb("gTb", [P, HALF])
        gb_in = a.sb("gb_in", [N_EXP, 2, 2, D])
        half = a.sb("half", [P, SLOTS_PER])
        pn = a.sb("pn", [P, 2, SLOTS_PER])
        hb = [a.sb(f"hb{u}", [P, QT, D]) for u in range(2)]
        stats = a.sb("stats", [P, ST, 6])
        mv = [a.sb(f"mv{u}", [P, QT, 2]) for u in range(2)]
        var = [a.sb(f"var{u}", [P, QT]) for u in range(2)]
        rstd = [a.sb(f"rstd{u}", [P, QT]) for u in range(2)]
        xn = [a.sb(f"xn{u}", [P, QT, D + 1]) for u in range(2)]
        xTa = a.sb("xTa", [P, LP])
        xTb = a.sb("xTb", [DB, LP])
        lg = [a.sb(f"lg{u}", [P, QT, S]) for u in range(2)]
        nmt = [a.sb(f"nmt{u}", [P, QT]) for u in range(2)]
        nms = [a.sb(f"nms{u}", [P, ST]) for u in range(2)]
        e2 = a.sb("e2", [P, QT, S])
        e2T = a.sb("e2T", [P, ST, L])
        e1T = a.sb("e1T", [P, ST, L])
        e1 = a.sb("e1", [P, QT, S])
        xs = a.sb("xs", [P, ST, D + 1])
        smv = a.sb("smv", [P, ST, 2])
        ssq = a.sb("ssq", [P, ST])
        svar = a.sb("svar", [P, ST])
        srstd = a.sb("srstd", [P, ST])
        xsn = a.sb("xsn", [P, ST, D])
        phi_in = e1[:, 0:2, 0:ST * D // 2]
        sq = e2[:, 0:2, :]
        vbank = [a.bank(f"vbank{i}") for i in range(RING)]
        sbank = [a.bank(f"sbank{i}") for i in range(RING)]

        consts_in = a.sem("consts_in")
        init_done = a.sem("init_done")
        setup_mm = a.sem("setup_mm")
        setup_step = a.sem("setup_step")
        pn_ready = a.sem("pn_ready")
        v_filled, v_freed = a.sem("v_filled"), a.sem("v_freed")
        s_filled, s_freed = a.sem("s_filled"), a.sem("s_freed")
        vec_step = a.sem("vec_step")
        carried = a.sem("carried")
        h_in = [a.sem(f"h_in{u}") for u in range(2)]
        var_ready = a.sem("var_ready")
        rstd_ready = a.sem("rstd_ready")
        xn_ready = a.sem("xn_ready")
        token_max = a.sem("token_max")
        slot_max = a.sem("slot_max")
        e2_ready = a.sem("e2_ready")
        e2_stored = a.sem("e2_stored")
        svar_ready = a.sem("svar_ready")
        srstd_ready = a.sem("srstd_ready")
        xsn_ready = a.sem("xsn_ready")
        block = ctx.enter_context(nc.Block())

        N_CONST = 7
        N_INIT = 5
        VN, SN = 28, 48
        L_END = (6, 20)
        TL_AT = (6, 30)
        XS_END = (30, 48)
        TE2_END = (12, 20)
        VSTEPS = 10

        phs = [phi_in[:, t // 4, (t % 4) * D:(t % 4) * D + D] for t in range(ST)]

        @block.sync
        def _(sp):
            sp.dma_start(ident[:], c_ident).then_inc(consts_in, 16)
            phv = phi.rearrange("n p d -> (n p) d").rearrange("(h t p) d -> h p t d", p=P, h=2)
            for k in range(2):
                sp.dma_start(phi_in[:, k, :].rearrange("p (t d) -> p t d", d=D), phv[k]).then_inc(consts_in, 16)
            sp.dma_start(gb_in[:, 0, 0, :], ln_g).then_inc(consts_in, 16)
            sp.dma_start(gb_in[:, 1, 0, :], ln_b).then_inc(consts_in, 16)
            for k, w in enumerate((ln_g, ln_b)):
                sp.dma_start(gb_in[0:HALF, k, 1, :], w[HALF:, :]).then_inc(consts_in, 16)
            sp.wait_ge(init_done, N_INIT)
            h2d = h2_d.rearrange("(i u) l d -> u i l d", u=2)
            e2d = e2_d.rearrange("(i u) p c -> u i p c", u=2)
            for u in range(2):
                sp.dma_start(hb[u][:, 0:2, :], h2d[u, 0, 0:2 * P].rearrange("(t p) d -> p t d", p=P)).then_inc(h_in[u], 16)
                sp.dma_start(hb[u][0:LAST, 2, :], h2d[u, 0, 2 * P:L]).then_inc(h_in[u], 16)
            with sp.Fori(0, B // 2) as i:
                for u in range(2):
                    sp.wait_ge(xn_ready, 2 * i + u + 1)
                    nxt = h2d[u, (i + 1) % (B // 2)]
                    sp.dma_start(hb[u][:, 0:2, :], nxt[0:2 * P].rearrange("(t p) d -> p t d", p=P)).then_inc(h_in[u], 16)
                    sp.dma_start(hb[u][0:LAST, 2, :], nxt[2 * P:L]).then_inc(h_in[u], 16)
                for u in range(2):
                    sp.wait_ge(v_freed, RING + i * VN + TE2_END[u])
                    sp.dma_start(e2d[u, i], e2T[:].rearrange("p t c -> p (t c)")).then_inc(e2_stored, 16)
            sp.wait_ge(e2_stored, 16 * (1 + B))
            for u in range(2):
                sp.wait_ge(h_in[u], 32 * (1 + B // 2))

        @block.gpsimd
        def _(pool):
            pool.memset(half[:], -0.5).then_inc(init_done, 1)
            pool.wait_ge(init_done, N_INIT)
            pool.wait_ge(pn_ready, 1)
            for k, rows in enumerate((P, DB)):
                pool.tensor_tensor(pn[0:rows, k, :], pn[0:rows, k, :], half[0:rows, :], ALU.pow).then_inc(pn_ready, 1)
            with pool.Fori(0, B // 2) as i:
                for u in range(2):
                    pool.wait_ge(var_ready, 2 * i + u + 1)
                    pool.tensor_tensor(rstd[u][:], var[u][:], half[:, 0:QT], ALU.pow).then_inc(rstd_ready, 1)
                for u in range(2):
                    pool.wait_ge(svar_ready, 2 * i + u + 1)
                    pool.tensor_tensor(srstd[:], svar[:], half[:, 0:ST], ALU.pow).then_inc(srstd_ready, 1)

        @block.tensor
        def _(pe):
            pe.wait_ge(consts_in, 16 * N_CONST)
            for t in range(ST):
                pe.transpose(vbank[t // 4][:, (t % 4) * P:(t % 4) * P + P], phs[t][:, 0:P], ident[:])
                pe.transpose(vbank[2 + t // 4][0:DB, (t % 4) * P:(t % 4) * P + P], phs[t][:, P:D], ident[:]
                             ).then_inc(setup_mm, 1)
            for k in range(2):
                pe.transpose(sbank[k][:, 0:N_EXP], gb_in[:, k, 0, 0:P], ident[0:N_EXP, 0:N_EXP])
                pe.transpose(sbank[k][0:DB, P:P + HALF], gb_in[0:HALF, k, 0, P:D], ident[0:HALF, 0:HALF])
                pe.transpose(sbank[k][:, 2 * P:2 * P + HALF], gb_in[0:HALF, k, 1, D - P:D], ident[0:HALF, 0:HALF]
                             ).then_inc(setup_mm, 1)
            pe.wait_ge(setup_step, 18)
            pe.wait_ge(init_done, N_INIT)
            with pe.Fori(0, B // 2) as i:
                v = Uses(vbank, VN)
                s = Uses(sbank, SN)
                at = {}

                def tokens_T(u):
                    pe.wait_ge(xn_ready, 2 * i + u + 1)
                    oa = v.take()
                    ob = v.take()
                    pe.wait_ge(v_freed, v.free(i))
                    for t in range(QT):
                        mm = pe.transpose(oa[:, t * P:t * P + P], xn[u][:, t, 0:P], ident[:])
                    mm.then_inc(v_filled, 1)
                    for t in range(QT):
                        mm = pe.transpose(ob[0:DB, t * P:t * P + P], xn[u][:, t, P:D], ident[:])
                    mm.then_inc(v_filled, 1)
                    at["xT", u] = v.n

                def logits(u):
                    pe.wait_ge(v_freed, v.read(i, at["xT", u]))
                    for t in range(QT):
                        for k in range(2):
                            o = s.take()
                            pe.wait_ge(s_freed, s.free(i))
                            pe.matmul(o[:], xTa[:, t * P:t * P + P], phiTa[:, 512 * k:512 * k + 512], start=True, stop=False)
                            pe.matmul(o[:], xTb[:, t * P:t * P + P], phiTb[:, 512 * k:512 * k + 512], start=False, stop=True
                                      ).then_inc(s_filled, 1)
                    at["lg", u] = s.n

                def rows_T(o, src, t0):
                    for t in range(QT):
                        r = P if t < 2 else LAST
                        mm = pe.transpose(o[:, t * P:t * P + r], src[0:r, t, t0:t0 + P], ident[0:r, 0:r])
                    return mm

                def logits_T(u):
                    pe.wait_ge(s_freed, s.read(i, at["lg", u]))
                    for t in range(ST):
                        o = s.take()
                        pe.wait_ge(s_freed, s.free(i))
                        rows_T(o, lg[u], t * P).then_inc(s_filled, 1)
                    at["e1T", u] = s.n

                def e2_T(u):
                    pe.wait_ge(e2_ready, QT * (2 * i + u + 1))
                    for t in range(ST):
                        o = v.take()
                        pe.wait_ge(v_freed, v.free(i))
                        rows_T(o, e2, t * P).then_inc(v_filled, 1)

                def e1_back(u):
                    pe.wait_ge(s_freed, s.read(i, at["e1T", u]))
                    for t in range(QT):
                        r = P if t < 2 else LAST
                        for k in range(2):
                            o = s.take()
                            pe.wait_ge(s_freed, s.free(i))
                            for j in range(4):
                                mm = pe.transpose(o[0:r, j * P:j * P + P], e1T[:, 4 * k + j, t * P:t * P + r], ident[:])
                            mm.then_inc(s_filled, 1)
                    at["e1", u] = s.n

                def slot_inputs(u):
                    pe.wait_ge(s_freed, s.read(i, at["e1", u]))
                    for k in range(ST // 2):
                        o = s.take()
                        pe.wait_ge(s_freed, s.free(i))
                        for j in range(2):
                            st = 2 * k + j
                            for t in range(QT):
                                r = P if t < 2 else LAST
                                mm = pe.matmul(o[:, j * (D + 1):(j + 1) * (D + 1)], e1[0:r, t, st * P:st * P + P],
                                               xn[u][0:r, t, :], start=(t == 0), stop=(t == QT - 1))
                        mm.then_inc(s_filled, 1)

                def slots_T(u):
                    for k in range(2):
                        pe.wait_ge(xsn_ready, 2 * (2 * i + u) + k + 1)
                        oa = v.take()
                        ob = v.take()
                        pe.wait_ge(v_freed, v.free(i))
                        for j in range(4):
                            mm = pe.transpose(oa[:, j * P:j * P + P], xsn[:, 4 * k + j, 0:P], ident[:])
                        mm.then_inc(v_filled, 1)
                        for j in range(4):
                            if k == 0:
                                mm = pe.transpose(ob[0:DB, j * P:j * P + P], xsn[:, j, P:D], ident[:])
                            else:
                                mm = pe.transpose(ob[:, j * P:j * P + P], xsn[:, 4 + j, D - P:D], ident[:])
                        mm.then_inc(v_filled, 1)

                tokens_T(0)
                logits(0)
                tokens_T(1)
                logits_T(0)
                e2_T(0)
                logits(1)
                e1_back(0)
                slot_inputs(0)
                logits_T(1)
                e2_T(1)
                slots_T(0)
                e1_back(1)
                slot_inputs(1)
                slots_T(1)
                v.end()
                s.end()

        @block.scalar
        def _(act):
            act.sem_inc(s_freed, RING)
            with act.Fori(0, B // 2) as i:
                s = Uses(sbank, SN)

                def logits(u):
                    for t in range(QT):
                        for k in range(2):
                            o = s.take()
                            act.wait_ge(s_filled, s.filled(i))
                            act.copy(lg[u][:, t, 512 * k:512 * k + 512], o[:]).then_inc(s_freed, 1)
                    assert s.n + 1 == L_END[u]

                def over_slots(u):
                    for t in range(QT):
                        act.wait_ge(s_freed, RING + i * SN + L_END[u])
                        act.wait_ge(token_max, QT * (2 * i + u) + t + 1)
                        act.activation(e2[:, t, :], lg[u][:, t, :], ACT.Exp, bias=nmt[u][:, t:t + 1]).then_inc(e2_ready, 1)

                def over_tokens(u):
                    assert s.n + 1 == TL_AT[u]
                    for t in range(ST):
                        o = s.take()
                        act.wait_ge(slot_max, ST * (2 * i + u) + t + 1)
                        act.activation(e1T[:, t, :], o[:, 0:L], ACT.Exp, bias=nms[u][:, t:t + 1]).then_inc(s_freed, 1)

                def e1_back(u):
                    for t in range(QT):
                        r = P if t < 2 else LAST
                        for k in range(2):
                            o = s.take()
                            act.wait_ge(s_filled, s.filled(i))
                            act.copy(e1[0:r, t, 512 * k:512 * k + 512], o[0:r, :]).then_inc(s_freed, 1)

                def slot_inputs(u):
                    for k in range(ST // 2):
                        o = s.take()
                        act.wait_ge(s_filled, s.filled(i))
                        act.copy(xs[:, 2 * k:2 * k + 2, :], o[:, 0:2 * (D + 1)].rearrange("p (t d) -> p t d", t=2)
                                 ).then_inc(s_freed, 1)
                    assert s.n + 1 == XS_END[u]

                logits(0)
                over_slots(0)
                over_tokens(0)
                logits(1)
                e1_back(0)
                slot_inputs(0)
                over_slots(1)
                over_tokens(1)
                e1_back(1)
                slot_inputs(1)
                s.end()

        @block.vector
        def _(dve):
            dve.sem_inc(v_freed, RING)
            dve.sem_inc(e2_stored, 16)
            for u in range(2):
                dve.memset(hb[u][:, 2, :], 0.0).then_inc(init_done, 1)
                dve.memset(xn[u][:, :, D:D + 1], 1.0).then_inc(init_done, 1)
            dve.wait_ge(setup_mm, ST)
            parts = ((phiTa, P, 0), (phiTb, DB, 2))
            for dst, rows, b0 in parts:
                for k in range(2):
                    dve.tensor_copy(dst[:, 512 * k:512 * k + 512], vbank[b0 + k][0:rows, :]).then_inc(setup_step, 1)
            dve.wait_ge(setup_step, 4)
            for k, (src, rows, _) in enumerate(parts):
                dve.tensor_tensor(sq[0:rows, k, :], src[:], src[:], ALU.mult).then_inc(setup_step, 1)
            dve.wait_ge(setup_step, 6)
            for k, (src, rows, _) in enumerate(parts):
                dve.tensor_reduce(pn[0:rows, k, :], sq[0:rows, k, :].rearrange("d (n p) -> d p n", n=N_EXP),
                                  AX.X, ALU.add).then_inc(setup_step, 1)
            dve.wait_ge(setup_step, 8)
            dve.tensor_scalar(pn[:, 0, :], pn[:, 0, :], PHI_EPS, None, ALU.add).then_inc(setup_step, 1)
            dve.tensor_scalar(pn[0:DB, 1, :], pn[0:DB, 1, :], PHI_EPS, None, ALU.add).then_inc(pn_ready, 1)
            dve.wait_ge(pn_ready, 3)
            for k, (src, rows, _) in enumerate(parts):
                w = src[:].rearrange("d (n p) -> d n p", n=N_EXP)
                dve.tensor_tensor(w, w, pn[0:rows, k:k + 1, :].to_broadcast([rows, N_EXP, SLOTS_PER]), ALU.mult
                                  ).then_inc(setup_step, 1)
            dve.wait_ge(setup_mm, ST + 2)
            for dst, col, k in ((gTa[:], (0, N_EXP), 0), (xsTa[:, :, EC], (0, N_EXP), 1)):
                dve.tensor_copy(dst, sbank[k][:, col[0]:col[1]]).then_inc(setup_step, 1)
            for dst, k in ((gTb, 0), (xsTb[:, :, EC], 1)):
                dve.tensor_copy(dst[0:DB, :], sbank[k][0:DB, P:P + HALF]).then_inc(setup_step, 1)
                dve.tensor_copy(dst[DB:P, :], sbank[k][DB:P, 2 * P:2 * P + HALF]).then_inc(setup_step, 1)
            dve.wait_ge(setup_step, 17)
            dve.sem_inc(setup_step, 1)
            with dve.Fori(0, B // 2) as i:
                v = Uses(vbank, VN)
                steps = [0]

                def link(ins):
                    steps[0] += 1
                    ins.then_inc(vec_step, 1)
                    dve.wait_ge(vec_step, i * VSTEPS + steps[0])

                def layernorm(u):
                    dve.wait_ge(h_in[u], 32 * (i + 1))
                    for t in range(QT):
                        ins = dve.bn_stats(stats[:, t, :], hb[u][:, t, :])
                    link(ins)
                    dve.sem_inc(carried, 1)
                    for t in range(QT):
                        ins = dve.bn_aggr(mv[u][:, t, :], stats[:, t, :])
                    link(ins)
                    dve.tensor_scalar(var[u][:], mv[u][:, :, 1], LN_EPS, None, ALU.add).then_inc(var_ready, 1)

                def normalize(u):
                    dve.wait_ge(rstd_ready, 2 * i + u + 1)
                    for t in range(QT):
                        ins = dve.tensor_scalar(xn[u][:, t, 0:D], hb[u][:, t, :], mv[u][:, t, 0:1], rstd[u][:, t:t + 1],
                                                ALU.subtract, ALU.mult)
                    ins.then_inc(xn_ready, 1)

                def tokens_T(u):
                    for dst, rows in ((xTa, P), (xTb, DB)):
                        o = v.take()
                        dve.wait_ge(v_filled, v.filled(i))
                        dve.tensor_copy(dst[:], o[0:rows, 0:LP]).then_inc(v_freed, 1)

                def token_maxima(u):
                    dve.wait_ge(s_freed, RING + i * SN + L_END[u])
                    for t in range(QT):
                        dve.tensor_reduce(nmt[u][:, t:t + 1], lg[u][:, t, :], AX.X, ALU.max, negate=True
                                          ).then_inc(token_max, 1)

                def slot_maxima(u):
                    for t in range(ST):
                        dve.wait_ge(s_filled, i * SN + TL_AT[u] + t + 1)
                        dve.tensor_reduce(nms[u][:, t:t + 1], sbank[(TL_AT[u] + t) % RING][:, 0:L], AX.X, ALU.max,
                                          negate=True).then_inc(slot_max, 1)

                def e2_T(u):
                    dve.wait_ge(e2_stored, 16 * (2 * i + u + 1))
                    for t in range(ST):
                        o = v.take()
                        dve.wait_ge(v_filled, v.filled(i))
                        dve.tensor_copy(e2T[:, t, :], o[:, 0:L]).then_inc(v_freed, 1)
                    assert v.n + 1 == TE2_END[u]

                def slot_norm(u):
                    dve.wait_ge(s_freed, RING + i * SN + XS_END[u])
                    for t in range(ST):
                        ins = dve.bn_stats(stats[:, t, :], xs[:, t, 0:D])
                    link(ins)
                    dve.sem_inc(carried, 1)
                    for t in range(ST):
                        ins = dve.bn_aggr(smv[:, t, :], stats[:, t, :])
                    link(ins)
                    link(dve.tensor_tensor(ssq[:], xs[:, :, D], xs[:, :, D], ALU.mult))
                    dve.scalar_tensor_tensor(svar[:], ssq[:], LN_EPS, smv[:, :, 1], ALU.mult, ALU.add
                                             ).then_inc(svar_ready, 1)
                    dve.wait_ge(srstd_ready, 2 * i + u + 1)
                    for k in range(2):
                        for t in range(4 * k, 4 * k + 4):
                            ins = dve.tensor_scalar(xsn[:, t, :], xs[:, t, 0:D], smv[:, t, 0:1], srstd[:, t:t + 1],
                                                    ALU.subtract, ALU.mult)
                        ins.then_inc(xsn_ready, 1)

                def slots_T(u):
                    for k in range(2):
                        c = bass.ds((2 * i + u) * SLOTS_PER, SLOTS_PER)
                        for dst, g, r0, r1 in (
                            (xsTa[:, HALF * k:HALF * k + HALF, c], gTa[:, HALF * k:HALF * k + HALF], 0, P),
                            (xsTb[DB * k:DB * k + DB, :, c], gTb[DB * k:DB * k + DB, :], DB * k, DB * k + DB),
                        ):
                            o = v.take()
                            dve.wait_ge(v_filled, v.filled(i))
                            dve.tensor_tensor(dst, o[r0:r1, :].rearrange("d (n p) -> d n p", n=HALF),
                                              g.unsqueeze(2).to_broadcast([r1 - r0, HALF, SLOTS_PER]), ALU.mult
                                              ).then_inc(v_freed, 1)

                layernorm(0)
                layernorm(1)
                normalize(0)
                normalize(1)
                tokens_T(0)
                tokens_T(1)
                token_maxima(0)
                slot_maxima(0)
                e2_T(0)
                slot_norm(0)
                token_maxima(1)
                slot_maxima(1)
                e2_T(1)
                slots_T(0)
                slot_norm(1)
                slots_T(1)
                v.end()
                assert steps[0] == VSTEPS, steps[0]


def expert_phase(nc, xsTa, xsTb, w1, b1, w2, b2, c_ident, ys_d):
    with ExitStack() as ctx:
        a = Pool_(nc, ctx, "ex")
        NB = 4
        ident = a.sb("ident", [P, P])
        b1_in = a.sb("b1_in", [N_EXP, HID])
        b1T = a.sb("b1T", [P, HT, N_EXP])
        w1a = [a.sb(f"w1a{j}", [P, HID]) for j in range(NB)]
        w1b = [a.sb(f"w1b{j}", [P, HID]) for j in range(NB)]
        w2s = [a.sb(f"w2s{j}", [P, HT, D]) for j in range(NB)]
        b2s = [a.sb(f"b2s{j}", [P, D]) for j in range(NB)]
        bias = [a.sb(f"bias{j}", [P, HT]) for j in range(NB)]
        hT = [a.sb(f"hT{j}", [P, HT, EC]) for j in range(2)]
        ys = [a.sb(f"ys{j}", [P, 2, D]) for j in range(2)]
        vbank = [a.bank(f"vbank{i}") for i in range(RING)]
        sbank = [a.bank(f"sbank{i}") for i in range(RING)]
        consts_in = a.sem("consts_in")
        init_done = a.sem("init_done")
        b1_mm = a.sem("b1_mm")
        b1_ready = a.sem("b1_ready")
        v_filled, v_freed = a.sem("v_filled"), a.sem("v_freed")
        s_filled, s_freed = a.sem("s_filled"), a.sem("s_freed")
        w_in = [a.sem(f"w_in{j}") for j in range(NB)]
        bias_ready = a.sem("bias_ready")
        ys_stored = [a.sem(f"ys_stored{j}") for j in range(2)]
        block = ctx.enter_context(nc.Block())
        VN, SN = 2 * NB, 3 * NB
        N_W = 4

        def expert(i, j):
            return HALF * (j // 2) + 2 * i + j % 2

        @block.sync
        def _(sp):
            sp.dma_start(ident[:], c_ident).then_inc(consts_in, 16)
            sp.dma_start(b1_in[:], b1).then_inc(consts_in, 16)
            sp.wait_ge(init_done, NB)

            def load(n, j):
                r = DB * (j // 2)
                sp.dma_start(w1a[j][:], w1[n, 0:P, :]).then_inc(w_in[j], 16)
                sp.dma_start(w1b[j][r:r + DB, :], w1[n, P:D, :]).then_inc(w_in[j], 16)
                sp.dma_start(w2s[j][:], w2[n].rearrange("(t p) d -> p t d", p=P)).then_inc(w_in[j], 16)
                sp.dma_start(b2s[j][:], b2[n:n + 1, :].to_broadcast([P, D])).then_inc(w_in[j], 16)

            for j in range(NB):
                load(expert(0, j), j)
            w1v = w1.rearrange("(h i e) d k -> h e i d k", h=2, e=2)
            w2v = w2.rearrange("(h i e) k d -> h e i k d", h=2, e=2)
            b2v = b2.rearrange("(h i e) d -> h e i d", h=2, e=2)
            with sp.Fori(0, N_EXP // NB) as i:
                for j in range(NB):
                    sp.wait_ge(v_freed, RING + i * VN + 2 * j + 2)
                    yv = ys_d.rearrange("(k b) (h i e p) d -> h e k i b p d", k=2, h=2, e=2, p=SLOTS_PER)
                    for k in range(2):
                        sp.dma_start(yv[j // 2, j % 2, k, i], ys[j % 2][:, k, :]).then_inc(ys_stored[j % 2], 16)
                    nx = (i + 1) % (N_EXP // NB)
                    r = DB * (j // 2)
                    sp.dma_start(w1a[j][:], w1v[j // 2, j % 2, nx, 0:P, :]).then_inc(w_in[j], 16)
                    sp.dma_start(w1b[j][r:r + DB, :], w1v[j // 2, j % 2, nx, P:D, :]).then_inc(w_in[j], 16)
                    sp.dma_start(w2s[j][:], w2v[j // 2, j % 2, nx].rearrange("(t p) d -> p t d", p=P)
                                 ).then_inc(w_in[j], 16)
                    sp.dma_start(b2s[j][:], b2v[j // 2, j % 2, nx].unsqueeze(0).to_broadcast([P, D])
                                 ).then_inc(w_in[j], 16)
            for j in range(NB):
                sp.wait_ge(w_in[j], 16 * N_W * (1 + N_EXP // NB))
            for j in range(2):
                sp.wait_ge(ys_stored[j], 32 * (1 + N_EXP // 2))

        @block.tensor
        def _(pe):
            pe.wait_ge(consts_in, 32)
            for t in range(HT):
                pe.transpose(vbank[0][:, t * N_EXP:(t + 1) * N_EXP], b1_in[:, t * P:t * P + P], ident[0:N_EXP, 0:N_EXP]
                             ).then_inc(b1_mm, 1)
            pe.wait_ge(b1_ready, 1)
            with pe.Fori(0, N_EXP // NB) as i:
                v = Uses(vbank, VN)
                s = Uses(sbank, SN)
                at = {}

                def up(j):
                    pe.wait_ge(w_in[j], 16 * N_W * (i + 1))
                    n = expert(i, j)
                    for t in range(HT):
                        o = s.take()
                        pe.wait_ge(s_freed, s.free(i))
                        pe.matmul(o[:, 0:EC1], w1a[j][:, t * P:t * P + P], xsTa[:, bass.ds(n, 1), :], start=True, stop=False)
                        pe.matmul(o[:, 0:EC1], w1b[j][:, t * P:t * P + P], xsTb[:, bass.ds(2 * i + j % 2, 1), :],
                                  start=False, stop=True).then_inc(s_filled, 1)
                    at[j] = s.n

                def down(j):
                    pe.wait_ge(s_freed, s.read(i, at[j]))
                    for k in range(2):
                        o = v.take()
                        pe.wait_ge(v_freed, v.free(i))
                        for t in range(HT):
                            mm = pe.matmul(o[:, 0:D], hT[j % 2][:, t, k * P:k * P + P], w2s[j][:, t, :],
                                           start=(t == 0), stop=(t == HT - 1))
                        mm.then_inc(v_filled, 1)

                up(0)
                up(1)
                down(0)
                up(2)
                down(1)
                up(3)
                down(2)
                down(3)
                v.end()
                s.end()

        @block.scalar
        def _(act):
            act.sem_inc(s_freed, RING)
            with act.Fori(0, N_EXP // NB) as i:
                s = Uses(sbank, SN)
                for j in range(NB):
                    n = expert(i, j)
                    for t in range(HT):
                        o = s.take()
                        act.wait_ge(s_filled, s.filled(i))
                        act.activation(bias[j][:, t:t + 1], o[:, EC:EC1], ACT.Identity,
                                       bias=b1T[:, t, bass.ds(n, 1)]).then_inc(bias_ready, 1)
                        act.wait_ge(bias_ready, i * SN + HT * j + t + 1)
                        act.activation(hT[j % 2][:, t, :], o[:, 0:EC], ACT.Gelu, bias=bias[j][:, t:t + 1]
                                       ).then_inc(s_freed, 1)
                s.end()

        @block.vector
        def _(dve):
            dve.sem_inc(v_freed, RING)
            for j in range(2):
                dve.sem_inc(ys_stored[j], 32)
            for j in range(NB):
                r = DB * (1 - j // 2)
                dve.memset(w1b[j][r:r + DB, :], 0.0).then_inc(init_done, 1)
            dve.wait_ge(b1_mm, HT)
            dve.tensor_copy(b1T[:], vbank[0][:, 0:HT * N_EXP].rearrange("p (t n) -> p t n", t=HT)).then_inc(b1_ready, 1)
            dve.wait_ge(b1_ready, 1)
            with dve.Fori(0, N_EXP // NB) as i:
                v = Uses(vbank, VN)
                for j in range(NB):
                    dve.wait_ge(ys_stored[j % 2], 32 * (2 * i + j // 2 + 1))
                    dve.wait_ge(w_in[j], 16 * N_W * (i + 1))
                    for k in range(2):
                        o = v.take()
                        dve.wait_ge(v_filled, v.filled(i))
                        dve.tensor_tensor(ys[j % 2][:, k, :], o[:, 0:D], b2s[j][:], ALU.add).then_inc(v_freed, 1)
                v.end()


def combine_phase(nc, h2_d, e2_d, ys_d, out):
    with ExitStack() as ctx:
        a = Pool_(nc, ctx, "co")
        ys = [a.sb(f"ys{u}", [P, ST, D + 1]) for u in range(2)]
        e2T = [a.sb(f"e2T{u}", [P, ST, L]) for u in range(2)]
        hb = [a.sb(f"hb{u}", [P, QT, D]) for u in range(2)]
        res = [a.sb(f"res{u}", [P, QT, D]) for u in range(2)]
        rec = a.sb("rec", [P, 2 * QT])
        bank = [a.bank(f"bank{i}") for i in range(2 * QT)]
        ones_set = a.sem("ones_set")
        loaded = [a.sem(f"loaded{u}") for u in range(2)]
        filled, freed = a.sem("filled"), a.sem("freed")
        rec_ready = a.sem("rec_ready")
        stored = [a.sem(f"stored{u}") for u in range(2)]
        block = ctx.enter_context(nc.Block())
        N_IN = 4

        @block.sync
        def _(sp):
            ysv = ys_d.rearrange("(i u) (t p) d -> u i p t d", u=2, p=P)
            e2v = e2_d.rearrange("(i u) p c -> u i p c", u=2)
            h2v = h2_d.rearrange("(i u) l d -> u i l d", u=2)
            with sp.Fori(0, B // 2) as i:
                for u in range(2):
                    sp.wait_ge(freed, QT * (2 * i + u + 1))
                    sp.dma_start(ys[u][:, :, 0:D], ysv[u, i]).then_inc(loaded[u], 16)
                    sp.dma_start(e2T[u][:].rearrange("p t c -> p (t c)"), e2v[u, i]).then_inc(loaded[u], 16)
                    sp.dma_start(hb[u][:, 0:2, :], h2v[u, i, 0:2 * P].rearrange("(t p) d -> p t d", p=P)
                                 ).then_inc(loaded[u], 16)
                    sp.dma_start(hb[u][0:LAST, 2, :], h2v[u, i, 2 * P:L]).then_inc(loaded[u], 16)

        @block.scalar
        def _(act):
            ov = out.rearrange("(i u) l d -> u i l d", u=2)
            with act.Fori(0, B // 2) as i:
                for u in range(2):
                    act.wait_ge(freed, QT * (2 * i + u + 3))
                    act.dma_start(ov[u, i, 0:2 * P].rearrange("(t p) d -> p t d", p=P), res[u][:, 0:2, :]
                                  ).then_inc(stored[u], 16)
                    act.dma_start(ov[u, i, 2 * P:L], res[u][0:LAST, 2, :]).then_inc(stored[u], 16)
            for u in range(2):
                act.wait_ge(stored[u], 32 * (1 + B // 2))

        @block.tensor
        def _(pe):
            pe.wait_ge(ones_set, 2)
            with pe.Fori(0, B // 2) as i:
                for u in range(2):
                    pe.wait_ge(loaded[u], 16 * N_IN * (i + 1))
                    for t in range(QT):
                        r = P if t < 2 else LAST
                        pe.wait_ge(freed, QT * (2 * i + u) + t + 1)
                        for st in range(ST):
                            mm = pe.matmul(bank[QT * u + t][0:r, 0:D + 1], e2T[u][:, st, t * P:t * P + r], ys[u][:, st, :],
                                           start=(st == 0), stop=(st == ST - 1))
                        mm.then_inc(filled, 1)

        @block.vector
        def _(dve):
            dve.sem_inc(freed, 2 * QT)
            for u in range(2):
                dve.sem_inc(stored[u], 32)
                dve.memset(ys[u][:, :, D:D + 1], 1.0).then_inc(ones_set, 1)
            with dve.Fori(0, B // 2) as i:
                for u in range(2):
                    dve.wait_ge(stored[u], 32 * (i + 1))
                    for t in range(QT):
                        r = P if t < 2 else LAST
                        o = bank[QT * u + t]
                        rc = rec[0:r, QT * u + t:QT * u + t + 1]
                        dve.wait_ge(filled, QT * (2 * i + u) + t + 1)
                        dve.reciprocal(rc, o[0:r, D:D + 1]).then_inc(rec_ready, 1)
                        dve.wait_ge(rec_ready, QT * (2 * i + u) + t + 1)
                        dve.scalar_tensor_tensor(res[u][0:r, t, :], o[0:r, 0:D], rc, hb[u][0:r, t, :],
                                                 ALU.mult, ALU.add).then_inc(freed, 1)


def fusion_kernel(nc, i, out):
    h_d = nc.dram_tensor("h_d", [B, L, D], F32, kind="Internal").ap()
    h2_d = nc.dram_tensor("h2_d", [B, L, D], F32, kind="Internal").ap()
    e2_d = nc.dram_tensor("e2_d", [B, P, ST * L], F32, kind="Internal").ap()
    ys_d = nc.dram_tensor("ys_d", [B, S, D], F32, kind="Internal").ap()
    tok = "L0_tok_"
    patch_phase(nc, i["x"], i["txt"], i[tok + "freq_weight_h"], i[tok + "freq_weight_w"], i[tok + "proj_w"],
                i[tok + "proj_b"], i[tok + "cls_token"], i[tok + "position_embeddings"], i["c_dft"], i["c_selh"],
                i["c_selw"], i["c_ident"], h_d)
    attention_phase(nc, h_d, *(i["L0_attn_" + n] for n in ("Wq", "bq", "Wk", "bk", "Wv", "bv", "Wo", "bo")),
                    i["c_rope"], i["c_ident"], i["c_mask"], i["c_maskT"], h2_d)
    with ExitStack() as ctx:
        xsTa = ctx.enter_context(nc.sbuf_tensor("xsTa", [P, N_EXP, EC1], F32))
        xsTb = ctx.enter_context(nc.sbuf_tensor("xsTb", [P, HALF, EC1], F32))
        f = {n: i["L0_ffn_" + n] for n in ("phi", "ln_g", "ln_b", "w1", "b1", "w2", "b2")}
        dispatch_phase(nc, xsTa, xsTb, h2_d, f["phi"], f["ln_g"], f["ln_b"], i["c_ident"], e2_d)
        expert_phase(nc, xsTa, xsTb, f["w1"], f["b1"], f["w2"], f["b2"], i["c_ident"], ys_d)
    combine_phase(nc, h2_d, e2_d, ys_d, out)


_INS = ["x", "txt", "L0_tok_freq_weight_h", "L0_tok_freq_weight_w", "L0_tok_proj_w", "L0_tok_proj_b",
        "L0_tok_cls_token", "L0_tok_position_embeddings", "L0_attn_Wq", "L0_attn_bq", "L0_attn_Wk", "L0_attn_bk",
        "L0_attn_Wv", "L0_attn_bv", "L0_attn_Wo", "L0_attn_bo", "L0_ffn_phi", "L0_ffn_ln_g", "L0_ffn_ln_b",
        "L0_ffn_w1", "L0_ffn_b1", "L0_ffn_w2", "L0_ffn_b2"]


def kernel(**inputs):
    import concourse.bacc as _bacc
    from concourse.bass_utils import run_bass_kernel_spmd as _run

    nc = _bacc.Bacc("TRN2", target_bir_lowering=False, num_devices=1)
    arrays, args = {}, {}
    for name, value in [(n, inputs[n]) for n in _INS] + list(shape_constants().items()):
        v = np.ascontiguousarray(value)
        arrays[f"in_{name}_dram"] = v
        args[name] = nc.dram_tensor(f"in_{name}_dram", v.shape, mybir.dt.from_np(v.dtype), kind="ExternalInput").ap()
    out = nc.dram_tensor("out_0_dram", (B, L, D), F32, kind="ExternalOutput").ap()
    fusion_kernel(nc, args, out)
    r = _run(nc, [arrays], core_ids=[0])
    return r.results[0]["out_0_dram"]
```

```python
from contextlib import ExitStack

import numpy as np

import concourse.bass as bass
from concourse import mybir

F32 = mybir.dt.float32
F32R = mybir.dt.float32r
BF16 = mybir.dt.bfloat16
ALU = mybir.AluOpType
ACT = mybir.ActivationFunctionType
AX = mybir.AxisListType

P = 128
D = 192
DB = D - P
B = 16
C_IN, IMG, PATCH = 3, 224, 16
NH = IMG // PATCH
NPATCH = NH * NH
TXT = 128
L = 1 + NPATCH + TXT
QT = 3
LAST = L - 2 * P
LE = L + L % 2
LASTE = LE - 2 * P
LP = QT * P
HEADS, HD = 12, 16
N_EXP, SLOTS_PER = 64, 16
S = N_EXP * SLOTS_PER
ST = S // P
EPT = P // SLOTS_PER
HID = 2 * D
HT = HID // P
KW = PATCH // 2 + 1
NF = PATCH * KW
FT = 4
FR = C_IN * NF // FT
SHIFTS = 2
PWS = PATCH // SHIFTS
ROWS = SHIFTS * C_IN * PATCH
NROW = NH // 2
PTOK = NROW * NH
LN_EPS = 1e-5
PHI_EPS = 1e-6
MASKED = -1e30
PRIME = 2
RING = 4


def shape_constants():
    k = np.arange(C_IN * NF)
    c, kh, kw = k // NF, (k % NF) // KW, k % KW
    ph = np.arange(PATCH)
    dft = np.zeros((C_IN * NF, PWS, SHIFTS, C_IN, PATCH), np.float64)
    for s in range(SHIFTS):
        for p in range(PWS):
            pw = p + PWS * s
            ang = 2 * np.pi * ((kh[:, None] * ph[None, :] + kw[:, None] * pw) % PATCH) / PATCH
            dft[k, p, s, c, :] = np.cos(ang) / PATCH
    dft = dft.reshape(FT, FR, PWS, ROWS).transpose(1, 0, 2, 3)
    sel_h = (np.arange(PATCH)[:, None] == kh[None, :]).astype(np.float32)
    sel_w = (np.arange(KW)[:, None] == kw[None, :]).astype(np.float32)
    inv = (1.0 / 10000.0 ** (np.arange(0, HD, 2, dtype=np.float32) / np.float32(HD))).astype(np.float32)
    ang = (np.arange(LP, dtype=np.float32)[:, None] * inv[None, :]).astype(np.float32)
    cos, sin = np.cos(ang.astype(np.float64)), np.sin(ang.astype(np.float64))
    rope = np.concatenate([cos, cos, -sin, sin], 1).reshape(QT, P, 4 * (HD // 2)).transpose(1, 0, 2)
    i = np.arange(P)
    return {
        "c_dft": np.ascontiguousarray(dft.astype(np.float32)),
        "c_selh": sel_h,
        "c_selw": sel_w,
        "c_rope": np.ascontiguousarray(rope.astype(np.float32)),
        "c_ident": np.eye(P, dtype=np.float32),
        "c_mask": np.where(i[None, :] > i[:, None], MASKED, 0.0).astype(np.float32),
        "c_maskT": np.where(i[:, None] > i[None, :], MASKED, 0.0).astype(np.float32),
    }


class Pool_:

    def __init__(self, nc, ctx, tag):
        self.nc, self.ctx, self.tag = nc, ctx, tag

    def sb(self, name, shape, dt=F32):
        return self.ctx.enter_context(self.nc.sbuf_tensor(f"{self.tag}_{name}", shape, dt))

    def bank(self, name):
        return self.ctx.enter_context(self.nc.psum_tensor(f"{self.tag}_{name}", [P, 512], F32))

    def sem(self, name):
        return self.ctx.enter_context(self.nc.semaphore(f"{self.tag}_{name}"))


def patch_phase(nc, x, txt, fh, fw, proj_w, proj_b, cls_token, pos, c_dft, c_selh, c_selw, c_ident, h_d):
    with ExitStack() as ctx:
        a = Pool_(nc, ctx, "pt")
        ident = a.sb("ident", [P, P])
        dft = a.sb("dft", [FR, FT, PWS, ROWS])
        selh = a.sb("selh", [PATCH, C_IN * NF])
        selw = a.sb("selw", [KW, C_IN * NF])
        fhc = a.sb("fhc", [PATCH, 1])
        fwc = a.sb("fwc", [KW, 1])
        pw_a = a.sb("pw_a", [P, C_IN * NF])
        pw_b = a.sb("pw_b", [DB, C_IN * NF])
        fsel = a.sb("fsel", [FR, 2 * FT])
        fcol = a.sb("fcol", [FR, FT])
        pT = a.sb("pT", [FR, FT, D])
        weff = a.sb("weff", [ROWS, PWS, D])
        ones = a.sb("ones", [1, P])
        brow = a.sb("brow", [1, D])
        clsr = a.sb("clsr", [1, D])
        pos0 = a.sb("pos0", [1, D])
        cls0 = a.sb("cls0", [1, D])
        clsb = a.sb("clsb", [B, D])
        posb = a.sb("posb", [PTOK, 2, D])
        img = [a.sb(f"img{u}", [ROWS, NH, IMG]) for u in range(2)]
        emb = [a.sb(f"emb{u}", [PTOK, 2, D]) for u in range(2)]
        bank = [a.bank(f"bank{i}") for i in range(8)]
        consts_in = a.sem("consts_in")
        ones_set = a.sem("ones_set")
        projT_done = a.sem("projT_done")
        fsel_done = a.sem("fsel_done")
        fsel_copied = a.sem("fsel_copied")
        fcol_done = a.sem("fcol_done")
        pT_ready = a.sem("pT_ready")
        weff_mm = a.sem("weff_mm")
        weff_ready = a.sem("weff_ready")
        bias_mm = a.sem("bias_mm")
        posb_ready = a.sem("posb_ready")
        cls0_ready = a.sem("cls0_ready")
        cls_mm = a.sem("cls_mm")
        clsb_ready = a.sem("clsb_ready")
        img_in = [a.sem(f"img_in{u}") for u in range(2)]
        emb_mm = a.sem("emb_mm")
        emb_ready = a.sem("emb_ready")
        emb_stored = [a.sem(f"emb_stored{u}") for u in range(2)]
        stored = a.sem("stored")
        N_CONST = 12
        block = ctx.enter_context(nc.Block())

        @block.sync
        def _(sp):
            sp.dma_start(h_d[:, 1 + NPATCH:L, :], txt).then_inc(stored, 16)
            for dst, src in (
                (ident[:], c_ident), (dft[:], c_dft), (selh[:], c_selh), (selw[:], c_selw),
                (fhc[:], fh.rearrange("(a b) -> a b", b=1)), (fwc[:], fw.rearrange("(a b) -> a b", b=1)),
                (pw_a[:], proj_w[0:P, :]), (pw_b[:], proj_w[P:D, :]),
                (brow[:], proj_b.rearrange("(a b) -> a b", a=1)), (clsr[:], cls_token[0]),
                (pos0[:], pos[0, 0:1, :]),
                (posb[:], pos[0, 1:1 + NPATCH, :].rearrange("(t p) d -> p t d", p=PTOK)),
            ):
                sp.dma_start(dst, src).then_inc(consts_in, 16)
            with sp.Fori(0, B // 2) as i:
                for u in range(2):
                    sp.wait_ge(emb_mm, 2 * i + u + 1)
                    xb = x.rearrange("(i u) c (nh ph) w -> u i c ph nh w", u=2, ph=PATCH)[u, i]
                    for s in range(SHIFTS):
                        for c in range(C_IN):
                            r0 = (s * C_IN + c) * PATCH
                            w = IMG - PWS * s
                            sp.dma_start(img[u][r0:r0 + PATCH, :, 0:w], xb[c, :, :, PWS * s:IMG]
                                         ).then_inc(img_in[u], 16)

        @block.scalar
        def _(act):
            for u in range(2):
                act.sem_inc(emb_stored[u], 16)
            act.wait_ge(clsb_ready, 1)
            act.dma_start(h_d[:, 0, :], clsb[:]).then_inc(stored, 16)
            with act.Fori(0, B // 2) as i:
                for u in range(2):
                    act.wait_ge(emb_ready, PRIME + 2 * i + u + 1)
                    hb = h_d.rearrange("(i u) l d -> u i l d", u=2)[u, i]
                    act.dma_start(hb[1:1 + NPATCH, :].rearrange("(t p) d -> p t d", p=PTOK), emb[u][:]
                                  ).then_inc(emb_stored[u], 16)
            act.wait_ge(stored, 32)
            for u in range(2):
                act.wait_ge(emb_stored[u], 16 * (1 + B // 2))

        @block.tensor
        def _(pe):
            pe.sem_inc(emb_mm, PRIME)
            pe.wait_ge(consts_in, 16 * N_CONST)
            for t in range(FT):
                o = bank[t // 2][0:FR, (t % 2) * D:(t % 2) * D + D]
                pe.transpose(o[:, 0:P], pw_a[:, FR * t:FR * t + FR], ident[:])
                pe.transpose(o[:, P:D], pw_b[:, FR * t:FR * t + FR], ident[0:DB, 0:DB]).then_inc(projT_done, 1)
            for t in range(FT):
                pe.matmul(bank[2][0:FR, t:t + 1], selh[:, FR * t:FR * t + FR], fhc[:], start=True, stop=True)
                pe.matmul(bank[2][0:FR, FT + t:FT + t + 1], selw[:, FR * t:FR * t + FR], fwc[:],
                          start=True, stop=True).then_inc(fsel_done, 1)
            pe.wait_ge(ones_set, 1)
            pe.matmul(bank[3][0:PTOK, 0:D], ones[:, 0:PTOK], brow[:], start=True, stop=True).then_inc(bias_mm, 1)
            for p in range(PWS):
                if p == 0:
                    pe.wait_ge(pT_ready, FT)
                for t in range(FT):
                    mm = pe.matmul(bank[4 + p // 2][0:ROWS, (p % 2) * D:(p % 2) * D + D], dft[:, t, p, :], pT[:, t, :],
                                   start=(t == 0), stop=(t == FT - 1))
                mm.then_inc(weff_mm, 1)
            pe.wait_ge(cls0_ready, 1)
            pe.matmul(bank[2][0:B, 256:256 + D], ones[:, 0:B], cls0[:], start=True, stop=True).then_inc(cls_mm, 1)
            pe.wait_ge(weff_ready, PWS)
            pe.wait_ge(clsb_ready, 1)
            with pe.Fori(0, B // 2) as i:
                for u in range(2):
                    pe.wait_ge(img_in[u], 16 * SHIFTS * C_IN * (i + 1))
                    pe.wait_ge(emb_ready, 2 * i + u + 1)
                    for t in range(2):
                        for p in range(PWS):
                            px = img[u][:, t * NROW:(t + 1) * NROW, p:p + PATCH * (NH - 1) + 1:PATCH]
                            mm = pe.matmul(bank[u * 2 + t][0:PTOK, 0:D], px, weff[:, p, :],
                                           start=(p == 0), stop=(p == PWS - 1))
                    mm.then_inc(emb_mm, 1)

        @block.vector
        def _(dve):
            dve.sem_inc(emb_ready, PRIME)
            dve.memset(ones[:], 1.0).then_inc(ones_set, 1)
            dve.wait_ge(fsel_done, FT)
            dve.tensor_copy(fsel[:], bank[2][0:FR, 0:2 * FT]).then_inc(fsel_copied, 1)
            dve.wait_ge(fsel_copied, 1)
            dve.tensor_tensor(fcol[:], fsel[:, 0:FT], fsel[:, FT:2 * FT], ALU.mult).then_inc(fcol_done, 1)
            dve.wait_ge(fcol_done, 1)
            for t in range(FT):
                dve.wait_ge(projT_done, 2 * (t // 2) + 2)
                dve.tensor_scalar(pT[:, t, :], bank[t // 2][0:FR, (t % 2) * D:(t % 2) * D + D], fcol[:, t:t + 1],
                                  None, ALU.mult).then_inc(pT_ready, 1)
            dve.wait_ge(consts_in, 16 * N_CONST)
            dve.wait_ge(bias_mm, 1)
            for t in range(2):
                dve.tensor_tensor(posb[:, t, :], posb[:, t, :], bank[3][0:PTOK, 0:D], ALU.add).then_inc(posb_ready, 1)
            dve.tensor_tensor(cls0[:], clsr[:], pos0[:], ALU.add).then_inc(cls0_ready, 1)
            for p in range(PWS):
                dve.wait_ge(weff_mm, 2 * (p // 2) + 2)
                dve.tensor_copy(weff[:, p, :], bank[4 + p // 2][0:ROWS, (p % 2) * D:(p % 2) * D + D]
                                ).then_inc(weff_ready, 1)
            dve.wait_ge(cls_mm, 1)
            dve.tensor_copy(clsb[:], bank[2][0:B, 256:256 + D]).then_inc(clsb_ready, 1)
            dve.wait_ge(posb_ready, 2)
            with dve.Fori(0, B // 2) as i:
                for u in range(2):
                    dve.wait_ge(emb_mm, PRIME + 2 * i + u + 1)
                    dve.wait_ge(emb_stored[u], 16 * (i + 1))
                    for t in range(2):
                        add = dve.tensor_tensor(emb[u][:, t, :], bank[u * 2 + t][0:PTOK, 0:D], posb[:, t, :], ALU.add)
                    add.then_inc(emb_ready, 1)


class Uses:

    def __init__(self, banks, per_body):
        self.banks, self.per_body, self.n = banks, per_body, -1
        assert per_body % len(banks) == 0

    def take(self):
        self.n += 1
        return self.banks[self.n % len(self.banks)]

    def free(self, i):
        return i * self.per_body + self.n + 1

    def filled(self, i):
        return i * self.per_body + self.n + 1

    def read(self, i, n=None):
        return i * self.per_body + (self.n if n is None else n) + 1 + len(self.banks)

    def end(self):
        assert self.n + 1 == self.per_body, (self.n + 1, self.per_body)


class Count:

    def __init__(self, per_body):
        self.per_body, self.n, self.base, self.start = per_body, 0, 0, None

    def enter(self, i):
        self.base, self.start = i * self.per_body, self.n

    def leave(self, bodies):
        assert self.n - self.start == self.per_body, (self.start, self.n)
        self.base = (bodies - 1) * self.per_body

    def value(self, more=0):
        return self.base + self.n + more


class Ring(Count):

    def __init__(self, banks, per_body):
        super().__init__(per_body)
        assert per_body % len(banks) == 0
        self.banks = banks

    def take(self):
        self.n += 1
        return self.banks[(self.n - 1) % len(self.banks)]

    def free(self):
        return self.value()

    def filled(self):
        return self.value()

    def read(self, n=None):
        return self.value(len(self.banks) + (0 if n is None else n - self.n))


GROUP = 4
NG = HEADS // GROUP
PAIRS = HEADS // 2
STK = 64
MROW = 3 * HD
PTC = LE + (LE - P) + LASTE
AC = LE + LASTE
BC = LE - P


def attention_phase(nc, h_d, wq, bq, wk, bk, wv, bv, wo, bo, c_rope, c_ident, c_mask, c_maskT, h2_d):
    with ExitStack() as ctx:
        a = Pool_(nc, ctx, "at")
        ident = a.sb("ident", [P, P])
        identb = a.sb("identb", [P, P], BF16)
        identr = a.sb("identr", [P, P])
        maskf = a.sb("maskf", [P, 2, P])
        mask = a.sb("mask", [P, 2, P], BF16)
        rope = a.sb("rope", [P, QT, 2 * HD])
        w_in = a.sb("w_in", [P, 4, 2, D])
        wa = a.sb("wa", [P, 4, D])
        wb = a.sb("wb", [DB + 1, 4, D])
        half = a.sb("half", [P, QT])
        hb = [a.sb(f"hb{u}", [P, QT, D]) for u in range(2)]
        hr = [a.sb(f"hr{u}", [P, QT, D]) for u in range(2)]
        stats = [a.sb(f"stats{u}", [P, QT, 6]) for u in range(2)]
        mv = [a.sb(f"mv{u}", [P, QT, 2]) for u in range(2)]
        var = [a.sb(f"var{u}", [P, QT]) for u in range(2)]
        rstd = [a.sb(f"rstd{u}", [P, QT]) for u in range(2)]
        xn = [a.sb(f"xn{u}", [P, QT, D]) for u in range(2)]
        xTa = [a.sb(f"xTa{u}", [P, LP]) for u in range(2)]
        xTb = [a.sb(f"xTb{u}", [DB + 1, LP]) for u in range(2)]
        rots = [a.sb(f"rot{u}", [P, 2, 2 * HEADS, HD]) for u in range(2)]
        stk = [a.sb(f"stk{u}", [P, QT, 2 * HEADS, STK]) for u in range(2)]
        vaug = [a.sb(f"vaug{u}", [P, QT, HEADS, 32]) for u in range(2)]
        qT = [a.sb(f"qT{u}", [P, PAIRS, LP]) for u in range(2)]
        kT = [a.sb(f"kT{u}", [P, PAIRS, LP]) for u in range(2)]
        mx = [a.sb(f"mx{u}", [P, QT, HEADS]) for u in range(2)]
        probs = [a.sb(f"probs{u}", [P, GROUP, PTC]) for u in range(2)]
        oT = [a.sb(f"oT{u}", [P, NG, LP]) for u in range(2)]
        rden = [a.sb(f"rden{u}", [P, QT, HEADS]) for u in range(2)]
        on = [a.sb(f"on{u}", [P, QT, D]) for u in range(2)]
        onTa = [a.sb(f"onTa{u}", [P, LP]) for u in range(2)]
        onTb = [a.sb(f"onTb{u}", [DB + 1, LP]) for u in range(2)]
        h2 = [a.sb(f"h2{u}", [P, QT, D]) for u in range(2)]
        vbank = [a.bank(f"vbank{i}") for i in range(RING)]
        sbank = [a.bank(f"sbank{i}") for i in range(RING)]

        consts_in = a.sem("consts_in")
        init_done = a.sem("init_done")
        wT_mm = a.sem("wT_mm")
        wT_ready = a.sem("wT_ready")
        v_filled, v_freed = a.sem("v_filled"), a.sem("v_freed")
        s_filled, s_freed = a.sem("s_filled"), a.sem("s_freed")
        vec_step = a.sem("vec_step")
        carried = a.sem("carried")
        h_in = [a.sem(f"h_in{u}") for u in range(2)]
        hr_in = [a.sem(f"hr_in{u}") for u in range(2)]
        var_ready = a.sem("var_ready")
        rstd_ready = a.sem("rstd_ready")
        xn_ready = a.sem("xn_ready")
        rope_ready = a.sem("rope_ready")
        dup_ready = a.sem("dup_ready")
        max_ready = a.sem("max_ready")
        h2_stored = [a.sem(f"h2_stored{u}") for u in range(2)]
        block = ctx.enter_context(nc.Block())

        N_CONST = 16
        N_INIT = 17
        BODIES = B // 2 - 1
        VN, SN = 68, 84
        V_FIRST = 19
        V_ALONE = 15
        VSTEPS = 24
        FIRST_MAXES = [(0, g + j, 3, P) for g in (0, 6) for j in range(2)]
        MIDDLE_MAXES = [(1, g + j, 2, 2 * P) for g in range(0, HEADS, 4) for j in range(2)]
        LAST_MAXES = [[(2, 2 * p + j, 1, LE) for j in range(2)] for p in range(PAIRS)]

        @block.sync
        def _(sp):
            for dst, src in ((ident[:], c_ident), (maskf[:, 0, :], c_mask), (maskf[:, 1, :], c_maskT), (rope[:], c_rope)):
                sp.dma_start(dst, src).then_inc(consts_in, 16)
            for j, w in enumerate((wq, wk, wv, wo)):
                sp.dma_start(w_in[:, j, 0, :], w[0:P, :]).then_inc(consts_in, 16)
                sp.dma_start(w_in[0:DB, j, 1, :], w[P:D, :]).then_inc(consts_in, 16)
            for j, w in enumerate((bq, bk, bv, bo)):
                sp.dma_start(wb[DB:DB + 1, j, :], w.rearrange("(a b) -> a b", a=1)).then_inc(consts_in, 16)
            sp.wait_ge(init_done, N_INIT)
            hd = h_d.rearrange("(i u) l d -> u i l d", u=2)
            h2d = h2_d.rearrange("(i u) l d -> u i l d", u=2)

            def load(dst, arrived, u, b2):
                sp.dma_start(dst[u][:, 0:2, :], hd[u, b2, 0:2 * P].rearrange("(t p) d -> p t d", p=P)
                             ).then_inc(arrived[u], 16)
                sp.dma_start(dst[u][0:LAST, 2, :], hd[u, b2, 2 * P:L]).then_inc(arrived[u], 16)

            def store(u, b2, v_before, uses):
                sp.wait_ge(v_freed, v_before + RING + uses)
                sp.dma_start(h2d[u, b2, 0:2 * P].rearrange("(t p) d -> p t d", p=P), h2[u][:, 0:2, :]
                             ).then_inc(h2_stored[u], 16)
                sp.dma_start(h2d[u, b2, 2 * P:L], h2[u][0:LAST, 2, :]).then_inc(h2_stored[u], 16)

            for u in range(2):
                load(hb, h_in, u, 0)
            for u in range(2):
                load(hr, hr_in, u, 0)
            for u in range(2):
                sp.wait_ge(xn_ready, u + 1)
                load(hb, h_in, u, 1)
            with sp.Fori(0, BODIES) as i:
                for u in range(2):
                    sp.wait_ge(xn_ready, 2 * i + u + 3)
                    load(hb, h_in, u, (i + 2) % (B // 2))
                    store(u, i, V_FIRST + i * VN + u * (VN // 2), VN // 2)
                    load(hr, hr_in, u, i + 1)
            store(0, BODIES, V_FIRST + BODIES * VN, VN // 2)
            store(1, BODIES, V_FIRST + BODIES * VN + VN // 2, V_ALONE)
            for u in range(2):
                sp.wait_ge(h2_stored[u], 32 * (1 + B // 2))
                sp.wait_ge(h_in[u], 32 * (1 + B // 2))

        @block.gpsimd
        def _(pool):
            pool.memset(half[:], -0.5).then_inc(init_done, 1)
            pool.wait_ge(init_done, N_INIT)

            def deviations(b, u):
                pool.wait_ge(var_ready, b + 1)
                pool.tensor_tensor(rstd[u][:], var[u][:], half[:], ALU.pow).then_inc(rstd_ready, 1)

            def duplicates(b, u):
                for t in range(QT):
                    pool.wait_ge(rope_ready, QT * b + t + 1)
                    pool.sem_inc(carried, 1)
                    pool.tensor_copy(stk[u][:, t, 0:HEADS, 2 * HD:3 * HD].bitcast(F32R), stk[u][:, t, 0:HEADS, 0:HD])
                    pool.tensor_copy(stk[u][:, t, HEADS:, HD:2 * HD].bitcast(F32R), stk[u][:, t, HEADS:, 0:HD]
                                     ).then_inc(dup_ready, 1)

            deviations(0, 0)
            deviations(1, 1)
            duplicates(0, 0)
            with pool.Fori(0, BODIES) as i:
                for u in range(2):
                    duplicates(2 * i + u + 1, 1 - u)
                    deviations(2 * i + u + 2, u)
            duplicates(B - 1, 1)

        @block.tensor
        def _(pe):
            pe.wait_ge(consts_in, 16 * N_CONST)
            for j in range(4):
                pe.transpose(vbank[j][:, 0:P], w_in[:, j, 0, 0:P], ident[:])
                pe.transpose(vbank[j][:, P:D], w_in[0:DB, j, 1, 0:P], ident[0:DB, 0:DB])
                pe.transpose(vbank[j][0:DB, D:D + P], w_in[:, j, 0, P:D], ident[:])
                pe.transpose(vbank[j][0:DB, D + P:2 * D], w_in[0:DB, j, 1, P:D], ident[0:DB, 0:DB]).then_inc(wT_mm, 1)
            pe.wait_ge(wT_ready, 12)
            pe.wait_ge(init_done, N_INIT)
            v = Ring(vbank, VN)
            s = Ring(sbank, SN)
            at = {}

            def layer_in(b, u):
                pe.wait_ge(xn_ready, b + 1)
                ta = s.take()
                pe.wait_ge(s_freed, s.free())
                for t in range(QT):
                    mm = pe.transpose(ta[:, t * P:t * P + P], xn[u][:, t, 0:P], ident[:])
                mm.then_inc(s_filled, 1)
                tb = s.take()
                pe.wait_ge(s_freed, s.free())
                pe.sem_inc(carried, 1)
                for t in range(QT):
                    mm = pe.transpose(tb[0:DB, t * P:t * P + P], xn[u][:, t, P:D], ident[:])
                mm.then_inc(s_filled, 1)

            def queries_keys(u, t):
                o = v.take()
                pe.wait_ge(v_freed, v.free())
                pe.matmul(o[:, 0:2 * D], xTa[u][:, t * P:t * P + P], wa[:, 0:2, :], start=True, stop=False)
                pe.matmul(o[:, 0:2 * D], xTb[u][:, t * P:t * P + P], wb[:, 0:2, :], start=False, stop=True
                          ).then_inc(v_filled, 1)

            def values(u, ts):
                o = s.take()
                pe.wait_ge(s_freed, s.free())
                for t in ts:
                    c = (t % 2) * D
                    pe.matmul(o[:, c:c + D], xTa[u][:, t * P:t * P + P], wa[:, 2, :], start=True, stop=False)
                    mm = pe.matmul(o[:, c:c + D], xTb[u][:, t * P:t * P + P], wb[:, 2, :], start=False, stop=True)
                mm.then_inc(s_filled, 1)

            def stack_T(u, first, p):
                o = s.take()
                pe.wait_ge(s_freed, s.free())
                for t in range(QT):
                    mm = pe.transpose(o[:, t * P:t * P + P].bitcast(F32R),
                                      stk[u][:, t, first + 2 * p:first + 2 * p + 2, :].bitcast(F32R), identr[:].bitcast(F32R))
                mm.then_inc(s_filled, 1)

            def pairs_in(b, u, pairs):
                if pairs[0] == 0:
                    pe.wait_ge(dup_ready, QT * (b + 1))
                for p in pairs:
                    stack_T(u, 0, p)
                    stack_T(u, HEADS, p)
                    at["qk", p] = s.n
                    if p > 0:
                        pe.wait_ge(s_freed, s.read(at["qk", p - 1]))
                        maxima(u, LAST_MAXES[p - 1])

            def maxima(u, tiles):
                for t, h0, n, keys in tiles:
                    o = v.take()
                    pe.wait_ge(v_freed, v.free())
                    ov = o[:, 0:n * keys].rearrange("p (n k) -> p n k", n=n)
                    diag = min(P, keys - t * P)
                    pe.matmul(ov[:, :, t * P:t * P + diag], identb[:],
                              mask[:, 0:1, 0:diag].to_broadcast([P, n, diag]), start=True, stop=True)
                    for j in range(n):
                        h = h0 + 2 * j
                        r = STK * (h % 2)
                        mm = pe.matmul(ov[:, j, :], qT[u][r:r + MROW, h // 2, t * P:t * P + P].bitcast(F32R),
                                       kT[u][r:r + MROW, h // 2, 0:keys].bitcast(F32R), start=False, stop=True,
                                       skip_group_check=True)
                    mm.then_inc(v_filled, 1)

            def q_T_again(b, u):
                pe.wait_ge(max_ready, b + 1)
                for p in range(PAIRS):
                    stack_T(u, 0, p)
                at["q2"] = s.n

            def scores(u, g):
                if g == 0:
                    pe.wait_ge(s_freed, s.read(at["q2"]))
                for j in range(2):
                    r = STK * j
                    pairs = (g * GROUP // 2, g * GROUP // 2 + 1)
                    for pr in pairs:
                        kh = kT[u][r:r + STK, pr, :].bitcast(F32R)
                        qh = qT[u][r:r + STK, pr, :].bitcast(F32R)
                        o = s.take()
                        pe.wait_ge(s_freed, s.free())
                        pe.matmul(o[:, 0:P], identb[:], mask[:, 1, :], start=True, stop=True, skip_group_check=True)
                        pe.matmul(o[:, LE:AC], identb[:], mask[:, 1, 0:LASTE], start=False, stop=True,
                                  skip_group_check=True)
                        pe.matmul(o[:, 0:LE], kh[:, 0:P], qh[:, 0:LE], start=False, stop=True, skip_group_check=True)
                        pe.matmul(o[:, LE:AC], kh[:, 2 * P:LP], qh[:, 2 * P:LE], start=False, stop=True,
                                  skip_group_check=True).then_inc(s_filled, 1)
                    o = s.take()
                    pe.wait_ge(s_freed, s.free())
                    ov = o[:, 0:2 * BC].rearrange("p (n k) -> p n k", n=2)
                    pe.matmul(ov[:, :, 0:P], identb[:], mask[:, 1:2, :].to_broadcast([P, 2, P]), start=True, stop=True,
                              skip_group_check=True)
                    for n, pr in enumerate(pairs):
                        mm = pe.matmul(ov[:, n, :], kT[u][r:r + STK, pr, P:2 * P].bitcast(F32R),
                                       qT[u][r:r + STK, pr, P:LE].bitcast(F32R), start=False, stop=True,
                                       skip_group_check=True)
                    mm.then_inc(s_filled, 1)
                at["probs", g] = s.n

            def attend(u, g):
                pe.wait_ge(s_freed, s.read(at["probs", g]))
                pb = probs[(NG * u + g) % 2]
                o = v.take()
                pe.wait_ge(v_freed, v.free())
                for kt, c0, src in ((0, 0, pb[:, :, 0:LE]), (1, P, pb[:, :, AC:PTC]), (2, 2 * P, pb[:, :, LE:AC])):
                    for j in range(GROUP):
                        mm = pe.matmul(o[32 * j:32 * j + 32, c0:LE], vaug[u][:, kt, g * GROUP + j, :], src[:, j, :],
                                       start=(kt == 0), stop=(kt == 2))
                mm.then_inc(v_filled, 1)
                at["oT"] = v.n

            def out_T(u):
                pe.wait_ge(v_freed, v.read(at["oT"]))
                for t in range(QT):
                    o = v.take()
                    pe.wait_ge(v_freed, v.free())
                    for g in range(NG):
                        mm = pe.transpose(o[:, g * P:g * P + P], oT[u][:, g, t * P:t * P + P], ident[:])
                    mm.then_inc(v_filled, 1)
                at["on"] = v.n

            def norm_T(u):
                pe.wait_ge(v_freed, v.read(at["on"]))
                ta = s.take()
                pe.wait_ge(s_freed, s.free())
                for t in range(QT):
                    mm = pe.transpose(ta[:, t * P:t * P + P], on[u][:, t, 0:P], ident[:])
                mm.then_inc(s_filled, 1)
                tb = s.take()
                pe.wait_ge(s_freed, s.free())
                pe.sem_inc(carried, 1)
                for t in range(QT):
                    mm = pe.transpose(tb[0:DB, t * P:t * P + P], on[u][:, t, P:D], ident[:])
                mm.then_inc(s_filled, 1)
                at["onT"] = s.n

            def project(u):
                pe.wait_ge(s_freed, s.read(at["onT"]))
                for t in range(QT):
                    o = v.take()
                    pe.wait_ge(v_freed, v.free())
                    pe.matmul(o[:, 0:D], onTa[u][:, t * P:t * P + P], wa[:, 3, :], start=True, stop=False)
                    pe.matmul(o[:, 0:D], onTb[u][:, t * P:t * P + P], wb[:, 3, :], start=False, stop=True
                              ).then_inc(v_filled, 1)

            def period(b, u, prepare=True, transpose=True):
                w = 1 - u
                maxima(u, MIDDLE_MAXES[:3])
                if prepare:
                    pe.wait_ge(s_freed, s.read())
                    values(w, (0, 1))
                maxima(u, MIDDLE_MAXES[3:])
                if prepare:
                    values(w, (2,))
                    queries_keys(w, 0)
                q_T_again(b, u)
                if prepare:
                    queries_keys(w, 1)
                scores(u, 0)
                if prepare:
                    queries_keys(w, 2)
                scores(u, 1)
                attend(u, 0)
                scores(u, 2)
                attend(u, 1)
                if prepare:
                    pairs_in(b + 1, w, [0])
                attend(u, 2)
                if prepare:
                    pairs_in(b + 1, w, [1, 2])
                out_T(u)
                if prepare:
                    pairs_in(b + 1, w, [3, 4])
                norm_T(u)
                if prepare:
                    pairs_in(b + 1, w, [5])
                if transpose:
                    layer_in(b + 2, u)
                if prepare:
                    pe.wait_ge(s_freed, s.read(at["qk", PAIRS - 1]))
                    maxima(w, LAST_MAXES[-1])
                    maxima(w, FIRST_MAXES)
                project(u)

            layer_in(0, 0)
            pe.wait_ge(s_freed, s.read())
            for t in range(QT):
                queries_keys(0, t)
            values(0, (0, 1))
            values(0, (2,))
            pairs_in(0, 0, range(PAIRS))
            layer_in(1, 1)
            pe.wait_ge(s_freed, s.read(at["qk", PAIRS - 1]))
            maxima(0, LAST_MAXES[-1])
            maxima(0, FIRST_MAXES)
            assert v.n == V_FIRST
            with pe.Fori(0, BODIES) as i:
                v.enter(i)
                s.enter(i)
                period(2 * i, 0)
                period(2 * i + 1, 1)
            v.leave(BODIES)
            s.leave(BODIES)
            period(B - 2, 0, transpose=False)
            period(B - 1, 1, prepare=False, transpose=False)

        @block.scalar
        def _(act):
            act.sem_inc(s_freed, RING)
            act.wait_ge(consts_in, 16 * N_CONST)
            act.copy(identb[:], ident[:]).then_inc(wT_ready, 1)
            act.copy(identr[:].bitcast(F32R), ident[:]).then_inc(wT_ready, 1)
            act.copy(mask[:], maskf[:]).then_inc(wT_ready, 1)
            s = Ring(sbank, SN)

            def two_parts(ta, tb):
                for dst, rows in ((ta, P), (tb, DB)):
                    o = s.take()
                    act.wait_ge(s_filled, s.filled())
                    act.copy(dst[0:rows, :], o[0:rows, 0:LP]).then_inc(s_freed, 1)

            def values(u, t0, n):
                o = s.take()
                act.wait_ge(s_filled, s.filled())
                act.copy(vaug[u][:, t0:t0 + n, :, 0:HD],
                         o[:, 0:n * D].rearrange("p (t h d) -> p t h d", t=n, h=HEADS)).then_inc(s_freed, 1)

            def stacks(pairs, *dsts):
                for p in pairs:
                    for dst in dsts:
                        o = s.take()
                        act.wait_ge(s_filled, s.filled())
                        act.copy(dst[:, p, :].bitcast(F32R), o[:, 0:LP].bitcast(F32R)).then_inc(s_freed, 1)

            def exps(u, g):
                pb = probs[(NG * u + g) % 2]
                for j in range(2):
                    for n in range(2):
                        o = s.take()
                        act.wait_ge(s_filled, s.filled())
                        act.activation(pb[:, 2 * n + j, 0:AC], o[:, 0:AC], ACT.Exp).then_inc(s_freed, 1)
                    o = s.take()
                    act.wait_ge(s_filled, s.filled())
                    act.activation(pb[:, j:j + 3:2, AC:PTC],
                                   o[:, 0:2 * BC].rearrange("p (n k) -> p n k", n=2), ACT.Exp).then_inc(s_freed, 1)

            def period(u, prepare=True, transpose=True):
                w = 1 - u
                if prepare:
                    values(w, 0, 2)
                    values(w, 2, 1)
                stacks(range(PAIRS), qT[u])
                exps(u, 0)
                exps(u, 1)
                exps(u, 2)
                if prepare:
                    stacks(range(0, 5), qT[w], kT[w])
                two_parts(onTa[u], onTb[u])
                if prepare:
                    stacks([5], qT[w], kT[w])
                if transpose:
                    two_parts(xTa[u], xTb[u])

            two_parts(xTa[0], xTb[0])
            values(0, 0, 2)
            values(0, 2, 1)
            stacks(range(PAIRS), qT[0], kT[0])
            two_parts(xTa[1], xTb[1])
            with act.Fori(0, BODIES) as i:
                s.enter(i)
                period(0)
                period(1)
            s.leave(BODIES)
            period(0, transpose=False)
            period(1, prepare=False, transpose=False)

        @block.vector
        def _(dve):
            dve.sem_inc(v_freed, RING)
            for u in range(2):
                dve.sem_inc(h2_stored[u], 32)
            for u in range(2):
                dve.memset(hb[u][:, 2, :], 0.0).then_inc(init_done, 1)
                dve.memset(xTb[u][DB:DB + 1, :], 1.0).then_inc(init_done, 1)
                dve.memset(onTb[u][DB:DB + 1, :], 1.0).then_inc(init_done, 1)
                dve.memset(stk[u][:, :, :, MROW:STK], 0.0).then_inc(init_done, 1)
                dve.memset(vaug[u][:, :, :, HD:32], 0.0).then_inc(init_done, 1)
                dve.memset(oT[u][:, :, LE:LP], 1.0).then_inc(init_done, 1)
            dve.wait_ge(init_done, 13)
            for u in range(2):
                dve.memset(stk[u][:, :, HEADS:, MROW:MROW + 2], 1.0).then_inc(init_done, 1)
                dve.memset(vaug[u][:, :, :, HD:HD + 1], 1.0).then_inc(init_done, 1)
            dve.wait_ge(consts_in, 16 * N_CONST)
            scale = float(HD) ** -0.5
            dve.tensor_scalar(wb[DB:DB + 1, 0, :], wb[DB:DB + 1, 0, :], scale, None, ALU.mult).then_inc(wT_ready, 1)
            for j in range(4):
                dve.wait_ge(wT_mm, j + 1)
                by = scale if j == 0 else 1.0
                dve.tensor_scalar(wa[:, j, :], vbank[j][:, 0:D], by, None, ALU.mult).then_inc(wT_ready, 1)
                dve.tensor_scalar(wb[0:DB, j, :], vbank[j][0:DB, D:2 * D], by, None, ALU.mult).then_inc(wT_ready, 1)
            dve.wait_ge(init_done, N_INIT)
            v = Ring(vbank, VN)
            chained = Count(VSTEPS)

            def link(ins):
                chained.n += 1
                ins.then_inc(vec_step, 1)
                dve.wait_ge(vec_step, chained.value())

            def layernorm(u, loads):
                dve.wait_ge(h_in[u], 32 * loads)
                for t in range(QT):
                    ins = dve.bn_stats(stats[u][:, t, :], hb[u][:, t, :])
                link(ins)
                dve.sem_inc(carried, 1)
                for t in range(QT):
                    ins = dve.bn_aggr(mv[u][:, t, :], stats[u][:, t, :])
                link(ins)
                dve.tensor_scalar(var[u][:], mv[u][:, :, 1], LN_EPS, None, ALU.add).then_inc(var_ready, 1)

            def normalize(b, u):
                dve.wait_ge(rstd_ready, b + 1)
                for t in range(QT):
                    ins = dve.tensor_scalar(xn[u][:, t, :], hb[u][:, t, :], mv[u][:, t, 0:1], rstd[u][:, t:t + 1],
                                            ALU.subtract, ALU.mult)
                ins.then_inc(xn_ready, 1)

            def rotate(u):
                for t in range(QT):
                    rot = rots[(u * QT + t) % 2]
                    o = v.take()
                    dve.wait_ge(v_filled, v.filled())
                    qk = o[:, 0:2 * D].rearrange("p (h d) -> p h d", d=HD)

                    def table(c0, n):
                        return rope[:, t:t + 1, c0:c0 + n].to_broadcast([P, 2 * HEADS, n])

                    dve.tensor_tensor(rot[:, 0], qk, table(0, HD), ALU.mult)
                    dve.tensor_tensor(rot[:, 1, :, 0:HD // 2], qk[:, :, HD // 2:HD], table(HD, HD // 2), ALU.mult)
                    dve.tensor_tensor(rot[:, 1, :, HD // 2:HD], qk[:, :, 0:HD // 2], table(HD + HD // 2, HD // 2),
                                      ALU.mult).then_inc(v_freed, 1)
                    dve.wait_ge(v_freed, v.read())
                    link(dve.tensor_tensor(rot[:, 0], rot[:, 0], rot[:, 1], ALU.add))
                    link(dve.tensor_copy(stk[u][:, t, :, 0:HD].bitcast(F32R), rot[:, 0]))
                    dve.tensor_tensor(stk[u][:, t, 0:HEADS, HD:2 * HD].bitcast(F32R), rot[:, 0, 0:HEADS],
                                      stk[u][:, t, 0:HEADS, 0:HD], ALU.subtract)
                    dve.tensor_tensor(stk[u][:, t, HEADS:, 2 * HD:3 * HD].bitcast(F32R), rot[:, 0, HEADS:],
                                      stk[u][:, t, HEADS:, 0:HD], ALU.subtract).then_inc(rope_ready, 1)

            def maxima(u, tiles):
                for t, h0, n, keys in tiles:
                    o = v.take()
                    dve.wait_ge(v_filled, v.filled())
                    dve.tensor_reduce(mx[u][:, t, h0:h0 + 2 * n - 1:2], o[:, 0:n * keys].rearrange("p (n k) -> p n k", n=n),
                                      AX.X, ALU.max).then_inc(v_freed, 1)

            def put_maxima(u):
                dve.wait_ge(v_freed, v.read())
                hi, lo = stk[u][:, :, 0:HEADS, MROW], stk[u][:, :, 0:HEADS, MROW + 1]
                link(dve.tensor_scalar(hi.bitcast(F32R), mx[u][:], -1.0, None, ALU.mult))
                dve.scalar_tensor_tensor(lo.bitcast(F32R), mx[u][:], -1.0, hi, ALU.mult, ALU.subtract
                                         ).then_inc(max_ready, 1)

            def attended(u, g):
                o = v.take()
                dve.wait_ge(v_filled, v.filled())
                dve.tensor_copy(oT[u][:, g, 0:LE], o[:, 0:LE]).then_inc(v_freed, 1)

            def divide(u):
                for t in range(QT):
                    o = v.take()
                    dve.wait_ge(v_filled, v.filled())
                    ov = o[:, 0:NG * P].rearrange("p (h d) -> p h d", d=32)
                    link(dve.reciprocal(rden[u][:, t, :], ov[:, :, HD]))
                    dve.tensor_tensor(on[u][:, t, :].rearrange("p (h d) -> p h d", d=HD), ov[:, :, 0:HD],
                                      rden[u][:, t, :].unsqueeze(2).to_broadcast([P, HEADS, HD]), ALU.mult
                                      ).then_inc(v_freed, 1)

            def residual(u, batch2):
                dve.wait_ge(h2_stored[u], 32 * (batch2 + 1))
                dve.wait_ge(hr_in[u], 32 * (batch2 + 1))
                for t in range(QT):
                    r = P if t < 2 else LAST
                    o = v.take()
                    dve.wait_ge(v_filled, v.filled())
                    dve.tensor_tensor(h2[u][0:r, t, :], o[0:r, 0:D], hr[u][0:r, t, :], ALU.add).then_inc(v_freed, 1)

            def period(b, u, batch2, prepare=True, transpose=True):
                w = 1 - u
                maxima(u, MIDDLE_MAXES)
                put_maxima(u)
                if prepare:
                    rotate(w)
                if transpose:
                    layernorm(u, batch2 + 2)
                attended(u, 0)
                attended(u, 1)
                if transpose:
                    normalize(b + 2, u)
                attended(u, 2)
                if prepare:
                    maxima(w, LAST_MAXES[0])
                    maxima(w, LAST_MAXES[1])
                divide(u)
                if prepare:
                    maxima(w, LAST_MAXES[2])
                if prepare:
                    for p in range(3, PAIRS):
                        maxima(w, LAST_MAXES[p])
                    maxima(w, FIRST_MAXES)
                residual(u, batch2)

            layernorm(0, 1)
            layernorm(1, 1)
            normalize(0, 0)
            normalize(1, 1)
            rotate(0)
            for p in range(PAIRS):
                maxima(0, LAST_MAXES[p])
            maxima(0, FIRST_MAXES)
            with dve.Fori(0, BODIES) as i:
                v.enter(i)
                chained.enter(i)
                period(2 * i, 0, i)
                period(2 * i + 1, 1, i)
            v.leave(BODIES)
            chained.leave(BODIES)
            period(B - 2, 0, BODIES, transpose=False)
            period(B - 1, 1, BODIES, prepare=False, transpose=False)


HALF = N_EXP // 2
EC = B * SLOTS_PER
EC1 = EC + 1


def dispatch_phase(nc, xsTa, xsTb, h2_d, phi, ln_g, ln_b, c_ident, e2_d):
    with ExitStack() as ctx:
        a = Pool_(nc, ctx, "di")
        ident = a.sb("ident", [P, P])
        phiTa = a.sb("phiTa", [P, S])
        phiTb = a.sb("phiTb", [DB, S])
        gTa = a.sb("gTa", [P, N_EXP])
        gTb = a.sb("gTb", [P, HALF])
        gb_in = a.sb("gb_in", [N_EXP, 2, 2, D])
        half = a.sb("half", [P, SLOTS_PER])
        pn = a.sb("pn", [P, 2, SLOTS_PER])
        hb = [a.sb(f"hb{u}", [P, QT, D]) for u in range(2)]
        stats = a.sb("stats", [P, ST, 6])
        mv = [a.sb(f"mv{u}", [P, QT, 2]) for u in range(2)]
        var = [a.sb(f"var{u}", [P, QT]) for u in range(2)]
        rstd = [a.sb(f"rstd{u}", [P, QT]) for u in range(2)]
        xn = [a.sb(f"xn{u}", [P, QT, D + 1]) for u in range(2)]
        xTa = a.sb("xTa", [P, LP])
        xTb = a.sb("xTb", [DB, LP])
        lg = [a.sb(f"lg{u}", [P, QT, S]) for u in range(2)]
        nmt = [a.sb(f"nmt{u}", [P, QT]) for u in range(2)]
        nms = [a.sb(f"nms{u}", [P, ST]) for u in range(2)]
        e2 = a.sb("e2", [P, QT, S])
        e2T = a.sb("e2T", [P, ST, L])
        e1T = a.sb("e1T", [P, ST, L])
        e1 = a.sb("e1", [P, QT, S])
        xs = a.sb("xs", [P, ST, D + 1])
        smv = a.sb("smv", [P, ST, 2])
        ssq = a.sb("ssq", [P, ST])
        svar = a.sb("svar", [P, ST])
        srstd = a.sb("srstd", [P, ST])
        xsn = a.sb("xsn", [P, ST, D])
        phi_in = e1[:, 0:2, 0:ST * D // 2]
        sq = e2[:, 0:2, :]
        vbank = [a.bank(f"vbank{i}") for i in range(RING)]
        sbank = [a.bank(f"sbank{i}") for i in range(RING)]

        consts_in = a.sem("consts_in")
        init_done = a.sem("init_done")
        setup_mm = a.sem("setup_mm")
        setup_step = a.sem("setup_step")
        pn_ready = a.sem("pn_ready")
        v_filled, v_freed = a.sem("v_filled"), a.sem("v_freed")
        s_filled, s_freed = a.sem("s_filled"), a.sem("s_freed")
        vec_step = a.sem("vec_step")
        carried = a.sem("carried")
        h_in = [a.sem(f"h_in{u}") for u in range(2)]
        var_ready = a.sem("var_ready")
        rstd_ready = a.sem("rstd_ready")
        xn_ready = a.sem("xn_ready")
        token_max = a.sem("token_max")
        slot_max = a.sem("slot_max")
        e2_ready = a.sem("e2_ready")
        e2_stored = a.sem("e2_stored")
        svar_ready = a.sem("svar_ready")
        srstd_ready = a.sem("srstd_ready")
        xsn_ready = a.sem("xsn_ready")
        block = ctx.enter_context(nc.Block())

        N_CONST = 7
        N_INIT = 5
        BODIES = (B - 2) // 2
        VN, SN = 28, 48
        V_FIRST, S_FIRST = 12, 30
        HEAD = [("T", t) for t in range(2)]
        MIXED = [("T", 2), ("T", 3), ("L", 0), ("T", 4), ("L", 1), ("T", 5), ("L", 2), ("T", 6), ("L", 3), ("T", 7), ("L", 4), ("L", 5)]
        ALONE = [("T", t) for t in range(2, ST)]
        S_PERIOD = SN // 2
        L_IN = len(HEAD) + len(MIXED)
        VSTEPS = 10

        phs = [phi_in[:, t // 4, (t % 4) * D:(t % 4) * D + D] for t in range(ST)]

        @block.sync
        def _(sp):
            sp.wait_ge(init_done, N_INIT)
            h2d = h2_d.rearrange("(i u) l d -> u i l d", u=2)
            e2d = e2_d.rearrange("(i u) p c -> u i p c", u=2)

            def load(u, b2):
                sp.dma_start(hb[u][:, 0:2, :], h2d[u, b2, 0:2 * P].rearrange("(t p) d -> p t d", p=P)).then_inc(h_in[u], 16)
                sp.dma_start(hb[u][0:LAST, 2, :], h2d[u, b2, 2 * P:L]).then_inc(h_in[u], 16)

            def period(b, u, b2, load_b2, v_before):
                if load_b2 is not None:
                    sp.wait_ge(xn_ready, b + 2)
                    load(1 - u, load_b2)
                sp.wait_ge(v_freed, v_before + RING + ST + (2 if load_b2 is not None else 0))
                sp.dma_start(e2d[u, b2], e2T[:].rearrange("p t c -> p (t c)")).then_inc(e2_stored, 16)

            load(0, 0)
            load(1, 0)
            sp.dma_start(ident[:], c_ident).then_inc(consts_in, 16)
            phv = phi.rearrange("n p d -> (n p) d").rearrange("(h t p) d -> h p t d", p=P, h=2)
            for k in range(2):
                sp.dma_start(phi_in[:, k, :].rearrange("p (t d) -> p t d", d=D), phv[k]).then_inc(consts_in, 16)
            sp.dma_start(gb_in[:, 0, 0, :], ln_g).then_inc(consts_in, 16)
            sp.dma_start(gb_in[:, 1, 0, :], ln_b).then_inc(consts_in, 16)
            for k, w in enumerate((ln_g, ln_b)):
                sp.dma_start(gb_in[0:HALF, k, 1, :], w[HALF:, :]).then_inc(consts_in, 16)
            sp.wait_ge(xn_ready, 1)
            load(0, 1)
            period(0, 0, 0, 1, 2)
            with sp.Fori(0, BODIES) as i:
                period(2 * i + 1, 1, i, (i + 2) % (B // 2), V_FIRST + VN * i)
                period(2 * i + 2, 0, i + 1, (i + 2) % (B // 2), V_FIRST + VN // 2 + VN * i)
            period(B - 1, 1, B // 2 - 1, None, V_FIRST + VN * BODIES)
            sp.wait_ge(e2_stored, 16 * (1 + B))
            for u in range(2):
                sp.wait_ge(h_in[u], 32 * (1 + B // 2))

        @block.gpsimd
        def _(pool):
            pool.memset(half[:], -0.5).then_inc(init_done, 1)
            pool.wait_ge(init_done, N_INIT)
            def of_tokens(b, u):
                pool.wait_ge(var_ready, b + 1)
                pool.tensor_tensor(rstd[u][:], var[u][:], half[:, 0:QT], ALU.pow).then_inc(rstd_ready, 1)

            def of_slots(b):
                pool.wait_ge(svar_ready, b + 1)
                pool.tensor_tensor(srstd[:], svar[:], half[:, 0:ST], ALU.pow).then_inc(srstd_ready, 1)

            of_tokens(0, 0)
            of_tokens(1, 1)
            pool.wait_ge(pn_ready, 1)
            for k, rows in enumerate((P, DB)):
                pool.tensor_tensor(pn[0:rows, k, :], pn[0:rows, k, :], half[0:rows, :], ALU.pow).then_inc(pn_ready, 1)
            of_tokens(2, 0)
            with pool.Fori(0, BODIES) as i:
                for u in range(2):
                    of_slots(2 * i + u)
                    of_tokens(2 * i + u + 3, 1 - u)
            of_slots(B - 2)
            of_slots(B - 1)

        @block.tensor
        def _(pe):
            pe.wait_ge(consts_in, 16 * N_CONST)
            for t in range(ST):
                pe.transpose(vbank[t // 4][:, (t % 4) * P:(t % 4) * P + P], phs[t][:, 0:P], ident[:])
                pe.transpose(vbank[2 + t // 4][0:DB, (t % 4) * P:(t % 4) * P + P], phs[t][:, P:D], ident[:]
                             ).then_inc(setup_mm, 1)
            for k in range(2):
                pe.transpose(sbank[k][:, 0:N_EXP], gb_in[:, k, 0, 0:P], ident[0:N_EXP, 0:N_EXP])
                pe.transpose(sbank[k][0:DB, P:P + HALF], gb_in[0:HALF, k, 0, P:D], ident[0:HALF, 0:HALF])
                pe.transpose(sbank[k][:, 2 * P:2 * P + HALF], gb_in[0:HALF, k, 1, D - P:D], ident[0:HALF, 0:HALF]
                             ).then_inc(setup_mm, 1)
            pe.wait_ge(setup_step, 18)
            pe.wait_ge(init_done, N_INIT)
            v = Ring(vbank, VN)
            s = Ring(sbank, SN)

            def tokens_T(b, u):
                pe.wait_ge(xn_ready, b + 1)
                oa = v.take()
                ob = v.take()
                pe.wait_ge(v_freed, v.free())
                for t in range(QT):
                    mm = pe.transpose(oa[:, t * P:t * P + P], xn[u][:, t, 0:P], ident[:])
                mm.then_inc(v_filled, 1)
                for t in range(QT):
                    mm = pe.transpose(ob[0:DB, t * P:t * P + P], xn[u][:, t, P:D], ident[:])
                mm.then_inc(v_filled, 1)

            def rows_T(o, src, t0):
                for t in range(QT):
                    r = P if t < 2 else LAST
                    mm = pe.transpose(o[:, t * P:t * P + r], src[0:r, t, t0:t0 + P], ident[0:r, 0:r])
                return mm

            def logits(u, pieces):
                for kind, n in pieces:
                    o = s.take()
                    if kind == "T":
                        pe.wait_ge(s_freed, s.free())
                        rows_T(o, lg[u], n * P).then_inc(s_filled, 1)
                    else:
                        if n == 0:
                            pe.wait_ge(v_freed, v.read())
                        t, k = n // 2, n % 2
                        pe.wait_ge(s_freed, s.free())
                        pe.matmul(o[:], xTa[:, t * P:t * P + P], phiTa[:, 512 * k:512 * k + 512], start=True, stop=False)
                        pe.matmul(o[:], xTb[:, t * P:t * P + P], phiTb[:, 512 * k:512 * k + 512], start=False, stop=True
                                  ).then_inc(s_filled, 1)

            def e2_T(b):
                pe.wait_ge(e2_ready, QT * (b + 1))
                for t in range(ST):
                    o = v.take()
                    pe.wait_ge(v_freed, v.free())
                    rows_T(o, e2, t * P).then_inc(v_filled, 1)

            def e1_back(e1T_read):
                pe.wait_ge(s_freed, e1T_read)
                for k in range(2):
                    for t in range(QT):
                        r = P if t < 2 else LAST
                        o = s.take()
                        pe.wait_ge(s_freed, s.free())
                        for j in range(4):
                            mm = pe.transpose(o[0:r, j * P:j * P + P], e1T[:, 4 * k + j, t * P:t * P + r], ident[:])
                        mm.then_inc(s_filled, 1)

            def slot_inputs(u):
                e1_half = s.read(s.n - QT), s.read()
                for k in range(ST // 2):
                    if k % 2 == 0:
                        pe.wait_ge(s_freed, e1_half[k // 2])
                    o = s.take()
                    pe.wait_ge(s_freed, s.free())
                    for j in range(2):
                        st = 2 * k + j
                        for t in range(QT):
                            r = P if t < 2 else LAST
                            mm = pe.matmul(o[:, j * (D + 1):(j + 1) * (D + 1)], e1[0:r, t, st * P:st * P + P],
                                           xn[u][0:r, t, :], start=(t == 0), stop=(t == QT - 1))
                    mm.then_inc(s_filled, 1)

            def slots_T(b):
                for k in range(2):
                    pe.wait_ge(xsn_ready, 2 * b + k + 1)
                    oa = v.take()
                    ob = v.take()
                    pe.wait_ge(v_freed, v.free())
                    for j in range(4):
                        mm = pe.transpose(oa[:, j * P:j * P + P], xsn[:, 4 * k + j, 0:P], ident[:])
                    mm.then_inc(v_filled, 1)
                    for j in range(4):
                        if k == 0:
                            mm = pe.transpose(ob[0:DB, j * P:j * P + P], xsn[:, j, P:D], ident[:])
                        else:
                            mm = pe.transpose(ob[:, j * P:j * P + P], xsn[:, 4 + j, D - P:D], ident[:])
                    mm.then_inc(v_filled, 1)

            def period(b, u, first=False, last=False):
                pe.wait_ge(s_freed, s.read() if first else s.value(RING + L_IN - S_PERIOD))
                logits(u, HEAD)
                if not last:
                    tokens_T(b + 1, 1 - u)
                logits(u, ALONE if last else MIXED)
                e1T_read = s.read()
                e2_T(b)
                if not first:
                    slots_T(b - 1)
                e1_back(e1T_read)
                slot_inputs(u)

            tokens_T(0, 0)
            logits(1, [("L", n) for n in range(2 * QT)])
            period(0, 0, first=True)
            assert (v.n, s.n) == (V_FIRST, S_FIRST)
            with pe.Fori(0, BODIES) as i:
                v.enter(i)
                s.enter(i)
                period(2 * i + 1, 1)
                period(2 * i + 2, 0)
            v.leave(BODIES)
            s.leave(BODIES)
            period(B - 1, 1, last=True)
            slots_T(B - 1)

        @block.scalar
        def _(act):
            act.sem_inc(s_freed, RING)
            s = Ring(sbank, SN)

            def logits(b, u, pieces):
                for kind, n in pieces:
                    o = s.take()
                    if kind == "T":
                        act.wait_ge(slot_max, ST * b + n + 1)
                        act.activation(e1T[:, n, :], o[:, 0:L], ACT.Exp, bias=nms[u][:, n:n + 1]).then_inc(s_freed, 1)
                    else:
                        t, k = n // 2, n % 2
                        act.wait_ge(s_filled, s.filled())
                        act.copy(lg[1 - u][:, t, 512 * k:512 * k + 512], o[:]).then_inc(s_freed, 1)

            def over_slots(b, u, lg_ready):
                act.wait_ge(s_freed, lg_ready)
                for t in range(QT):
                    act.wait_ge(token_max, QT * b + t + 1)
                    act.activation(e2[:, t, :], lg[u][:, t, :], ACT.Exp, bias=nmt[u][:, t:t + 1]).then_inc(e2_ready, 1)

            def e1_back():
                for k in range(2):
                    for t in range(QT):
                        r = P if t < 2 else LAST
                        o = s.take()
                        act.wait_ge(s_filled, s.filled())
                        act.copy(e1[0:r, t, 512 * k:512 * k + 512], o[0:r, :]).then_inc(s_freed, 1)

            def slot_inputs():
                for k in range(ST // 2):
                    o = s.take()
                    act.wait_ge(s_filled, s.filled())
                    act.copy(xs[:, 2 * k:2 * k + 2, :], o[:, 0:2 * (D + 1)].rearrange("p (t d) -> p t d", t=2)
                             ).then_inc(s_freed, 1)

            def period(b, u, last=False):
                logits(b, u, HEAD)
                logits(b, u, ALONE if last else MIXED)
                lg_ready = s.read()
                e1_back()
                if not last:
                    over_slots(b + 1, 1 - u, lg_ready)
                slot_inputs()

            logits(-1, 1, [("L", n) for n in range(2 * QT)])
            over_slots(0, 0, s.read())
            period(0, 0)
            with act.Fori(0, BODIES) as i:
                s.enter(i)
                period(2 * i + 1, 1)
                period(2 * i + 2, 0)
            s.leave(BODIES)
            period(B - 1, 1, last=True)

        @block.vector
        def _(dve):
            dve.sem_inc(v_freed, RING)
            dve.sem_inc(e2_stored, 16)
            for u in range(2):
                dve.memset(hb[u][:, 2, :], 0.0).then_inc(init_done, 1)
                dve.memset(xn[u][:, :, D:D + 1], 1.0).then_inc(init_done, 1)
            v = Ring(vbank, VN)
            s = Ring(sbank, SN)
            chained = Count(VSTEPS)

            def link(ins):
                chained.n += 1
                ins.then_inc(vec_step, 1)
                dve.wait_ge(vec_step, chained.value())

            def layernorm(u, loads):
                dve.wait_ge(h_in[u], 32 * loads)
                for t in range(QT):
                    ins = dve.bn_stats(stats[:, t, :], hb[u][:, t, :])
                link(ins)
                dve.sem_inc(carried, 1)
                for t in range(QT):
                    ins = dve.bn_aggr(mv[u][:, t, :], stats[:, t, :])
                link(ins)
                dve.tensor_scalar(var[u][:], mv[u][:, :, 1], LN_EPS, None, ALU.add).then_inc(var_ready, 1)

            def normalize(b, u):
                dve.wait_ge(rstd_ready, b + 1)
                for t in range(QT):
                    ins = dve.tensor_scalar(xn[u][:, t, 0:D], hb[u][:, t, :], mv[u][:, t, 0:1], rstd[u][:, t:t + 1],
                                            ALU.subtract, ALU.mult)
                ins.then_inc(xn_ready, 1)

            def tokens_T():
                for dst, rows in ((xTa, P), (xTb, DB)):
                    o = v.take()
                    dve.wait_ge(v_filled, v.filled())
                    dve.tensor_copy(dst[:], o[0:rows, 0:LP]).then_inc(v_freed, 1)

            def token_maxima(u, lg_ready):
                dve.wait_ge(s_freed, lg_ready)
                for t in range(QT):
                    dve.tensor_reduce(nmt[u][:, t:t + 1], lg[u][:, t, :], AX.X, ALU.max, negate=True
                                      ).then_inc(token_max, 1)

            def slot_maxima(u, pieces):
                for kind, n in pieces:
                    o = s.take()
                    if kind == "T":
                        dve.wait_ge(s_filled, s.filled())
                        dve.tensor_reduce(nms[u][:, n:n + 1], o[:, 0:L], AX.X, ALU.max, negate=True
                                          ).then_inc(slot_max, 1)

            def e2_T(b):
                dve.wait_ge(e2_stored, 16 * (b + 1))
                for t in range(ST):
                    o = v.take()
                    dve.wait_ge(v_filled, v.filled())
                    dve.tensor_copy(e2T[:, t, :], o[:, 0:L]).then_inc(v_freed, 1)

            def slot_statistics(xs_ready):
                dve.wait_ge(s_freed, xs_ready)
                for t in range(ST):
                    ins = dve.bn_stats(stats[:, t, :], xs[:, t, 0:D])
                link(ins)
                dve.sem_inc(carried, 1)
                for t in range(ST):
                    ins = dve.bn_aggr(smv[:, t, :], stats[:, t, :])
                link(ins)
                link(dve.tensor_tensor(ssq[:], xs[:, :, D], xs[:, :, D], ALU.mult))
                dve.scalar_tensor_tensor(svar[:], ssq[:], LN_EPS, smv[:, :, 1], ALU.mult, ALU.add
                                         ).then_inc(svar_ready, 1)

            def slot_scale(b):
                dve.wait_ge(srstd_ready, b + 1)
                for k in range(2):
                    for t in range(4 * k, 4 * k + 4):
                        ins = dve.tensor_scalar(xsn[:, t, :], xs[:, t, 0:D], smv[:, t, 0:1], srstd[:, t:t + 1],
                                                ALU.subtract, ALU.mult)
                    ins.then_inc(xsn_ready, 1)

            def slots_T(b):
                for k in range(2):
                    c = bass.ds(b * SLOTS_PER, SLOTS_PER)
                    for dst, g, r0, r1 in (
                        (xsTa[:, HALF * k:HALF * k + HALF, c], gTa[:, HALF * k:HALF * k + HALF], 0, P),
                        (xsTb[DB * k:DB * k + DB, :, c], gTb[DB * k:DB * k + DB, :], DB * k, DB * k + DB),
                    ):
                        o = v.take()
                        dve.wait_ge(v_filled, v.filled())
                        dve.tensor_tensor(dst, o[r0:r1, :].rearrange("d (n p) -> d n p", n=HALF),
                                          g.unsqueeze(2).to_broadcast([r1 - r0, HALF, SLOTS_PER]), ALU.mult
                                          ).then_inc(v_freed, 1)

            def period(b, u, loads, first=False, last=False):
                xs_ready = s.read()
                if not first:
                    dve.wait_ge(s_filled, s.filled())
                if not last:
                    normalize(b + 1, 1 - u)
                slot_maxima(u, HEAD)
                if not last:
                    tokens_T()
                pieces = ALONE if last else MIXED
                slot_maxima(u, pieces[:2])
                if not first:
                    slot_statistics(xs_ready)
                slot_maxima(u, pieces[2:])
                lg_ready = s.read()
                if not first:
                    slot_scale(b - 1)
                e2_T(b)
                if not first:
                    slots_T(b - 1)
                if not last:
                    token_maxima(1 - u, lg_ready)
                    layernorm(u, loads)
                s.n = s.n + 2 * QT + ST // 2

            layernorm(0, 1)
            layernorm(1, 1)
            dve.wait_ge(setup_mm, ST)
            parts = ((phiTa, P, 0), (phiTb, DB, 2))
            for dst, rows, b0 in parts:
                for k in range(2):
                    dve.tensor_copy(dst[:, 512 * k:512 * k + 512], vbank[b0 + k][0:rows, :]).then_inc(setup_step, 1)
            dve.wait_ge(setup_step, 4)
            for k, (src, rows, _) in enumerate(parts):
                dve.tensor_tensor(sq[0:rows, k, :], src[:], src[:], ALU.mult).then_inc(setup_step, 1)
            dve.wait_ge(setup_step, 6)
            for k, (src, rows, _) in enumerate(parts):
                dve.tensor_reduce(pn[0:rows, k, :], sq[0:rows, k, :].rearrange("d (n p) -> d p n", n=N_EXP),
                                  AX.X, ALU.add).then_inc(setup_step, 1)
            dve.wait_ge(setup_step, 8)
            dve.tensor_scalar(pn[:, 0, :], pn[:, 0, :], PHI_EPS, None, ALU.add).then_inc(setup_step, 1)
            dve.tensor_scalar(pn[0:DB, 1, :], pn[0:DB, 1, :], PHI_EPS, None, ALU.add).then_inc(pn_ready, 1)
            normalize(0, 0)
            dve.wait_ge(pn_ready, 3)
            for k, (src, rows, _) in enumerate(parts):
                w = src[:].rearrange("d (n p) -> d n p", n=N_EXP)
                dve.tensor_tensor(w, w, pn[0:rows, k:k + 1, :].to_broadcast([rows, N_EXP, SLOTS_PER]), ALU.mult
                                  ).then_inc(setup_step, 1)
            dve.wait_ge(setup_mm, ST + 2)
            for dst, col, k in ((gTa[:], (0, N_EXP), 0), (xsTa[:, :, EC], (0, N_EXP), 1)):
                dve.tensor_copy(dst, sbank[k][:, col[0]:col[1]]).then_inc(setup_step, 1)
            for dst, k in ((gTb, 0), (xsTb[:, :, EC], 1)):
                dve.tensor_copy(dst[0:DB, :], sbank[k][0:DB, P:P + HALF]).then_inc(setup_step, 1)
                dve.tensor_copy(dst[DB:P, :], sbank[k][DB:P, 2 * P:2 * P + HALF]).then_inc(setup_step, 1)
            dve.wait_ge(setup_step, 17)
            dve.sem_inc(setup_step, 1)
            tokens_T()
            s.n = 2 * QT
            token_maxima(0, s.read())
            period(0, 0, 2, first=True)
            with dve.Fori(0, BODIES) as i:
                v.enter(i)
                s.enter(i)
                chained.enter(i)
                period(2 * i + 1, 1, i + 2)
                period(2 * i + 2, 0, i + 3)
            v.leave(BODIES)
            s.leave(BODIES)
            chained.leave(BODIES)
            period(B - 1, 1, None, last=True)
            slot_statistics(s.read())
            slot_scale(B - 1)
            slots_T(B - 1)


def expert_phase(nc, xsTa, xsTb, w1, b1, w2, b2, c_ident, ys_d):
    with ExitStack() as ctx:
        a = Pool_(nc, ctx, "ex")
        NB = 4
        ident = a.sb("ident", [P, P])
        b1_in = a.sb("b1_in", [N_EXP, HID])
        b1T = a.sb("b1T", [P, HT, N_EXP])
        w1a = [a.sb(f"w1a{j}", [P, HID]) for j in range(NB)]
        w1b = [a.sb(f"w1b{j}", [P, HID]) for j in range(NB)]
        w2s = [a.sb(f"w2s{j}", [P, HT, D]) for j in range(NB)]
        b2s = [a.sb(f"b2s{j}", [P, D]) for j in range(NB)]
        bias = [a.sb(f"bias{j}", [P, HT]) for j in range(NB)]
        hT = [a.sb(f"hT{j}", [P, HT, EC]) for j in range(2)]
        ys = [a.sb(f"ys{j}", [P, 2, D]) for j in range(2)]
        vbank = [a.bank(f"vbank{i}") for i in range(RING)]
        sbank = [a.bank(f"sbank{i}") for i in range(RING)]
        consts_in = a.sem("consts_in")
        init_done = a.sem("init_done")
        b1_mm = a.sem("b1_mm")
        b1_ready = a.sem("b1_ready")
        v_filled, v_freed = a.sem("v_filled"), a.sem("v_freed")
        s_filled, s_freed = a.sem("s_filled"), a.sem("s_freed")
        w_in = [a.sem(f"w_in{j}") for j in range(NB)]
        bias_ready = a.sem("bias_ready")
        ys_stored = [a.sem(f"ys_stored{j}") for j in range(2)]
        block = ctx.enter_context(nc.Block())
        VN, SN = 2 * NB, 3 * NB
        N_W = 4

        def expert(i, j):
            return HALF * (j // 2) + 2 * i + j % 2

        @block.sync
        def _(sp):
            sp.dma_start(ident[:], c_ident).then_inc(consts_in, 16)
            sp.dma_start(b1_in[:], b1).then_inc(consts_in, 16)
            sp.wait_ge(init_done, NB)

            def load(n, j):
                r = DB * (j // 2)
                sp.dma_start(w1a[j][:], w1[n, 0:P, :]).then_inc(w_in[j], 16)
                sp.dma_start(w1b[j][r:r + DB, :], w1[n, P:D, :]).then_inc(w_in[j], 16)
                sp.dma_start(w2s[j][:], w2[n].rearrange("(t p) d -> p t d", p=P)).then_inc(w_in[j], 16)
                sp.dma_start(b2s[j][:], b2[n:n + 1, :].to_broadcast([P, D])).then_inc(w_in[j], 16)

            for j in range(NB):
                load(expert(0, j), j)
            w1v = w1.rearrange("(h i e) d k -> h e i d k", h=2, e=2)
            w2v = w2.rearrange("(h i e) k d -> h e i k d", h=2, e=2)
            b2v = b2.rearrange("(h i e) d -> h e i d", h=2, e=2)
            with sp.Fori(0, N_EXP // NB) as i:
                for j in range(NB):
                    sp.wait_ge(v_freed, RING + i * VN + 2 * j + 2)
                    yv = ys_d.rearrange("(k b) (h i e p) d -> h e k i b p d", k=2, h=2, e=2, p=SLOTS_PER)
                    for k in range(2):
                        sp.dma_start(yv[j // 2, j % 2, k, i], ys[j % 2][:, k, :]).then_inc(ys_stored[j % 2], 16)
                    nx = (i + 1) % (N_EXP // NB)
                    r = DB * (j // 2)
                    sp.dma_start(w1a[j][:], w1v[j // 2, j % 2, nx, 0:P, :]).then_inc(w_in[j], 16)
                    sp.dma_start(w1b[j][r:r + DB, :], w1v[j // 2, j % 2, nx, P:D, :]).then_inc(w_in[j], 16)
                    sp.dma_start(w2s[j][:], w2v[j // 2, j % 2, nx].rearrange("(t p) d -> p t d", p=P)
                                 ).then_inc(w_in[j], 16)
                    sp.dma_start(b2s[j][:], b2v[j // 2, j % 2, nx].unsqueeze(0).to_broadcast([P, D])
                                 ).then_inc(w_in[j], 16)
            for j in range(NB):
                sp.wait_ge(w_in[j], 16 * N_W * (1 + N_EXP // NB))
            for j in range(2):
                sp.wait_ge(ys_stored[j], 32 * (1 + N_EXP // 2))

        @block.tensor
        def _(pe):
            pe.wait_ge(consts_in, 32)
            for t in range(HT):
                pe.transpose(vbank[0][:, t * N_EXP:(t + 1) * N_EXP], b1_in[:, t * P:t * P + P], ident[0:N_EXP, 0:N_EXP]
                             ).then_inc(b1_mm, 1)
            pe.wait_ge(b1_ready, 1)
            with pe.Fori(0, N_EXP // NB) as i:
                v = Uses(vbank, VN)
                s = Uses(sbank, SN)
                at = {}

                def up(j):
                    pe.wait_ge(w_in[j], 16 * N_W * (i + 1))
                    n = expert(i, j)
                    for t in range(HT):
                        o = s.take()
                        pe.wait_ge(s_freed, s.free(i))
                        pe.matmul(o[:, 0:EC1], w1a[j][:, t * P:t * P + P], xsTa[:, bass.ds(n, 1), :], start=True, stop=False)
                        pe.matmul(o[:, 0:EC1], w1b[j][:, t * P:t * P + P], xsTb[:, bass.ds(2 * i + j % 2, 1), :],
                                  start=False, stop=True).then_inc(s_filled, 1)
                    at[j] = s.n

                def down(j):
                    pe.wait_ge(s_freed, s.read(i, at[j]))
                    for k in range(2):
                        o = v.take()
                        pe.wait_ge(v_freed, v.free(i))
                        for t in range(HT):
                            mm = pe.matmul(o[:, 0:D], hT[j % 2][:, t, k * P:k * P + P], w2s[j][:, t, :],
                                           start=(t == 0), stop=(t == HT - 1))
                        mm.then_inc(v_filled, 1)

                up(0)
                up(1)
                down(0)
                up(2)
                down(1)
                up(3)
                down(2)
                down(3)
                v.end()
                s.end()

        @block.scalar
        def _(act):
            act.sem_inc(s_freed, RING)
            with act.Fori(0, N_EXP // NB) as i:
                s = Uses(sbank, SN)
                for j in range(NB):
                    n = expert(i, j)
                    for t in range(HT):
                        o = s.take()
                        act.wait_ge(s_filled, s.filled(i))
                        act.activation(bias[j][:, t:t + 1], o[:, EC:EC1], ACT.Identity,
                                       bias=b1T[:, t, bass.ds(n, 1)]).then_inc(bias_ready, 1)
                        act.wait_ge(bias_ready, i * SN + HT * j + t + 1)
                        act.activation(hT[j % 2][:, t, :], o[:, 0:EC], ACT.Gelu, bias=bias[j][:, t:t + 1]
                                       ).then_inc(s_freed, 1)
                s.end()

        @block.vector
        def _(dve):
            dve.sem_inc(v_freed, RING)
            for j in range(2):
                dve.sem_inc(ys_stored[j], 32)
            for j in range(NB):
                r = DB * (1 - j // 2)
                dve.memset(w1b[j][r:r + DB, :], 0.0).then_inc(init_done, 1)
            dve.wait_ge(b1_mm, HT)
            dve.tensor_copy(b1T[:], vbank[0][:, 0:HT * N_EXP].rearrange("p (t n) -> p t n", t=HT)).then_inc(b1_ready, 1)
            dve.wait_ge(b1_ready, 1)
            with dve.Fori(0, N_EXP // NB) as i:
                v = Uses(vbank, VN)
                for j in range(NB):
                    dve.wait_ge(ys_stored[j % 2], 32 * (2 * i + j // 2 + 1))
                    dve.wait_ge(w_in[j], 16 * N_W * (i + 1))
                    for k in range(2):
                        o = v.take()
                        dve.wait_ge(v_filled, v.filled(i))
                        dve.tensor_tensor(ys[j % 2][:, k, :], o[:, 0:D], b2s[j][:], ALU.add).then_inc(v_freed, 1)
                v.end()


def combine_phase(nc, h2_d, e2_d, ys_d, out):
    with ExitStack() as ctx:
        a = Pool_(nc, ctx, "co")
        ys = [a.sb(f"ys{u}", [P, ST, D + 1]) for u in range(2)]
        e2T = [a.sb(f"e2T{u}", [P, ST, L]) for u in range(2)]
        hb = [a.sb(f"hb{u}", [P, QT, D]) for u in range(2)]
        res = [a.sb(f"res{u}", [P, QT, D]) for u in range(2)]
        rec = a.sb("rec", [P, 2 * QT])
        bank = [a.bank(f"bank{i}") for i in range(2 * QT)]
        ones_set = a.sem("ones_set")
        loaded = [a.sem(f"loaded{u}") for u in range(2)]
        filled, freed = a.sem("filled"), a.sem("freed")
        rec_ready = a.sem("rec_ready")
        stored = [a.sem(f"stored{u}") for u in range(2)]
        block = ctx.enter_context(nc.Block())
        N_IN = 4

        @block.sync
        def _(sp):
            ysv = ys_d.rearrange("(i u) (t p) d -> u i p t d", u=2, p=P)
            e2v = e2_d.rearrange("(i u) p c -> u i p c", u=2)
            h2v = h2_d.rearrange("(i u) l d -> u i l d", u=2)
            with sp.Fori(0, B // 2) as i:
                for u in range(2):
                    sp.wait_ge(freed, QT * (2 * i + u + 1))
                    sp.dma_start(ys[u][:, :, 0:D], ysv[u, i]).then_inc(loaded[u], 16)
                    sp.dma_start(e2T[u][:].rearrange("p t c -> p (t c)"), e2v[u, i]).then_inc(loaded[u], 16)
                    sp.dma_start(hb[u][:, 0:2, :], h2v[u, i, 0:2 * P].rearrange("(t p) d -> p t d", p=P)
                                 ).then_inc(loaded[u], 16)
                    sp.dma_start(hb[u][0:LAST, 2, :], h2v[u, i, 2 * P:L]).then_inc(loaded[u], 16)

        @block.scalar
        def _(act):
            ov = out.rearrange("(i u) l d -> u i l d", u=2)
            with act.Fori(0, B // 2) as i:
                for u in range(2):
                    act.wait_ge(freed, QT * (2 * i + u + 3))
                    act.dma_start(ov[u, i, 0:2 * P].rearrange("(t p) d -> p t d", p=P), res[u][:, 0:2, :]
                                  ).then_inc(stored[u], 16)
                    act.dma_start(ov[u, i, 2 * P:L], res[u][0:LAST, 2, :]).then_inc(stored[u], 16)
            for u in range(2):
                act.wait_ge(stored[u], 32 * (1 + B // 2))

        @block.tensor
        def _(pe):
            pe.wait_ge(ones_set, 2)
            with pe.Fori(0, B // 2) as i:
                for u in range(2):
                    pe.wait_ge(loaded[u], 16 * N_IN * (i + 1))
                    for t in range(QT):
                        r = P if t < 2 else LAST
                        pe.wait_ge(freed, QT * (2 * i + u) + t + 1)
                        for st in range(ST):
                            mm = pe.matmul(bank[QT * u + t][0:r, 0:D + 1], e2T[u][:, st, t * P:t * P + r], ys[u][:, st, :],
                                           start=(st == 0), stop=(st == ST - 1))
                        mm.then_inc(filled, 1)

        @block.vector
        def _(dve):
            dve.sem_inc(freed, 2 * QT)
            for u in range(2):
                dve.sem_inc(stored[u], 32)
                dve.memset(ys[u][:, :, D:D + 1], 1.0).then_inc(ones_set, 1)
            with dve.Fori(0, B // 2) as i:
                for u in range(2):
                    dve.wait_ge(stored[u], 32 * (i + 1))
                    for t in range(QT):
                        r = P if t < 2 else LAST
                        o = bank[QT * u + t]
                        rc = rec[0:r, QT * u + t:QT * u + t + 1]
                        dve.wait_ge(filled, QT * (2 * i + u) + t + 1)
                        dve.reciprocal(rc, o[0:r, D:D + 1]).then_inc(rec_ready, 1)
                        dve.wait_ge(rec_ready, QT * (2 * i + u) + t + 1)
                        dve.scalar_tensor_tensor(res[u][0:r, t, :], o[0:r, 0:D], rc, hb[u][0:r, t, :],
                                                 ALU.mult, ALU.add).then_inc(freed, 1)


def fusion_kernel(nc, i, out):
    h_d = nc.dram_tensor("h_d", [B, L, D], F32, kind="Internal").ap()
    h2_d = nc.dram_tensor("h2_d", [B, L, D], F32, kind="Internal").ap()
    e2_d = nc.dram_tensor("e2_d", [B, P, ST * L], F32, kind="Internal").ap()
    ys_d = nc.dram_tensor("ys_d", [B, S, D], F32, kind="Internal").ap()
    tok = "L0_tok_"
    patch_phase(nc, i["x"], i["txt"], i[tok + "freq_weight_h"], i[tok + "freq_weight_w"], i[tok + "proj_w"],
                i[tok + "proj_b"], i[tok + "cls_token"], i[tok + "position_embeddings"], i["c_dft"], i["c_selh"],
                i["c_selw"], i["c_ident"], h_d)
    attention_phase(nc, h_d, *(i["L0_attn_" + n] for n in ("Wq", "bq", "Wk", "bk", "Wv", "bv", "Wo", "bo")),
                    i["c_rope"], i["c_ident"], i["c_mask"], i["c_maskT"], h2_d)
    with ExitStack() as ctx:
        xsTa = ctx.enter_context(nc.sbuf_tensor("xsTa", [P, N_EXP, EC1], F32))
        xsTb = ctx.enter_context(nc.sbuf_tensor("xsTb", [P, HALF, EC1], F32))
        f = {n: i["L0_ffn_" + n] for n in ("phi", "ln_g", "ln_b", "w1", "b1", "w2", "b2")}
        dispatch_phase(nc, xsTa, xsTb, h2_d, f["phi"], f["ln_g"], f["ln_b"], i["c_ident"], e2_d)
        expert_phase(nc, xsTa, xsTb, f["w1"], f["b1"], f["w2"], f["b2"], i["c_ident"], ys_d)
    combine_phase(nc, h2_d, e2_d, ys_d, out)


_INS = ["x", "txt", "L0_tok_freq_weight_h", "L0_tok_freq_weight_w", "L0_tok_proj_w", "L0_tok_proj_b",
        "L0_tok_cls_token", "L0_tok_position_embeddings", "L0_attn_Wq", "L0_attn_bq", "L0_attn_Wk", "L0_attn_bk",
        "L0_attn_Wv", "L0_attn_bv", "L0_attn_Wo", "L0_attn_bo", "L0_ffn_phi", "L0_ffn_ln_g", "L0_ffn_ln_b",
        "L0_ffn_w1", "L0_ffn_b1", "L0_ffn_w2", "L0_ffn_b2"]


def kernel(**inputs):
    import concourse.bacc as _bacc
    from concourse.bass_utils import run_bass_kernel_spmd as _run

    nc = _bacc.Bacc("TRN2", target_bir_lowering=False, num_devices=1)
    arrays, args = {}, {}
    for name, value in [(n, inputs[n]) for n in _INS] + list(shape_constants().items()):
        v = np.ascontiguousarray(value)
        arrays[f"in_{name}_dram"] = v
        args[name] = nc.dram_tensor(f"in_{name}_dram", v.shape, mybir.dt.from_np(v.dtype), kind="ExternalInput").ap()
    out = nc.dram_tensor("out_0_dram", (B, L, D), F32, kind="ExternalOutput").ap()
    fusion_kernel(nc, args, out)
    r = _run(nc, [arrays], core_ids=[0])
    return r.results[0]["out_0_dram"]
```

```python
from contextlib import ExitStack

import numpy as np

import concourse.bass as bass
from concourse import mybir

F32 = mybir.dt.float32
F32R = mybir.dt.float32r
BF16 = mybir.dt.bfloat16
ALU = mybir.AluOpType
ACT = mybir.ActivationFunctionType
AX = mybir.AxisListType

P = 128
D = 192
DB = D - P
B = 16
C_IN, IMG, PATCH = 3, 224, 16
NH = IMG // PATCH
NPATCH = NH * NH
TXT = 128
L = 1 + NPATCH + TXT
QT = 3
LAST = L - 2 * P
LE = L + L % 2
LASTE = LE - 2 * P
LP = QT * P
HEADS, HD = 12, 16
N_EXP, SLOTS_PER = 64, 16
S = N_EXP * SLOTS_PER
ST = S // P
EPT = P // SLOTS_PER
HID = 2 * D
HT = HID // P
KW = PATCH // 2 + 1
NF = PATCH * KW
FT = 4
FR = C_IN * NF // FT
SHIFTS = 2
PWS = PATCH // SHIFTS
ROWS = SHIFTS * C_IN * PATCH
NROW = NH // 2
PTOK = NROW * NH
LN_EPS = 1e-5
PHI_EPS = 1e-6
MASKED = -1e30
PRIME = 2
RING = 4


def shape_constants():
    k = np.arange(C_IN * NF)
    c, kh, kw = k // NF, (k % NF) // KW, k % KW
    ph = np.arange(PATCH)
    dft = np.zeros((C_IN * NF, PWS, SHIFTS, C_IN, PATCH), np.float64)
    for s in range(SHIFTS):
        for p in range(PWS):
            pw = p + PWS * s
            ang = 2 * np.pi * ((kh[:, None] * ph[None, :] + kw[:, None] * pw) % PATCH) / PATCH
            dft[k, p, s, c, :] = np.cos(ang) / PATCH
    dft = dft.reshape(FT, FR, PWS, ROWS).transpose(1, 0, 2, 3)
    sel_h = (np.arange(PATCH)[:, None] == kh[None, :]).astype(np.float32)
    sel_w = (np.arange(KW)[:, None] == kw[None, :]).astype(np.float32)
    inv = (1.0 / 10000.0 ** (np.arange(0, HD, 2, dtype=np.float32) / np.float32(HD))).astype(np.float32)
    ang = (np.arange(LP, dtype=np.float32)[:, None] * inv[None, :]).astype(np.float32)
    cos, sin = np.cos(ang.astype(np.float64)), np.sin(ang.astype(np.float64))
    rope = np.concatenate([cos, cos, -sin, sin], 1).reshape(QT, P, 4 * (HD // 2)).transpose(1, 0, 2)
    i = np.arange(P)
    return {
        "c_dft": np.ascontiguousarray(dft.astype(np.float32)),
        "c_selh": sel_h,
        "c_selw": sel_w,
        "c_rope": np.ascontiguousarray(rope.astype(np.float32)),
        "c_ident": np.eye(P, dtype=np.float32),
        "c_mask": np.where(i[None, :] > i[:, None], MASKED, 0.0).astype(np.float32),
        "c_maskT": np.where(i[:, None] > i[None, :], MASKED, 0.0).astype(np.float32),
    }


class Alloc:

    def __init__(self, nc, ctx, tag):
        self.nc, self.ctx, self.tag = nc, ctx, tag

    def sb(self, name, shape, dt=F32):
        return self.ctx.enter_context(self.nc.sbuf_tensor(f"{self.tag}_{name}", shape, dt))

    def bank(self, name):
        return self.ctx.enter_context(self.nc.psum_tensor(f"{self.tag}_{name}", [P, 512], F32))

    def sem(self, name):
        return self.ctx.enter_context(self.nc.semaphore(f"{self.tag}_{name}"))


def patch_phase(nc, x, txt, fh, fw, proj_w, proj_b, cls_token, pos, c_dft, c_selh, c_selw, c_ident, h_d,
                phi, phis, attn, attn_in):
    phAh, phAl, phBs, phBl = phis
    c_mask, c_maskT, c_rope, *attn_w = attn_in
    with ExitStack() as ctx:
        a = Alloc(nc, ctx, "pt")
        ident = a.sb("ident", [P, P])
        dft = a.sb("dft", [FR, FT, PWS, ROWS])
        selh = a.sb("selh", [PATCH, C_IN * NF])
        selw = a.sb("selw", [KW, C_IN * NF])
        fhc = a.sb("fhc", [PATCH, 1])
        fwc = a.sb("fwc", [KW, 1])
        pw_a = a.sb("pw_a", [P, C_IN * NF])
        pw_b = a.sb("pw_b", [DB, C_IN * NF])
        fsel = a.sb("fsel", [FR, 2 * FT])
        fcol = a.sb("fcol", [FR, FT])
        pT = a.sb("pT", [FR, FT, D])
        weff = a.sb("weff", [ROWS, PWS, D])
        ones = a.sb("ones", [1, P])
        brow = a.sb("brow", [1, D])
        clsr = a.sb("clsr", [1, D])
        pos0 = a.sb("pos0", [1, D])
        cls0 = a.sb("cls0", [1, D])
        clsb = a.sb("clsb", [B, D])
        posb = a.sb("posb", [PTOK, 2, D])
        img = [a.sb(f"img{u}", [ROWS, NH, IMG]) for u in range(2)]
        emb = [a.sb(f"emb{u}", [PTOK, 2, D]) for u in range(2)]
        ident_phi = a.sb("ident_phi", [P, P])
        phi_in = a.sb("phi_in", [P, ST, D])
        phiT = a.sb("phiT", [P, 2, S])
        sq = a.sb("sq", [P, 2, S])
        pn = a.sb("pn", [P, 2, SLOTS_PER])
        half = a.sb("half", [P, SLOTS_PER])
        w_in = a.sb("w_in", [P, 4, 2, D])
        maskf = a.sb("maskf", [P, 2, P])
        bank = [a.bank(f"bank{i}") for i in range(8)]
        phi_loaded = a.sem("phi_loaded")
        phi_mm = a.sem("phi_mm")
        phi_step = a.sem("phi_step")
        half_set = a.sem("half_set")
        pn_ready = a.sem("pn_ready")
        attn_loaded = a.sem("attn_loaded")
        wT_mm = a.sem("wT_mm")
        attn_ready = a.sem("attn_ready")
        consts_in = a.sem("consts_in")
        ones_set = a.sem("ones_set")
        projT_done = a.sem("projT_done")
        fsel_done = a.sem("fsel_done")
        fsel_copied = a.sem("fsel_copied")
        fcol_done = a.sem("fcol_done")
        pT_ready = a.sem("pT_ready")
        weff_mm = a.sem("weff_mm")
        weff_ready = a.sem("weff_ready")
        bias_mm = a.sem("bias_mm")
        posb_ready = a.sem("posb_ready")
        cls0_ready = a.sem("cls0_ready")
        cls_mm = a.sem("cls_mm")
        clsb_ready = a.sem("clsb_ready")
        img_in = [a.sem(f"img_in{u}") for u in range(2)]
        emb_mm = a.sem("emb_mm")
        emb_ready = a.sem("emb_ready")
        emb_stored = [a.sem(f"emb_stored{u}") for u in range(2)]
        stored = a.sem("stored")
        N_CONST = 12
        N_ATTN = 16
        block = ctx.enter_context(nc.Block())

        @block.sync
        def _(sp):
            sp.dma_start(h_d[:, 1 + NPATCH:L, :], txt).then_inc(stored, 16)
            for dst, src in (
                (ident[:], c_ident), (dft[:], c_dft), (selh[:], c_selh), (selw[:], c_selw),
                (fhc[:], fh.rearrange("(a b) -> a b", b=1)), (fwc[:], fw.rearrange("(a b) -> a b", b=1)),
                (pw_a[:], proj_w[0:P, :]), (pw_b[:], proj_w[P:D, :]),
                (brow[:], proj_b.rearrange("(a b) -> a b", a=1)), (clsr[:], cls_token[0]),
                (pos0[:], pos[0, 0:1, :]),
                (posb[:], pos[0, 1:1 + NPATCH, :].rearrange("(t p) d -> p t d", p=PTOK)),
            ):
                sp.dma_start(dst, src).then_inc(consts_in, 16)
            for dst, src in ((attn["ident"][:], c_ident), (maskf[:, 0, :], c_mask), (maskf[:, 1, :], c_maskT),
                             (attn["rope"][:], c_rope)):
                sp.dma_start(dst, src).then_inc(attn_loaded, 16)
            for j, w in enumerate(attn_w[0::2]):
                sp.dma_start(w_in[:, j, 0, :], w[0:P, :]).then_inc(attn_loaded, 16)
                sp.dma_start(w_in[0:DB, j, 1, :], w[P:D, :]).then_inc(attn_loaded, 16)
            for j, w in enumerate(attn_w[1::2]):
                sp.dma_start(attn["wb"][DB:DB + 1, j, :], w.rearrange("(a b) -> a b", a=1)).then_inc(attn_loaded, 16)
            with sp.Fori(0, B // 2) as i:
                for u in range(2):
                    sp.wait_ge(emb_mm, 2 * i + u + 1)
                    xb = x.rearrange("(i u) c (nh ph) w -> u i c ph nh w", u=2, ph=PATCH)[u, i]
                    for s in range(SHIFTS):
                        for c in range(C_IN):
                            r0 = (s * C_IN + c) * PATCH
                            w = IMG - PWS * s
                            sp.dma_start(img[u][r0:r0 + PATCH, :, 0:w], xb[c, :, :, PWS * s:IMG]
                                         ).then_inc(img_in[u], 16)

        @block.gpsimd
        def _(pool):
            pool.memset(half[:], -0.5).then_inc(half_set, 1)
            pool.wait_ge(half_set, 1)
            pool.wait_ge(pn_ready, 2)
            for k, r in enumerate((P, DB)):
                pool.tensor_tensor(pn[0:r, k, :], pn[0:r, k, :], half[0:r, :], ALU.pow).then_inc(pn_ready, 1)

        @block.scalar
        def _(act):
            act.dma_start(ident_phi[:], c_ident).then_inc(phi_loaded, 16)
            act.dma_start(phi_in[:], phi.rearrange("n p d -> (n p) d").rearrange("(t p) d -> p t d", p=P)
                          ).then_inc(phi_loaded, 16)
            for u in range(2):
                act.sem_inc(emb_stored[u], 16)
            act.wait_ge(attn_loaded, 16 * N_ATTN)
            act.copy(attn["identb"][:], attn["ident"][:]).then_inc(attn_ready, 1)
            act.copy(attn["identr"][:].bitcast(F32R), attn["ident"][:]).then_inc(attn_ready, 1)
            act.copy(attn["mask"][:], maskf[:]).then_inc(attn_ready, 1)
            act.wait_ge(clsb_ready, 1)
            act.dma_start(h_d[:, 0, :], clsb[:]).then_inc(stored, 16)
            with act.Fori(0, B // 2) as i:
                for u in range(2):
                    act.wait_ge(emb_ready, PRIME + 2 * i + u + 1)
                    hb = h_d.rearrange("(i u) l d -> u i l d", u=2)[u, i]
                    act.dma_start(hb[1:1 + NPATCH, :].rearrange("(t p) d -> p t d", p=PTOK), emb[u][:]
                                  ).then_inc(emb_stored[u], 16)
            act.wait_ge(stored, 32)
            for u in range(2):
                act.wait_ge(emb_stored[u], 16 * (1 + B // 2))

        @block.tensor
        def _(pe):
            pe.sem_inc(emb_mm, PRIME)
            pe.wait_ge(phi_loaded, 32)
            for t in range(ST):
                pe.transpose(bank[4 + t // 4][:, (t % 4) * P:(t % 4) * P + P], phi_in[:, t, 0:P], ident_phi[:])
                pe.transpose(bank[6 + t // 4][0:DB, (t % 4) * P:(t % 4) * P + P], phi_in[:, t, P:D], ident_phi[:]
                             ).then_inc(phi_mm, 1)
            pe.wait_ge(consts_in, 16 * N_CONST)
            for t in range(FT):
                o = bank[t // 2][0:FR, (t % 2) * D:(t % 2) * D + D]
                pe.transpose(o[:, 0:P], pw_a[:, FR * t:FR * t + FR], ident[:])
                pe.transpose(o[:, P:D], pw_b[:, FR * t:FR * t + FR], ident[0:DB, 0:DB]).then_inc(projT_done, 1)
            for t in range(FT):
                pe.matmul(bank[2][0:FR, t:t + 1], selh[:, FR * t:FR * t + FR], fhc[:], start=True, stop=True)
                pe.matmul(bank[2][0:FR, FT + t:FT + t + 1], selw[:, FR * t:FR * t + FR], fwc[:],
                          start=True, stop=True).then_inc(fsel_done, 1)
            pe.wait_ge(ones_set, 1)
            pe.matmul(bank[3][0:PTOK, 0:D], ones[:, 0:PTOK], brow[:], start=True, stop=True).then_inc(bias_mm, 1)
            for p in range(PWS):
                if p == 0:
                    pe.wait_ge(pT_ready, FT)
                    pe.wait_ge(phi_step, 4)
                for t in range(FT):
                    mm = pe.matmul(bank[4 + p // 2][0:ROWS, (p % 2) * D:(p % 2) * D + D], dft[:, t, p, :], pT[:, t, :],
                                   start=(t == 0), stop=(t == FT - 1))
                mm.then_inc(weff_mm, 1)
            pe.wait_ge(cls0_ready, 1)
            pe.matmul(bank[2][0:B, 256:256 + D], ones[:, 0:B], cls0[:], start=True, stop=True).then_inc(cls_mm, 1)
            pe.wait_ge(weff_ready, PWS)
            pe.wait_ge(clsb_ready, 1)
            pe.wait_ge(attn_loaded, 16 * N_ATTN)
            for j in range(4):
                o = bank[4 + j]
                pe.transpose(o[:, 0:P], w_in[:, j, 0, 0:P], ident[:])
                pe.transpose(o[:, P:D], w_in[0:DB, j, 1, 0:P], ident[0:DB, 0:DB])
                pe.transpose(o[0:DB, D:D + P], w_in[:, j, 0, P:D], ident[:])
                pe.transpose(o[0:DB, D + P:2 * D], w_in[0:DB, j, 1, P:D], ident[0:DB, 0:DB]).then_inc(wT_mm, 1)
            with pe.Fori(0, B // 2) as i:
                for u in range(2):
                    pe.wait_ge(img_in[u], 16 * SHIFTS * C_IN * (i + 1))
                    pe.wait_ge(emb_ready, 2 * i + u + 1)
                    for t in range(2):
                        for p in range(PWS):
                            px = img[u][:, t * NROW:(t + 1) * NROW, p:p + PATCH * (NH - 1) + 1:PATCH]
                            mm = pe.matmul(bank[u * 2 + t][0:PTOK, 0:D], px, weff[:, p, :],
                                           start=(p == 0), stop=(p == PWS - 1))
                    mm.then_inc(emb_mm, 1)

        @block.vector
        def _(dve):
            dve.sem_inc(emb_ready, PRIME)
            dve.memset(ones[:], 1.0).then_inc(ones_set, 1)
            dve.wait_ge(phi_mm, ST)
            parts = ((4, P), (6, DB))
            for k, (b0, r) in enumerate(parts):
                for j in range(2):
                    dve.tensor_copy(phiT[0:r, k, 512 * j:512 * j + 512], bank[b0 + j][0:r, :]).then_inc(phi_step, 1)
            dve.wait_ge(fsel_done, FT)
            dve.tensor_copy(fsel[:], bank[2][0:FR, 0:2 * FT]).then_inc(fsel_copied, 1)
            dve.wait_ge(fsel_copied, 1)
            dve.tensor_tensor(fcol[:], fsel[:, 0:FT], fsel[:, FT:2 * FT], ALU.mult).then_inc(fcol_done, 1)
            dve.wait_ge(fcol_done, 1)
            for t in range(FT):
                dve.wait_ge(projT_done, 2 * (t // 2) + 2)
                dve.tensor_scalar(pT[:, t, :], bank[t // 2][0:FR, (t % 2) * D:(t % 2) * D + D], fcol[:, t:t + 1],
                                  None, ALU.mult).then_inc(pT_ready, 1)
            dve.wait_ge(consts_in, 16 * N_CONST)
            dve.wait_ge(bias_mm, 1)
            for t in range(2):
                dve.tensor_tensor(posb[:, t, :], posb[:, t, :], bank[3][0:PTOK, 0:D], ALU.add).then_inc(posb_ready, 1)
            dve.tensor_tensor(cls0[:], clsr[:], pos0[:], ALU.add).then_inc(cls0_ready, 1)
            dve.wait_ge(phi_step, 4)
            for k, (_, r) in enumerate(parts):
                dve.tensor_tensor(sq[0:r, k, :], phiT[0:r, k, :], phiT[0:r, k, :], ALU.mult).then_inc(phi_step, 1)
            dve.wait_ge(phi_step, 6)
            for k, (_, r) in enumerate(parts):
                dve.tensor_reduce(pn[0:r, k, :], sq[0:r, k, :].rearrange("d (n p) -> d p n", n=N_EXP),
                                  AX.X, ALU.add).then_inc(phi_step, 1)
            dve.wait_ge(phi_step, 8)
            for k, (_, r) in enumerate(parts):
                dve.tensor_scalar(pn[0:r, k, :], pn[0:r, k, :], PHI_EPS, None, ALU.add).then_inc(pn_ready, 1)
            for p in range(PWS):
                dve.wait_ge(weff_mm, 2 * (p // 2) + 2)
                dve.tensor_copy(weff[:, p, :], bank[4 + p // 2][0:ROWS, (p % 2) * D:(p % 2) * D + D]
                                ).then_inc(weff_ready, 1)
            dve.wait_ge(cls_mm, 1)
            dve.tensor_copy(clsb[:], bank[2][0:B, 256:256 + D]).then_inc(clsb_ready, 1)
            wa, wb = attn["wa"], attn["wb"]
            scale = float(HD) ** -0.5
            dve.wait_ge(attn_loaded, 16 * N_ATTN)
            dve.tensor_scalar(wb[DB:DB + 1, 0, :], wb[DB:DB + 1, 0, :], scale, None, ALU.mult).then_inc(attn_ready, 1)
            for j in range(4):
                dve.wait_ge(wT_mm, j + 1)
                by = scale if j == 0 else 1.0
                dve.tensor_scalar(wa[:, j, :], bank[4 + j][:, 0:D], by, None, ALU.mult).then_inc(attn_ready, 1)
                dve.tensor_scalar(wb[0:DB, j, :], bank[4 + j][0:DB, D:2 * D], by, None, ALU.mult).then_inc(attn_ready, 1)
            dve.wait_ge(pn_ready, 4)
            for k, (_, r) in enumerate(parts):
                w = phiT[0:r, k, :].rearrange("d (n p) -> d n p", n=N_EXP)
                dve.tensor_tensor(w, w, pn[0:r, k:k + 1, :].to_broadcast([r, N_EXP, SLOTS_PER]), ALU.mult
                                  ).then_inc(phi_step, 1)
            dve.wait_ge(phi_step, 10)
            for k, (dst, r) in enumerate(((phAh[:], P), (phBs[0:DB, :], DB), (phBs[DB:P, :], DB))):
                dve.tensor_copy(dst.bitcast(F32R), phiT[0:r, min(k, 1), :]).then_inc(phi_step, 1)
            dve.wait_ge(phi_step, 13)
            for k, (low, high, r) in enumerate(((phAl, phAh, P), (phBl, phBs, DB))):
                dve.tensor_tensor(low[:].bitcast(F32R), phiT[0:r, k, :], high[0:r, :], ALU.subtract).then_inc(phi_step, 1)
            dve.wait_ge(posb_ready, 2)
            with dve.Fori(0, B // 2) as i:
                for u in range(2):
                    dve.wait_ge(emb_mm, PRIME + 2 * i + u + 1)
                    dve.wait_ge(emb_stored[u], 16 * (i + 1))
                    for t in range(2):
                        add = dve.tensor_tensor(emb[u][:, t, :], bank[u * 2 + t][0:PTOK, 0:D], posb[:, t, :], ALU.add)
                    add.then_inc(emb_ready, 1)


class Uses:

    def __init__(self, banks, per_body):
        self.banks, self.per_body, self.n = banks, per_body, -1
        assert per_body % len(banks) == 0

    def take(self):
        self.n += 1
        return self.banks[self.n % len(self.banks)]

    def free(self, i):
        return i * self.per_body + self.n + 1

    def filled(self, i):
        return i * self.per_body + self.n + 1

    def read(self, i, n=None):
        return i * self.per_body + (self.n if n is None else n) + 1 + len(self.banks)

    def end(self):
        assert self.n + 1 == self.per_body, (self.n + 1, self.per_body)


class Count:

    def __init__(self, per_body):
        self.per_body, self.n, self.base, self.start = per_body, 0, 0, None

    def enter(self, i):
        self.base, self.start = i * self.per_body, self.n

    def leave(self, bodies):
        assert self.n - self.start == self.per_body, (self.start, self.n)
        self.base = (bodies - 1) * self.per_body

    def value(self, more=0):
        return self.base + self.n + more


class Ring(Count):

    def __init__(self, banks, per_body):
        super().__init__(per_body)
        assert per_body % len(banks) == 0
        self.banks = banks

    def take(self):
        self.n += 1
        return self.banks[(self.n - 1) % len(self.banks)]

    def free(self):
        return self.value()

    def filled(self):
        return self.value()

    def read(self, n=None):
        return self.value(len(self.banks) + (0 if n is None else n - self.n))


GROUP = 4
NG = HEADS // GROUP
PAIRS = HEADS // 2
STK = 64
MROW = 3 * HD
PTC = LE + (LE - P) + LASTE
AC = LE + LASTE
BC = LE - P


ATTN_TENSORS = ("ident", "identb", "identr", "mask", "rope", "wa", "wb")


def attention_phase(nc, h_d, attn, h2_d):
    with ExitStack() as ctx:
        a = Alloc(nc, ctx, "at")
        ident, identb, identr, mask, rope, wa, wb = (attn[n] for n in ATTN_TENSORS)
        half = a.sb("half", [P, QT])
        hb = [a.sb(f"hb{u}", [P, QT, D]) for u in range(2)]
        hr = [a.sb(f"hr{u}", [P, QT, D]) for u in range(2)]
        stats = [a.sb(f"stats{u}", [P, QT, 6]) for u in range(2)]
        mv = [a.sb(f"mv{u}", [P, QT, 2]) for u in range(2)]
        var = [a.sb(f"var{u}", [P, QT]) for u in range(2)]
        rstd = [a.sb(f"rstd{u}", [P, QT]) for u in range(2)]
        xn = [a.sb(f"xn{u}", [P, QT, D]) for u in range(2)]
        xTa = [a.sb(f"xTa{u}", [P, LP]) for u in range(2)]
        xTb = [a.sb(f"xTb{u}", [DB + 1, LP]) for u in range(2)]
        rots = [a.sb(f"rot{u}", [P, 2, 2 * HEADS, HD]) for u in range(2)]
        stk = [a.sb(f"stk{u}", [P, QT, 2 * HEADS, STK]) for u in range(2)]
        vaug = [a.sb(f"vaug{u}", [P, QT, HEADS, 32]) for u in range(2)]
        qT = [a.sb(f"qT{u}", [P, PAIRS, LP]) for u in range(2)]
        kT = [a.sb(f"kT{u}", [P, PAIRS, LP]) for u in range(2)]
        mx = [a.sb(f"mx{u}", [P, QT, HEADS]) for u in range(2)]
        probs = [a.sb(f"probs{u}", [P, GROUP, PTC]) for u in range(2)]
        oT = [a.sb(f"oT{u}", [P, NG, LP]) for u in range(2)]
        rden = [a.sb(f"rden{u}", [P, QT, HEADS]) for u in range(2)]
        on = [a.sb(f"on{u}", [P, QT, D]) for u in range(2)]
        onTa = [a.sb(f"onTa{u}", [P, LP]) for u in range(2)]
        onTb = [a.sb(f"onTb{u}", [DB + 1, LP]) for u in range(2)]
        h2 = [a.sb(f"h2{u}", [P, QT, D]) for u in range(2)]
        vbank = [a.bank(f"vbank{i}") for i in range(RING)]
        sbank = [a.bank(f"sbank{i}") for i in range(RING)]

        padded = a.sem("padded")
        init_done = a.sem("init_done")
        v_filled, v_freed = a.sem("v_filled"), a.sem("v_freed")
        s_filled, s_freed = a.sem("s_filled"), a.sem("s_freed")
        vec_step = a.sem("vec_step")
        carried = a.sem("carried")
        h_in = [a.sem(f"h_in{u}") for u in range(2)]
        hr_in = [a.sem(f"hr_in{u}") for u in range(2)]
        var_ready = a.sem("var_ready")
        rstd_ready = a.sem("rstd_ready")
        xn_ready = a.sem("xn_ready")
        rope_ready = a.sem("rope_ready")
        dup_ready = a.sem("dup_ready")
        max_ready = a.sem("max_ready")
        h2_stored = [a.sem(f"h2_stored{u}") for u in range(2)]
        block = ctx.enter_context(nc.Block())

        N_INIT = 15
        BODIES = B // 2 - 1
        VN, SN = 68, 84
        V_FIRST = 19
        V_ALONE = 15
        VSTEPS = 24
        FIRST_MAXES = [(0, g + j, 3, P) for g in (0, 6) for j in range(2)]
        MIDDLE_MAXES = [(1, g + j, 2, 2 * P) for g in range(0, HEADS, 4) for j in range(2)]
        LAST_MAXES = [[(2, 2 * p + j, 1, LE) for j in range(2)] for p in range(PAIRS)]

        @block.sync
        def _(sp):
            sp.wait_ge(padded, 2)
            hd = h_d.rearrange("(i u) l d -> u i l d", u=2)
            h2d = h2_d.rearrange("(i u) l d -> u i l d", u=2)

            def load(dst, arrived, u, b2):
                sp.dma_start(dst[u][:, 0:2, :], hd[u, b2, 0:2 * P].rearrange("(t p) d -> p t d", p=P)
                             ).then_inc(arrived[u], 16)
                sp.dma_start(dst[u][0:LAST, 2, :], hd[u, b2, 2 * P:L]).then_inc(arrived[u], 16)

            def store(u, b2, v_before, uses):
                sp.wait_ge(v_freed, v_before + RING + uses)
                sp.dma_start(h2d[u, b2, 0:2 * P].rearrange("(t p) d -> p t d", p=P), h2[u][:, 0:2, :]
                             ).then_inc(h2_stored[u], 16)
                sp.dma_start(h2d[u, b2, 2 * P:L], h2[u][0:LAST, 2, :]).then_inc(h2_stored[u], 16)

            for u in range(2):
                load(hb, h_in, u, 0)
            for u in range(2):
                load(hr, hr_in, u, 0)
            for u in range(2):
                sp.wait_ge(xn_ready, u + 1)
                load(hb, h_in, u, 1)
            with sp.Fori(0, BODIES) as i:
                for u in range(2):
                    sp.wait_ge(xn_ready, 2 * i + u + 3)
                    load(hb, h_in, u, (i + 2) % (B // 2))
                    store(u, i, V_FIRST + i * VN + u * (VN // 2), VN // 2)
                    load(hr, hr_in, u, i + 1)
            store(0, BODIES, V_FIRST + BODIES * VN, VN // 2)
            store(1, BODIES, V_FIRST + BODIES * VN + VN // 2, V_ALONE)
            for u in range(2):
                sp.wait_ge(h2_stored[u], 32 * (1 + B // 2))
                sp.wait_ge(h_in[u], 32 * (1 + B // 2))

        @block.gpsimd
        def _(pool):
            pool.memset(half[:], -0.5).then_inc(init_done, 1)
            pool.wait_ge(init_done, N_INIT)

            def deviations(b, u):
                pool.wait_ge(var_ready, b + 1)
                pool.tensor_tensor(rstd[u][:], var[u][:], half[:], ALU.pow).then_inc(rstd_ready, 1)

            def duplicates(b, u):
                for t in range(QT):
                    pool.wait_ge(rope_ready, QT * b + t + 1)
                    pool.sem_inc(carried, 1)
                    pool.tensor_copy(stk[u][:, t, 0:HEADS, 2 * HD:3 * HD].bitcast(F32R), stk[u][:, t, 0:HEADS, 0:HD])
                    pool.tensor_copy(stk[u][:, t, HEADS:, HD:2 * HD].bitcast(F32R), stk[u][:, t, HEADS:, 0:HD]
                                     ).then_inc(dup_ready, 1)

            deviations(0, 0)
            deviations(1, 1)
            duplicates(0, 0)
            with pool.Fori(0, BODIES) as i:
                for u in range(2):
                    duplicates(2 * i + u + 1, 1 - u)
                    deviations(2 * i + u + 2, u)
            duplicates(B - 1, 1)

        @block.tensor
        def _(pe):
            pe.wait_ge(init_done, N_INIT)
            v = Ring(vbank, VN)
            s = Ring(sbank, SN)
            at = {}

            def layer_in(b, u):
                pe.wait_ge(xn_ready, b + 1)
                ta = s.take()
                pe.wait_ge(s_freed, s.free())
                for t in range(QT):
                    mm = pe.transpose(ta[:, t * P:t * P + P], xn[u][:, t, 0:P], ident[:])
                mm.then_inc(s_filled, 1)
                tb = s.take()
                pe.wait_ge(s_freed, s.free())
                pe.sem_inc(carried, 1)
                for t in range(QT):
                    mm = pe.transpose(tb[0:DB, t * P:t * P + P], xn[u][:, t, P:D], ident[:])
                mm.then_inc(s_filled, 1)

            def queries_keys(u, t):
                o = v.take()
                pe.wait_ge(v_freed, v.free())
                pe.matmul(o[:, 0:2 * D], xTa[u][:, t * P:t * P + P], wa[:, 0:2, :], start=True, stop=False)
                pe.matmul(o[:, 0:2 * D], xTb[u][:, t * P:t * P + P], wb[:, 0:2, :], start=False, stop=True
                          ).then_inc(v_filled, 1)

            def values(u, ts):
                o = s.take()
                pe.wait_ge(s_freed, s.free())
                for t in ts:
                    c = (t % 2) * D
                    pe.matmul(o[:, c:c + D], xTa[u][:, t * P:t * P + P], wa[:, 2, :], start=True, stop=False)
                    mm = pe.matmul(o[:, c:c + D], xTb[u][:, t * P:t * P + P], wb[:, 2, :], start=False, stop=True)
                mm.then_inc(s_filled, 1)

            def stack_T(u, first, p):
                o = s.take()
                pe.wait_ge(s_freed, s.free())
                for t in range(QT):
                    mm = pe.transpose(o[:, t * P:t * P + P].bitcast(F32R),
                                      stk[u][:, t, first + 2 * p:first + 2 * p + 2, :].bitcast(F32R), identr[:].bitcast(F32R))
                mm.then_inc(s_filled, 1)

            def pairs_in(b, u, pairs):
                if pairs[0] == 0:
                    pe.wait_ge(dup_ready, QT * (b + 1))
                for p in pairs:
                    stack_T(u, 0, p)
                    stack_T(u, HEADS, p)
                    at["qk", p] = s.n
                    if p > 0:
                        pe.wait_ge(s_freed, s.read(at["qk", p - 1]))
                        maxima(u, LAST_MAXES[p - 1])

            def maxima(u, tiles):
                for t, h0, n, keys in tiles:
                    o = v.take()
                    pe.wait_ge(v_freed, v.free())
                    ov = o[:, 0:n * keys].rearrange("p (n k) -> p n k", n=n)
                    diag = min(P, keys - t * P)
                    pe.matmul(ov[:, :, t * P:t * P + diag], identb[:],
                              mask[:, 0:1, 0:diag].to_broadcast([P, n, diag]), start=True, stop=True)
                    for j in range(n):
                        h = h0 + 2 * j
                        r = STK * (h % 2)
                        mm = pe.matmul(ov[:, j, :], qT[u][r:r + MROW, h // 2, t * P:t * P + P].bitcast(F32R),
                                       kT[u][r:r + MROW, h // 2, 0:keys].bitcast(F32R), start=False, stop=True,
                                       skip_group_check=True)
                    mm.then_inc(v_filled, 1)

            def q_T_again(b, u):
                pe.wait_ge(max_ready, b + 1)
                for p in range(PAIRS):
                    stack_T(u, 0, p)
                at["q2"] = s.n

            def scores(u, g):
                if g == 0:
                    pe.wait_ge(s_freed, s.read(at["q2"]))
                for j in range(2):
                    r = STK * j
                    pairs = (g * GROUP // 2, g * GROUP // 2 + 1)
                    for pr in pairs:
                        kh = kT[u][r:r + STK, pr, :].bitcast(F32R)
                        qh = qT[u][r:r + STK, pr, :].bitcast(F32R)
                        o = s.take()
                        pe.wait_ge(s_freed, s.free())
                        pe.matmul(o[:, 0:P], identb[:], mask[:, 1, :], start=True, stop=True, skip_group_check=True)
                        pe.matmul(o[:, LE:AC], identb[:], mask[:, 1, 0:LASTE], start=False, stop=True,
                                  skip_group_check=True)
                        pe.matmul(o[:, 0:LE], kh[:, 0:P], qh[:, 0:LE], start=False, stop=True, skip_group_check=True)
                        pe.matmul(o[:, LE:AC], kh[:, 2 * P:LP], qh[:, 2 * P:LE], start=False, stop=True,
                                  skip_group_check=True).then_inc(s_filled, 1)
                    o = s.take()
                    pe.wait_ge(s_freed, s.free())
                    ov = o[:, 0:2 * BC].rearrange("p (n k) -> p n k", n=2)
                    pe.matmul(ov[:, :, 0:P], identb[:], mask[:, 1:2, :].to_broadcast([P, 2, P]), start=True, stop=True,
                              skip_group_check=True)
                    for n, pr in enumerate(pairs):
                        mm = pe.matmul(ov[:, n, :], kT[u][r:r + STK, pr, P:2 * P].bitcast(F32R),
                                       qT[u][r:r + STK, pr, P:LE].bitcast(F32R), start=False, stop=True,
                                       skip_group_check=True)
                    mm.then_inc(s_filled, 1)
                at["probs", g] = s.n

            def attend(u, g):
                pe.wait_ge(s_freed, s.read(at["probs", g]))
                pb = probs[(NG * u + g) % 2]
                o = v.take()
                pe.wait_ge(v_freed, v.free())
                for kt, c0, src in ((0, 0, pb[:, :, 0:LE]), (1, P, pb[:, :, AC:PTC]), (2, 2 * P, pb[:, :, LE:AC])):
                    for j in range(GROUP):
                        mm = pe.matmul(o[32 * j:32 * j + 32, c0:LE], vaug[u][:, kt, g * GROUP + j, :], src[:, j, :],
                                       start=(kt == 0), stop=(kt == 2))
                mm.then_inc(v_filled, 1)
                at["oT"] = v.n

            def out_T(u):
                pe.wait_ge(v_freed, v.read(at["oT"]))
                for t in range(QT):
                    o = v.take()
                    pe.wait_ge(v_freed, v.free())
                    for g in range(NG):
                        mm = pe.transpose(o[:, g * P:g * P + P], oT[u][:, g, t * P:t * P + P], ident[:])
                    mm.then_inc(v_filled, 1)
                at["on"] = v.n

            def norm_T(u):
                pe.wait_ge(v_freed, v.read(at["on"]))
                ta = s.take()
                pe.wait_ge(s_freed, s.free())
                for t in range(QT):
                    mm = pe.transpose(ta[:, t * P:t * P + P], on[u][:, t, 0:P], ident[:])
                mm.then_inc(s_filled, 1)
                tb = s.take()
                pe.wait_ge(s_freed, s.free())
                pe.sem_inc(carried, 1)
                for t in range(QT):
                    mm = pe.transpose(tb[0:DB, t * P:t * P + P], on[u][:, t, P:D], ident[:])
                mm.then_inc(s_filled, 1)
                at["onT"] = s.n

            def project(u):
                pe.wait_ge(s_freed, s.read(at["onT"]))
                for t in range(QT):
                    o = v.take()
                    pe.wait_ge(v_freed, v.free())
                    pe.matmul(o[:, 0:D], onTa[u][:, t * P:t * P + P], wa[:, 3, :], start=True, stop=False)
                    pe.matmul(o[:, 0:D], onTb[u][:, t * P:t * P + P], wb[:, 3, :], start=False, stop=True
                              ).then_inc(v_filled, 1)

            def period(b, u, prepare=True, transpose=True):
                w = 1 - u
                maxima(u, MIDDLE_MAXES[:3])
                if prepare:
                    pe.wait_ge(s_freed, s.read())
                    values(w, (0, 1))
                maxima(u, MIDDLE_MAXES[3:])
                if prepare:
                    values(w, (2,))
                    queries_keys(w, 0)
                q_T_again(b, u)
                if prepare:
                    queries_keys(w, 1)
                scores(u, 0)
                if prepare:
                    queries_keys(w, 2)
                scores(u, 1)
                attend(u, 0)
                scores(u, 2)
                attend(u, 1)
                if prepare:
                    pairs_in(b + 1, w, [0])
                attend(u, 2)
                if prepare:
                    pairs_in(b + 1, w, [1, 2])
                out_T(u)
                if prepare:
                    pairs_in(b + 1, w, [3, 4])
                norm_T(u)
                if prepare:
                    pairs_in(b + 1, w, [5])
                if transpose:
                    layer_in(b + 2, u)
                if prepare:
                    pe.wait_ge(s_freed, s.read(at["qk", PAIRS - 1]))
                    maxima(w, LAST_MAXES[-1])
                    maxima(w, FIRST_MAXES)
                project(u)

            layer_in(0, 0)
            pe.wait_ge(s_freed, s.read())
            for t in range(QT):
                queries_keys(0, t)
            values(0, (0, 1))
            values(0, (2,))
            pairs_in(0, 0, range(PAIRS))
            layer_in(1, 1)
            pe.wait_ge(s_freed, s.read(at["qk", PAIRS - 1]))
            maxima(0, LAST_MAXES[-1])
            maxima(0, FIRST_MAXES)
            assert v.n == V_FIRST
            with pe.Fori(0, BODIES) as i:
                v.enter(i)
                s.enter(i)
                period(2 * i, 0)
                period(2 * i + 1, 1)
            v.leave(BODIES)
            s.leave(BODIES)
            period(B - 2, 0, transpose=False)
            period(B - 1, 1, prepare=False, transpose=False)

        @block.scalar
        def _(act):
            act.sem_inc(s_freed, RING)
            s = Ring(sbank, SN)

            def two_parts(ta, tb):
                for dst, rows in ((ta, P), (tb, DB)):
                    o = s.take()
                    act.wait_ge(s_filled, s.filled())
                    act.copy(dst[0:rows, :], o[0:rows, 0:LP]).then_inc(s_freed, 1)

            def values(u, t0, n):
                o = s.take()
                act.wait_ge(s_filled, s.filled())
                act.copy(vaug[u][:, t0:t0 + n, :, 0:HD],
                         o[:, 0:n * D].rearrange("p (t h d) -> p t h d", t=n, h=HEADS)).then_inc(s_freed, 1)

            def stacks(pairs, *dsts):
                for p in pairs:
                    for dst in dsts:
                        o = s.take()
                        act.wait_ge(s_filled, s.filled())
                        act.copy(dst[:, p, :].bitcast(F32R), o[:, 0:LP].bitcast(F32R)).then_inc(s_freed, 1)

            def exps(u, g):
                pb = probs[(NG * u + g) % 2]
                for j in range(2):
                    for n in range(2):
                        o = s.take()
                        act.wait_ge(s_filled, s.filled())
                        act.activation(pb[:, 2 * n + j, 0:AC], o[:, 0:AC], ACT.Exp).then_inc(s_freed, 1)
                    o = s.take()
                    act.wait_ge(s_filled, s.filled())
                    act.activation(pb[:, j:j + 3:2, AC:PTC],
                                   o[:, 0:2 * BC].rearrange("p (n k) -> p n k", n=2), ACT.Exp).then_inc(s_freed, 1)

            def period(u, prepare=True, transpose=True):
                w = 1 - u
                if prepare:
                    values(w, 0, 2)
                    values(w, 2, 1)
                stacks(range(PAIRS), qT[u])
                exps(u, 0)
                exps(u, 1)
                exps(u, 2)
                if prepare:
                    stacks(range(0, 5), qT[w], kT[w])
                two_parts(onTa[u], onTb[u])
                if prepare:
                    stacks([5], qT[w], kT[w])
                if transpose:
                    two_parts(xTa[u], xTb[u])

            two_parts(xTa[0], xTb[0])
            values(0, 0, 2)
            values(0, 2, 1)
            stacks(range(PAIRS), qT[0], kT[0])
            two_parts(xTa[1], xTb[1])
            with act.Fori(0, BODIES) as i:
                s.enter(i)
                period(0)
                period(1)
            s.leave(BODIES)
            period(0, transpose=False)
            period(1, prepare=False, transpose=False)

        @block.vector
        def _(dve):
            dve.sem_inc(v_freed, RING)
            for u in range(2):
                dve.sem_inc(h2_stored[u], 32)
            for u in range(2):
                dve.memset(hb[u][:, 2, :], 0.0).then_inc(padded, 1)
            for u in range(2):
                dve.memset(xTb[u][DB:DB + 1, :], 1.0).then_inc(init_done, 1)
                dve.memset(onTb[u][DB:DB + 1, :], 1.0).then_inc(init_done, 1)
                dve.memset(stk[u][:, :, :, MROW:STK], 0.0).then_inc(init_done, 1)
                dve.memset(vaug[u][:, :, :, HD:32], 0.0).then_inc(init_done, 1)
                dve.memset(oT[u][:, :, LE:LP], 1.0).then_inc(init_done, 1)
            dve.wait_ge(init_done, 11)
            for u in range(2):
                dve.memset(stk[u][:, :, HEADS:, MROW:MROW + 2], 1.0).then_inc(init_done, 1)
                dve.memset(vaug[u][:, :, :, HD:HD + 1], 1.0).then_inc(init_done, 1)
            dve.wait_ge(init_done, N_INIT)
            v = Ring(vbank, VN)
            chained = Count(VSTEPS)

            def link(ins):
                chained.n += 1
                ins.then_inc(vec_step, 1)
                dve.wait_ge(vec_step, chained.value())

            def layernorm(u, loads):
                dve.wait_ge(h_in[u], 32 * loads)
                for t in range(QT):
                    ins = dve.bn_stats(stats[u][:, t, :], hb[u][:, t, :])
                link(ins)
                dve.sem_inc(carried, 1)
                for t in range(QT):
                    ins = dve.bn_aggr(mv[u][:, t, :], stats[u][:, t, :])
                link(ins)
                dve.tensor_scalar(var[u][:], mv[u][:, :, 1], LN_EPS, None, ALU.add).then_inc(var_ready, 1)

            def normalize(b, u):
                dve.wait_ge(rstd_ready, b + 1)
                for t in range(QT):
                    ins = dve.tensor_scalar(xn[u][:, t, :], hb[u][:, t, :], mv[u][:, t, 0:1], rstd[u][:, t:t + 1],
                                            ALU.subtract, ALU.mult)
                ins.then_inc(xn_ready, 1)

            def rotate(u):
                for t in range(QT):
                    rot = rots[(u * QT + t) % 2]
                    o = v.take()
                    dve.wait_ge(v_filled, v.filled())
                    qk = o[:, 0:2 * D].rearrange("p (h d) -> p h d", d=HD)

                    def table(c0, n):
                        return rope[:, t:t + 1, c0:c0 + n].to_broadcast([P, 2 * HEADS, n])

                    dve.tensor_tensor(rot[:, 0], qk, table(0, HD), ALU.mult)
                    dve.tensor_tensor(rot[:, 1, :, 0:HD // 2], qk[:, :, HD // 2:HD], table(HD, HD // 2), ALU.mult)
                    dve.tensor_tensor(rot[:, 1, :, HD // 2:HD], qk[:, :, 0:HD // 2], table(HD + HD // 2, HD // 2),
                                      ALU.mult).then_inc(v_freed, 1)
                    dve.wait_ge(v_freed, v.read())
                    link(dve.tensor_tensor(rot[:, 0], rot[:, 0], rot[:, 1], ALU.add))
                    link(dve.tensor_copy(stk[u][:, t, :, 0:HD].bitcast(F32R), rot[:, 0]))
                    dve.tensor_tensor(stk[u][:, t, 0:HEADS, HD:2 * HD].bitcast(F32R), rot[:, 0, 0:HEADS],
                                      stk[u][:, t, 0:HEADS, 0:HD], ALU.subtract)
                    dve.tensor_tensor(stk[u][:, t, HEADS:, 2 * HD:3 * HD].bitcast(F32R), rot[:, 0, HEADS:],
                                      stk[u][:, t, HEADS:, 0:HD], ALU.subtract).then_inc(rope_ready, 1)

            def maxima(u, tiles):
                for t, h0, n, keys in tiles:
                    o = v.take()
                    dve.wait_ge(v_filled, v.filled())
                    dve.tensor_reduce(mx[u][:, t, h0:h0 + 2 * n - 1:2], o[:, 0:n * keys].rearrange("p (n k) -> p n k", n=n),
                                      AX.X, ALU.max).then_inc(v_freed, 1)

            def put_maxima(u):
                dve.wait_ge(v_freed, v.read())
                hi, lo = stk[u][:, :, 0:HEADS, MROW], stk[u][:, :, 0:HEADS, MROW + 1]
                link(dve.tensor_scalar(hi.bitcast(F32R), mx[u][:], -1.0, None, ALU.mult))
                dve.scalar_tensor_tensor(lo.bitcast(F32R), mx[u][:], -1.0, hi, ALU.mult, ALU.subtract
                                         ).then_inc(max_ready, 1)

            def attended(u, g):
                o = v.take()
                dve.wait_ge(v_filled, v.filled())
                dve.tensor_copy(oT[u][:, g, 0:LE], o[:, 0:LE]).then_inc(v_freed, 1)

            def divide(u):
                for t in range(QT):
                    o = v.take()
                    dve.wait_ge(v_filled, v.filled())
                    ov = o[:, 0:NG * P].rearrange("p (h d) -> p h d", d=32)
                    link(dve.reciprocal(rden[u][:, t, :], ov[:, :, HD]))
                    dve.tensor_tensor(on[u][:, t, :].rearrange("p (h d) -> p h d", d=HD), ov[:, :, 0:HD],
                                      rden[u][:, t, :].unsqueeze(2).to_broadcast([P, HEADS, HD]), ALU.mult
                                      ).then_inc(v_freed, 1)

            def residual(u, batch2):
                dve.wait_ge(h2_stored[u], 32 * (batch2 + 1))
                dve.wait_ge(hr_in[u], 32 * (batch2 + 1))
                for t in range(QT):
                    r = P if t < 2 else LAST
                    o = v.take()
                    dve.wait_ge(v_filled, v.filled())
                    dve.tensor_tensor(h2[u][0:r, t, :], o[0:r, 0:D], hr[u][0:r, t, :], ALU.add).then_inc(v_freed, 1)

            def period(b, u, batch2, prepare=True, transpose=True):
                w = 1 - u
                maxima(u, MIDDLE_MAXES)
                put_maxima(u)
                if prepare:
                    rotate(w)
                if transpose:
                    layernorm(u, batch2 + 2)
                attended(u, 0)
                attended(u, 1)
                if transpose:
                    normalize(b + 2, u)
                attended(u, 2)
                if prepare:
                    maxima(w, LAST_MAXES[0])
                    maxima(w, LAST_MAXES[1])
                divide(u)
                if prepare:
                    maxima(w, LAST_MAXES[2])
                if prepare:
                    for p in range(3, PAIRS):
                        maxima(w, LAST_MAXES[p])
                    maxima(w, FIRST_MAXES)
                residual(u, batch2)

            layernorm(0, 1)
            layernorm(1, 1)
            normalize(0, 0)
            normalize(1, 1)
            rotate(0)
            for p in range(PAIRS):
                maxima(0, LAST_MAXES[p])
            maxima(0, FIRST_MAXES)
            with dve.Fori(0, BODIES) as i:
                v.enter(i)
                chained.enter(i)
                period(2 * i, 0, i)
                period(2 * i + 1, 1, i)
            v.leave(BODIES)
            chained.leave(BODIES)
            period(B - 2, 0, BODIES, transpose=False)
            period(B - 1, 1, BODIES, prepare=False, transpose=False)


HALF = N_EXP // 2
EC = B * SLOTS_PER
EC1 = EC + 1


def dispatch_phase(nc, xsTa, xsTb, h2_d, phis, ln_g, ln_b, c_ident, e2_d):
    VRING = 3
    with ExitStack() as ctx:
        a = Alloc(nc, ctx, "di")
        ident = a.sb("ident", [P, P])
        phAh, phAl, phBs, phBl = phis
        gTa = a.sb("gTa", [P, N_EXP])
        gTb = a.sb("gTb", [P, HALF])
        gb_in = a.sb("gb_in", [N_EXP, 2, 2, D])
        half = a.sb("half", [P, ST])
        hb = [a.sb(f"hb{u}", [P, QT, D]) for u in range(2)]
        stats = a.sb("stats", [P, ST, 6])
        mv = [a.sb(f"mv{u}", [P, QT, 2]) for u in range(2)]
        var = [a.sb(f"var{u}", [P, QT]) for u in range(2)]
        rstd = [a.sb(f"rstd{u}", [P, QT]) for u in range(2)]
        xn = [a.sb(f"xn{u}", [P, QT, D + 1]) for u in range(2)]
        xAh = a.sb("xAh", [P, LP])
        xAl = a.sb("xAl", [P, LP])
        xBs = a.sb("xBs", [P, LP])
        lg = [a.sb(f"lg{u}", [P, QT, S]) for u in range(2)]
        nmt = [a.sb(f"nmt{u}", [P, QT]) for u in range(2)]
        nms = [a.sb(f"nms{u}", [P, ST]) for u in range(2)]
        e2T = a.sb("e2T", [P, ST, L])
        e1T = a.sb("e1T", [P, ST, L])
        e1 = a.sb("e1", [P, QT, S])
        xs = [a.sb(f"xs{u}", [P, ST, D + 1]) for u in range(2)]
        smv = a.sb("smv", [P, ST, 2])
        ssq = a.sb("ssq", [P, ST])
        svar = a.sb("svar", [P, ST])
        srstd = a.sb("srstd", [P, ST])
        xsn = a.sb("xsn", [P, ST, D])
        vbank = [a.bank(f"vbank{i}") for i in range(VRING)]
        mbank = a.bank("mbank")
        mrows = a.sb("mrows", [P, L])
        sbank = [a.bank(f"sbank{i}") for i in range(RING)]

        consts_in = a.sem("consts_in")
        init_done = a.sem("init_done")
        setup_mm = a.sem("setup_mm")
        setup_step = a.sem("setup_step")
        v_filled, v_freed = a.sem("v_filled"), a.sem("v_freed")
        s_filled, s_freed = a.sem("s_filled"), a.sem("s_freed")
        vec_step = a.sem("vec_step")
        carried = a.sem("carried")
        h_in = [a.sem(f"h_in{u}") for u in range(2)]
        var_ready = a.sem("var_ready")
        rstd_ready = a.sem("rstd_ready")
        xn_ready = a.sem("xn_ready")
        token_max = a.sem("token_max")
        max_rows = a.sem("max_rows")
        mrows_ready = a.sem("mrows_ready")
        shifted = a.sem("shifted")
        e2_ready = a.sem("e2_ready")
        high_ready = a.sem("high_ready")
        e2_stored = [a.sem(f"e2_stored{k}") for k in range(2)]
        svar_ready = a.sem("svar_ready")
        srstd_ready = a.sem("srstd_ready")
        xsn_ready = [a.sem(f"xsn_ready{k}") for k in range(2)]
        block = ctx.enter_context(nc.Block())

        N_CONST = 5
        N_INIT = 5
        BODIES = (B - 2) // 2
        VN, SN = 12, 48
        V_FIRST, S_FIRST = 6, 30
        MIXED = [("T", 0), ("T", 1), ("L", 0), ("L", 1), ("T", 2), ("T", 3), ("L", 2),
                 ("T", 4), ("L", 3), ("T", 5), ("T", 6), ("L", 4), ("T", 7), ("L", 5)]
        ALONE = [("T", t) for t in range(ST)]
        POOL_TILES = 3
        SPLIT = 9
        S_PERIOD = SN // 2
        L_IN = len(MIXED)
        VSTEPS = 10

        @block.sync
        def _(sp):
            sp.wait_ge(init_done, N_INIT)
            h2d = h2_d.rearrange("(i u) l d -> u i l d", u=2)
            e2d = e2_d.rearrange("(i u) p c -> u i p c", u=2)

            def load(u, b2):
                sp.dma_start(hb[u][:, 0:2, :], h2d[u, b2, 0:2 * P].rearrange("(t p) d -> p t d", p=P)).then_inc(h_in[u], 16)
                sp.dma_start(hb[u][0:LAST, 2, :], h2d[u, b2, 2 * P:L]).then_inc(h_in[u], 16)

            def period(b, u, b2, load_b2):
                for k in range(2):
                    sp.wait_ge(e2_ready, 2 * b + k + 1)
                    sp.dma_start(e2d[u, b2, :, ST // 2 * L * k:ST // 2 * L * (k + 1)],
                                 e2T[:, ST // 2 * k:ST // 2 * (k + 1), :].rearrange("p t c -> p (t c)")
                                 ).then_inc(e2_stored[k], 16)
                if load_b2 is not None:
                    sp.wait_ge(xn_ready, b + 3)
                    load(u, load_b2)

            load(0, 0)
            load(1, 0)
            sp.dma_start(ident[:], c_ident).then_inc(consts_in, 16)
            sp.dma_start(gb_in[:, 0, 0, :], ln_g).then_inc(consts_in, 16)
            sp.dma_start(gb_in[:, 1, 0, :], ln_b).then_inc(consts_in, 16)
            for k, w in enumerate((ln_g, ln_b)):
                sp.dma_start(gb_in[0:HALF, k, 1, :], w[HALF:, :]).then_inc(consts_in, 16)
            for u in range(2):
                sp.wait_ge(xn_ready, u + 1)
                load(u, 1)
            period(0, 0, 0, 2)
            with sp.Fori(0, BODIES) as i:
                period(2 * i + 1, 1, i, (i + 2) % (B // 2))
                period(2 * i + 2, 0, i + 1, (i + 3) % (B // 2))
            period(B - 1, 1, B // 2 - 1, None)
            for k in range(2):
                sp.wait_ge(e2_stored[k], 16 * (1 + B))
            for u, loads in enumerate((B // 2 + 2, B // 2 + 1)):
                sp.wait_ge(h_in[u], 32 * loads)

        @block.gpsimd
        def _(pool):
            pool.memset(half[:], -0.5).then_inc(init_done, 1)
            pool.wait_ge(init_done, N_INIT)
            def of_tokens(b, u):
                pool.wait_ge(var_ready, b + 1)
                pool.tensor_tensor(rstd[u][:], var[u][:], half[:, 0:QT], ALU.pow).then_inc(rstd_ready, 1)

            def of_slots(b, u):
                pool.wait_ge(svar_ready, b + 1)
                pool.tensor_tensor(srstd[:], svar[:], half[:, 0:ST], ALU.pow).then_inc(srstd_ready, 1)
                pool.wait_ge(srstd_ready, b + 1)
                pool.sem_inc(carried, 1)
                for t in range(POOL_TILES):
                    ins = pool.tensor_scalar(xsn[:, t, :], xs[u][:, t, 0:D], smv[:, t, 0:1], srstd[:, t:t + 1],
                                             ALU.subtract, ALU.mult)
                ins.then_inc(xsn_ready[0], 1)

            of_tokens(0, 0)
            of_tokens(1, 1)
            of_tokens(2, 0)
            with pool.Fori(0, BODIES) as i:
                for u in range(2):
                    of_slots(2 * i + u, u)
                    of_tokens(2 * i + u + 3, 1 - u)
            of_slots(B - 2, 0)
            of_slots(B - 1, 1)

        @block.tensor
        def _(pe):
            pe.wait_ge(consts_in, 16 * N_CONST)
            for k in range(2):
                pe.transpose(sbank[2 + k][:, 0:N_EXP], gb_in[:, k, 0, 0:P], ident[0:N_EXP, 0:N_EXP])
                pe.transpose(sbank[2 + k][0:DB, P:P + HALF], gb_in[0:HALF, k, 0, P:D], ident[0:HALF, 0:HALF])
                pe.transpose(sbank[2 + k][:, 2 * P:2 * P + HALF], gb_in[0:HALF, k, 1, D - P:D], ident[0:HALF, 0:HALF]
                             ).then_inc(setup_mm, 1)
            pe.wait_ge(setup_step, 6)
            pe.wait_ge(init_done, N_INIT)
            v = Ring(vbank, VN)
            s = Ring(sbank, SN)

            def tokens_T(b, u):
                pe.wait_ge(xn_ready, b + 1)
                oa = v.take()
                ob = v.take()
                pe.wait_ge(v_freed, v.free())
                for t in range(QT):
                    mm = pe.transpose(oa[:, t * P:t * P + P], xn[u][:, t, 0:P], ident[:])
                mm.then_inc(v_filled, 1)
                for t in range(QT):
                    mm = pe.transpose(ob[0:DB, t * P:t * P + P], xn[u][:, t, P:D], ident[:])
                mm.then_inc(v_filled, 1)

            def rows_T(o, src, t0):
                for t in range(QT):
                    r = P if t < 2 else LAST
                    mm = pe.transpose(o[:, t * P:t * P + r], src[0:r, t, t0:t0 + P], ident[0:r, 0:r])
                return mm

            def logits(u, pieces):
                for kind, n in pieces:
                    o = s.take()
                    if kind == "T":
                        pe.wait_ge(s_freed, s.free())
                        rows_T(o, lg[u], n * P).then_inc(s_filled, 1)
                    else:
                        if n == 0:
                            pe.wait_ge(v_freed, v.value(VRING))
                        c, k = slice(n // 2 * P, n // 2 * P + P), slice(n % 2 * 512, n % 2 * 512 + 512)
                        pe.wait_ge(s_freed, s.free())
                        terms = ((xAh[:, c], phAh[:, k]), (xAl[:, c], phAh[:, k]), (xAh[:, c], phAl[:, k]),
                                 (xBs[:, c], phBs[:, k]), (xBs[0:DB, c], phBl[:, k]))
                        for j, (x, ph) in enumerate(terms):
                            mm = pe.matmul(o[:], x.bitcast(F32R), ph.bitcast(F32R), start=(j == 0),
                                           stop=(j == len(terms) - 1))
                        mm.then_inc(s_filled, 1)

            def maxima_rows(b, u, first=False):
                pe.wait_ge(token_max, QT * (b + 1))
                if not first:
                    pe.wait_ge(mrows_ready, b)
                for t in range(QT):
                    r = P if t < 2 else LAST
                    mm = pe.transpose(mbank[:, t * P:t * P + r], nmt[u][0:r, t:t + 1].to_broadcast([r, P]), ident[0:r, 0:r])
                mm.then_inc(max_rows, 1)

            def e1_back(e1T_read):
                pe.wait_ge(s_freed, e1T_read)
                for k in range(2):
                    for t in range(QT):
                        r = P if t < 2 else LAST
                        o = s.take()
                        pe.wait_ge(s_freed, s.free())
                        for j in range(4):
                            mm = pe.transpose(o[0:r, j * P:j * P + P], e1T[:, 4 * k + j, t * P:t * P + r], ident[:])
                        mm.then_inc(s_filled, 1)

            def slot_inputs(u, pairs, e1_half):
                for k in pairs:
                    if k % 2 == 0:
                        pe.wait_ge(s_freed, e1_half[k // 2])
                    o = s.take()
                    pe.wait_ge(s_freed, s.free())
                    for j in range(2):
                        st = 2 * k + j
                        for t in range(QT):
                            r = P if t < 2 else LAST
                            mm = pe.matmul(o[:, j * (D + 1):(j + 1) * (D + 1)], e1[0:r, t, st * P:st * P + P],
                                           xn[u][0:r, t, :], start=(t == 0), stop=(t == QT - 1))
                    mm.then_inc(s_filled, 1)

            def slots_T(b, k):
                pe.wait_ge(xsn_ready[k], b + 1)
                oa = v.take()
                ob = v.take()
                pe.wait_ge(v_freed, v.free())
                for j in range(4):
                    mm = pe.transpose(oa[:, j * P:j * P + P], xsn[:, 4 * k + j, 0:P], ident[:])
                mm.then_inc(v_filled, 1)
                for j in range(4):
                    if k == 0:
                        mm = pe.transpose(ob[0:DB, j * P:j * P + P], xsn[:, j, P:D], ident[:])
                    else:
                        mm = pe.transpose(ob[:, j * P:j * P + P], xsn[:, 4 + j, D - P:D], ident[:])
                mm.then_inc(v_filled, 1)

            def period(b, u, first=False, last=False):
                pe.wait_ge(s_freed, s.read() if first else s.value(RING + L_IN - S_PERIOD))
                logits(u, ALONE if last else MIXED)
                e1T_read = s.read()
                e1_back(e1T_read)
                e1_half = s.read(s.n - QT), s.read()
                slot_inputs(u, range(0, 3), e1_half)
                if not first:
                    slots_T(b - 1, 1)
                slot_inputs(u, [3], e1_half)
                if not last:
                    maxima_rows(b + 1, 1 - u)
                if not first:
                    slots_T(b - 1, 0)
                if not last:
                    tokens_T(b + 2, u)

            tokens_T(0, 0)
            logits(1, [("L", n) for n in range(2 * QT)])
            maxima_rows(0, 0, first=True)
            tokens_T(1, 1)
            period(0, 0, first=True)
            assert (v.n, s.n) == (V_FIRST, S_FIRST)
            with pe.Fori(0, BODIES) as i:
                v.enter(i)
                s.enter(i)
                period(2 * i + 1, 1)
                period(2 * i + 2, 0)
            v.leave(BODIES)
            s.leave(BODIES)
            period(B - 1, 1, last=True)
            slots_T(B - 1, 1)
            slots_T(B - 1, 0)

        @block.scalar
        def _(act):
            act.sem_inc(s_freed, RING)
            s = Ring(sbank, SN)
            v = Ring(vbank, VN)

            def high_parts():
                for dst, r in ((xAh, P), (xBs, DB)):
                    o = v.take()
                    act.wait_ge(v_filled, v.filled())
                    act.copy(dst[0:r, :].bitcast(F32R), o[0:r, 0:LP]).then_inc(high_ready, 1)

            def logits(b, u, pieces):
                for kind, n in pieces:
                    o = s.take()
                    if kind == "T":
                        act.wait_ge(shifted, ST * b + n + 1)
                        act.activation(e1T[:, n, :], o[:, 0:L], ACT.Exp, bias=nms[u][:, n:n + 1]).then_inc(s_freed, 1)
                    else:
                        t, k = n // 2, n % 2
                        act.wait_ge(s_filled, s.filled())
                        act.copy(lg[1 - u][:, t, 512 * k:512 * k + 512], o[:]).then_inc(s_freed, 1)

            def over_slots(k):
                half_e2T = e2T[:, ST // 2 * k:ST // 2 * (k + 1), :]
                act.activation(half_e2T, half_e2T, ACT.Exp).then_inc(e2_ready, 1)

            def maxima_rows(b):
                act.wait_ge(max_rows, b + 1)
                act.copy(mrows[:], mbank[:, 0:L]).then_inc(mrows_ready, 1)

            def e1_back():
                for k in range(2):
                    for t in range(QT):
                        r = P if t < 2 else LAST
                        o = s.take()
                        act.wait_ge(s_filled, s.filled())
                        act.copy(e1[0:r, t, 512 * k:512 * k + 512], o[0:r, :]).then_inc(s_freed, 1)

            def slot_inputs(u):
                for k in range(ST // 2):
                    o = s.take()
                    act.wait_ge(s_filled, s.filled())
                    act.copy(xs[u][:, 2 * k:2 * k + 2, :], o[:, 0:2 * (D + 1)].rearrange("p (t d) -> p t d", t=2)
                             ).then_inc(s_freed, 1)

            def period(b, u, first=False, last=False):
                pieces = ALONE if last else MIXED
                logits(b, u, pieces[:SPLIT])
                over_slots(0)
                logits(b, u, pieces[SPLIT:])
                e1_back()
                over_slots(1)
                slot_inputs(u)
                if not first:
                    v.n += 4
                if not last:
                    maxima_rows(b + 1)
                    high_parts()

            high_parts()
            logits(-1, 1, [("L", n) for n in range(2 * QT)])
            maxima_rows(0)
            high_parts()
            period(0, 0, first=True)
            with act.Fori(0, BODIES) as i:
                s.enter(i)
                v.enter(i)
                period(2 * i + 1, 1)
                period(2 * i + 2, 0)
            s.leave(BODIES)
            v.leave(BODIES)
            period(B - 1, 1, last=True)

        @block.vector
        def _(dve):
            dve.sem_inc(v_freed, VRING)
            for k in range(2):
                dve.sem_inc(e2_stored[k], 16)
            for u in range(2):
                dve.memset(hb[u][:, 2, :], 0.0).then_inc(init_done, 1)
                dve.memset(xn[u][:, :, D:D + 1], 1.0).then_inc(init_done, 1)
            v = Ring(vbank, VN)
            s = Ring(sbank, SN)
            chained = Count(VSTEPS)

            def link(ins):
                chained.n += 1
                ins.then_inc(vec_step, 1)
                dve.wait_ge(vec_step, chained.value())

            def layernorm(u, loads):
                dve.wait_ge(h_in[u], 32 * loads)
                for t in range(QT):
                    ins = dve.bn_stats(stats[:, t, :], hb[u][:, t, :])
                link(ins)
                dve.sem_inc(carried, 1)
                for t in range(QT):
                    ins = dve.bn_aggr(mv[u][:, t, :], stats[:, t, :])
                link(ins)
                dve.tensor_scalar(var[u][:], mv[u][:, :, 1], LN_EPS, None, ALU.add).then_inc(var_ready, 1)

            def normalize(b, u):
                dve.wait_ge(rstd_ready, b + 1)
                for t in range(QT):
                    ins = dve.tensor_scalar(xn[u][:, t, 0:D], hb[u][:, t, :], mv[u][:, t, 0:1], rstd[u][:, t:t + 1],
                                            ALU.subtract, ALU.mult)
                ins.then_inc(xn_ready, 1)

            def low_parts(b):
                for j, (dst, high) in enumerate(((xAl[:], xAh[:]), (xBs[DB:P, :], xBs[0:DB, :]))):
                    o = v.take()
                    dve.wait_ge(high_ready, 2 * b + j + 1)
                    dve.tensor_tensor(dst.bitcast(F32R), o[0:high.shape[0], 0:LP], high, ALU.subtract
                                      ).then_inc(v_freed, 1)

            def token_maxima(u, lg_ready):
                dve.wait_ge(s_freed, lg_ready)
                for t in range(QT):
                    dve.tensor_reduce(nmt[u][:, t:t + 1], lg[u][:, t, :], AX.X, ALU.max, negate=True
                                      ).then_inc(token_max, 1)

            def slot_maxima(b, u, pieces):
                for kind, n in pieces:
                    o = s.take()
                    if kind == "T":
                        dve.wait_ge(s_filled, s.filled())
                        dve.tensor_reduce(nms[u][:, n:n + 1], o[:, 0:L], AX.X, ALU.max, negate=True)
                        if n == 0:
                            dve.wait_ge(mrows_ready, b + 1)
                        if n % (ST // 2) == 0:
                            dve.wait_ge(e2_stored[n // (ST // 2)], 16 * (b + 1))
                        dve.tensor_tensor(e2T[:, n, :], o[:, 0:L], mrows[:], ALU.add).then_inc(shifted, 1)

            def slot_statistics(u, xs_ready):
                dve.wait_ge(s_freed, xs_ready)
                for t in range(ST):
                    ins = dve.bn_stats(stats[:, t, :], xs[u][:, t, 0:D])
                link(ins)
                dve.sem_inc(carried, 1)
                for t in range(ST):
                    ins = dve.bn_aggr(smv[:, t, :], stats[:, t, :])
                link(ins)
                link(dve.tensor_tensor(ssq[:], xs[u][:, :, D], xs[u][:, :, D], ALU.mult))
                dve.scalar_tensor_tensor(svar[:], ssq[:], LN_EPS, smv[:, :, 1], ALU.mult, ALU.add
                                         ).then_inc(svar_ready, 1)

            def slot_scale(b, u):
                dve.wait_ge(srstd_ready, b + 1)
                for t in range(POOL_TILES, ST):
                    ins = dve.tensor_scalar(xsn[:, t, :], xs[u][:, t, 0:D], smv[:, t, 0:1], srstd[:, t:t + 1],
                                            ALU.subtract, ALU.mult)
                ins.then_inc(xsn_ready[1], 1)

            def slots_T(b, k):
                c = bass.ds(b * SLOTS_PER, SLOTS_PER)
                for dst, g, r0, r1 in (
                    (xsTa[:, HALF * k:HALF * k + HALF, c], gTa[:, HALF * k:HALF * k + HALF], 0, P),
                    (xsTb[DB * k:DB * k + DB, :, c], gTb[DB * k:DB * k + DB, :], DB * k, DB * k + DB),
                ):
                    o = v.take()
                    dve.wait_ge(v_filled, v.filled())
                    dve.tensor_tensor(dst, o[r0:r1, :].rearrange("d (n p) -> d n p", n=HALF),
                                      g.unsqueeze(2).to_broadcast([r1 - r0, HALF, SLOTS_PER]), ALU.mult
                                      ).then_inc(v_freed, 1)

            def period(b, u, loads, first=False, last=False):
                xs_ready = s.read()
                low_parts(b + 1)
                slot_maxima(b, u, ALONE if last else MIXED)
                lg_ready = s.read()
                if not first:
                    slot_statistics(1 - u, xs_ready)
                if not last:
                    token_maxima(1 - u, lg_ready)
                if not first:
                    slot_scale(b - 1, 1 - u)
                if not last:
                    layernorm(u, loads)
                s.n = s.n + 2 * QT + ST // 2
                if not first:
                    slots_T(b - 1, 1)
                if not last:
                    dve.wait_ge(s_filled, s.filled())
                    normalize(b + 2, u)
                if not first:
                    slots_T(b - 1, 0)

            layernorm(0, 1)
            layernorm(1, 1)
            normalize(0, 0)
            dve.wait_ge(setup_mm, 2)
            for dst, col, k in ((gTa[:], (0, N_EXP), 0), (xsTa[:, :, EC], (0, N_EXP), 1)):
                dve.tensor_copy(dst, sbank[2 + k][:, col[0]:col[1]]).then_inc(setup_step, 1)
            for dst, k in ((gTb, 0), (xsTb[:, :, EC], 1)):
                dve.tensor_copy(dst[0:DB, :], sbank[2 + k][0:DB, P:P + HALF]).then_inc(setup_step, 1)
                dve.tensor_copy(dst[DB:P, :], sbank[2 + k][DB:P, 2 * P:2 * P + HALF]).then_inc(setup_step, 1)
            low_parts(0)
            s.n = 2 * QT
            token_maxima(0, s.read())
            normalize(1, 1)
            period(0, 0, 2, first=True)
            with dve.Fori(0, BODIES) as i:
                v.enter(i)
                s.enter(i)
                chained.enter(i)
                period(2 * i + 1, 1, i + 2)
                period(2 * i + 2, 0, i + 3)
            v.leave(BODIES)
            s.leave(BODIES)
            chained.leave(BODIES)
            period(B - 1, 1, None, last=True)
            slot_statistics(1, s.read())
            slot_scale(B - 1, 1)
            slots_T(B - 1, 1)
            slots_T(B - 1, 0)


def expert_phase(nc, xsTa, xsTb, w1, b1, w2, b2, c_ident, ys_d, ahead, e2_d, h2_d):
    with ExitStack() as ctx:
        a = Alloc(nc, ctx, "ex")
        NB = 4
        ident = a.sb("ident", [P, P])
        b1_in = a.sb("b1_in", [N_EXP, HID])
        b1T = a.sb("b1T", [P, HT, N_EXP])
        w1a = [a.sb(f"w1a{j}", [P, HID]) for j in range(NB)]
        w1b = [a.sb(f"w1b{j}", [P, HID]) for j in range(NB)]
        wAh, wAl, wBs, wBl = ([a.sb(f"{n}{j}", [P, HID]) for j in range(NB)] for n in ("wAh", "wAl", "wBs", "wBl"))
        xAh, xAl, xBs = ([a.sb(f"{n}{j}", [P, EC]) for j in range(NB)] for n in ("xAh", "xAl", "xBs"))
        w2s = [a.sb(f"w2s{j}", [P, HT, D]) for j in range(NB)]
        b2s = [a.sb(f"b2s{j}", [P, D]) for j in range(NB)]
        hT = [a.sb(f"hT{j}", [P, HT, EC]) for j in range(2)]
        ys = [a.sb(f"ys{j}", [P, 2, D]) for j in range(2)]
        vbank = [a.bank(f"vbank{i}") for i in range(RING)]
        sbank = [a.bank(f"sbank{i}") for i in range(RING)]
        consts_in = a.sem("consts_in")
        init_done = a.sem("init_done")
        b1_mm = a.sem("b1_mm")
        b1_ready = a.sem("b1_ready")
        v_filled, v_freed = a.sem("v_filled"), a.sem("v_freed")
        s_filled, s_freed = a.sem("s_filled"), a.sem("s_freed")
        w1_in = [a.sem(f"w1_in{j}") for j in range(NB)]
        w2_in = [a.sem(f"w2_in{j}") for j in range(NB)]
        vec_step = a.sem("vec_step")
        pool_step = a.sem("pool_step")
        carried = a.sem("carried")
        wA_ready = a.sem("wA_ready")
        xwB_ready = a.sem("xwB_ready")
        ys_stored = [a.sem(f"ys_stored{j}") for j in range(2)]
        block = ctx.enter_context(nc.Block())
        VN, SN = 2 * NB, 3 * NB
        N_W = 2

        def expert(i, j):
            return HALF * (j // 2) + 2 * i + j % 2

        @block.sync
        def _(sp):
            sp.dma_start(ident[:], c_ident).then_inc(consts_in, 16)
            sp.dma_start(b1_in[:], b1).then_inc(consts_in, 16)
            w1v = w1.rearrange("(h i e) d k -> h e i d k", h=2, e=2)
            w2v = w2.rearrange("(h i e) k d -> h e i k d", h=2, e=2)
            b2v = b2.rearrange("(h i e) d -> h e i d", h=2, e=2)
            yv = ys_d.rearrange("(k b) (h i e p) d -> h e k i b p d", k=2, h=2, e=2, p=SLOTS_PER)

            def load_w1(i, j):
                h, e, r = j // 2, j % 2, DB * (j // 2)
                sp.dma_start(w1a[j][:], w1v[h, e, i, 0:P, :]).then_inc(w1_in[j], 16)
                sp.dma_start(w1b[j][r:r + DB, :], w1v[h, e, i, P:D, :]).then_inc(w1_in[j], 16)

            def load_w2(i, j):
                h, e = j // 2, j % 2
                sp.dma_start(w2s[j][:], w2v[h, e, i].rearrange("(t p) d -> p t d", p=P)).then_inc(w2_in[j], 16)
                sp.dma_start(b2s[j][:], b2v[h, e, i].unsqueeze(0).to_broadcast([P, D])).then_inc(w2_in[j], 16)

            for j in range(NB):
                load_w1(0, j)
            for j in range(NB):
                load_w2(0, j)
            for u in range(2):
                load_tokens(sp, ahead, e2_d, h2_d, u, 0)
            with sp.Fori(0, N_EXP // NB) as i:
                for j in range(NB):
                    sp.wait_ge(v_freed, RING + i * VN + 2 * j + 2)
                    load_w1((i + 1) % (N_EXP // NB), j)
                    load_w2((i + 1) % (N_EXP // NB), j)
                    for k in range(2):
                        sp.dma_start(yv[j // 2, j % 2, k, i], ys[j % 2][:, k, :]).then_inc(ys_stored[j % 2], 16)
            for j in range(NB):
                sp.wait_ge(w1_in[j], 16 * N_W * (1 + N_EXP // NB))
                sp.wait_ge(w2_in[j], 16 * N_W * (1 + N_EXP // NB))
            for j in range(2):
                sp.wait_ge(ys_stored[j], 32 * (1 + N_EXP // 2))

        @block.gpsimd
        def _(pool):
            with pool.Fori(0, N_EXP // NB) as i:
                for j in range(NB):
                    pool.wait_ge(w1_in[j], 16 * N_W * (i + 1))
                    pool.sem_inc(carried, 1)
                    pool.tensor_copy(wAh[j][:].bitcast(F32R), w1a[j][:]).then_inc(pool_step, 1)
                    pool.wait_ge(pool_step, NB * i + j + 1)
                    pool.tensor_tensor(wAl[j][:].bitcast(F32R), w1a[j][:], wAh[j][:], ALU.subtract).then_inc(wA_ready, 1)

        @block.tensor
        def _(pe):
            pe.wait_ge(consts_in, 32)
            for t in range(HT):
                pe.transpose(vbank[0][:, t * N_EXP:(t + 1) * N_EXP], b1_in[:, t * P:t * P + P], ident[0:N_EXP, 0:N_EXP]
                             ).then_inc(b1_mm, 1)
            pe.wait_ge(b1_ready, 1)
            with pe.Fori(0, N_EXP // NB) as i:
                v = Uses(vbank, VN)
                s = Uses(sbank, SN)
                at = {}

                def up(j):
                    pe.wait_ge(wA_ready, NB * i + j + 1)
                    pe.wait_ge(xwB_ready, NB * i + j + 1)
                    for t in range(HT):
                        o = s.take()
                        c = slice(t * P, t * P + P)
                        pe.wait_ge(s_freed, s.free(i))
                        terms = ((wAh[j], xAh[j]), (wAh[j], xAl[j]), (wAl[j], xAh[j]), (wBs[j], xBs[j]), (wBl[j], xBs[j]))
                        for k, (w, x) in enumerate(terms):
                            mm = pe.matmul(o[:, 0:EC], w[:, c].bitcast(F32R), x[:].bitcast(F32R), start=(k == 0),
                                           stop=(k == len(terms) - 1))
                        mm.then_inc(s_filled, 1)
                    at[j] = s.n

                def down(j):
                    pe.wait_ge(s_freed, s.read(i, at[j]))
                    pe.wait_ge(w2_in[j], 16 * N_W * (i + 1))
                    for k in range(2):
                        o = v.take()
                        pe.wait_ge(v_freed, v.free(i))
                        for t in range(HT):
                            mm = pe.matmul(o[:, 0:D], hT[j % 2][:, t, k * P:k * P + P], w2s[j][:, t, :],
                                           start=(t == 0), stop=(t == HT - 1))
                        mm.then_inc(v_filled, 1)

                up(0)
                up(1)
                down(0)
                up(2)
                down(1)
                up(3)
                down(2)
                down(3)
                v.end()
                s.end()

        @block.scalar
        def _(act):
            act.sem_inc(s_freed, RING)
            with act.Fori(0, N_EXP // NB) as i:
                s = Uses(sbank, SN)
                for j in range(NB):
                    n = expert(i, j)
                    for t in range(HT):
                        o = s.take()
                        act.wait_ge(s_filled, s.filled(i))
                        act.activation(hT[j % 2][:, t, :], o[:, 0:EC], ACT.Gelu, bias=b1T[:, t, bass.ds(n, 1)]
                                       ).then_inc(s_freed, 1)
                s.end()

        @block.vector
        def _(dve):
            dve.sem_inc(v_freed, RING)
            for j in range(2):
                dve.sem_inc(ys_stored[j], 32)
            for j in range(NB):
                r = DB * (1 - j // 2)
                dve.memset(wBl[j][r:r + DB, :], 0.0).then_inc(init_done, 1)
            dve.wait_ge(b1_mm, HT)
            dve.tensor_copy(b1T[:], vbank[0][:, 0:HT * N_EXP].rearrange("p (t n) -> p t n", t=HT)).then_inc(b1_ready, 1)
            dve.wait_ge(b1_ready, 1)
            dve.wait_ge(init_done, NB)

            def split(i, nx, j):
                own, other = (slice(DB * h, DB * h + DB) for h in (j // 2, 1 - j // 2))
                xa = xsTa[:, bass.ds(expert(nx, j), 1), :].squeeze(1)
                xb = xsTb[own, bass.ds(2 * nx + j % 2, 1), :].squeeze(1)
                dve.wait_ge(w1_in[j], 16 * N_W * (i + 1))
                dve.tensor_copy(wBs[j][own, :].bitcast(F32R), w1b[j][own, :])
                dve.tensor_scalar(xAh[j][:].bitcast(F32R), xa[:, 0:EC], xa[:, EC:EC1], None, ALU.add)
                dve.tensor_scalar(xBs[j][own, :].bitcast(F32R), xb[:, 0:EC], xb[:, EC:EC1], None, ALU.add
                                  ).then_inc(vec_step, 1)
                dve.wait_ge(vec_step, NB * i + j + 1)
                dve.tensor_copy(wBs[j][other, :].bitcast(F32R), wBs[j][own, :])
                dve.tensor_tensor(wBl[j][own, :].bitcast(F32R), w1b[j][own, :], wBs[j][own, :], ALU.subtract)
                dve.scalar_tensor_tensor(xAl[j][:].bitcast(F32R), xa[:, 0:EC], xa[:, EC:EC1], xAh[j][:], ALU.add,
                                         ALU.subtract)
                dve.scalar_tensor_tensor(xBs[j][other, :].bitcast(F32R), xb[:, 0:EC], xb[:, EC:EC1], xBs[j][own, :],
                                         ALU.add, ALU.subtract).then_inc(xwB_ready, 1)

            split(0, 0, 0)
            split(0, 0, 1)
            with dve.Fori(0, N_EXP // NB) as i:
                v = Uses(vbank, VN)

                def outputs(j):
                    dve.wait_ge(ys_stored[j % 2], 32 * (2 * i + j // 2 + 1))
                    dve.wait_ge(w2_in[j], 16 * N_W * (i + 1))
                    for k in range(2):
                        o = v.take()
                        dve.wait_ge(v_filled, v.filled(i))
                        dve.tensor_tensor(ys[j % 2][:, k, :], o[:, 0:D], b2s[j][:], ALU.add).then_inc(v_freed, 1)

                split(i, i, 2)
                outputs(0)
                split(i, i, 3)
                outputs(1)
                nx = (i + 1) % (N_EXP // NB)
                split(i + 1, nx, 0)
                outputs(2)
                split(i + 1, nx, 1)
                outputs(3)
                v.end()


CW = 4


class Ahead:

    def __init__(self, nc, ctx, tag, *space):
        a = Alloc(nc, ctx, tag)
        self.e2T = [x[:, 0:ST * L].rearrange("p (t c) -> p t c", t=ST) for x in space]
        self.hb = [x[:, ST * L:ST * L + QT * D].rearrange("p (t d) -> p t d", t=QT) for x in space]
        self.loaded = [a.sem(f"loaded{u}") for u in range(len(space))]


def load_tokens(eng, ahead, e2_d, h2_d, u, i):
    e2v = e2_d.rearrange("(i u) p c -> u i p c", u=CW)
    h2v = h2_d.rearrange("(i u) l d -> u i l d", u=CW)
    eng.dma_start(ahead.e2T[u].rearrange("p t c -> p (t c)"), e2v[u, i]).then_inc(ahead.loaded[u], 16)
    eng.dma_start(ahead.hb[u][:, 0:2, :], h2v[u, i, 0:2 * P].rearrange("(t p) d -> p t d", p=P)
                  ).then_inc(ahead.loaded[u], 16)
    eng.dma_start(ahead.hb[u][0:LAST, 2, :], h2v[u, i, 2 * P:L]).then_inc(ahead.loaded[u], 16)


def combine_phase(nc, ahead, h2_d, e2_d, ys_d, out):
    with ExitStack() as ctx:
        a = Alloc(nc, ctx, "co")
        ys = [a.sb(f"ys{u}", [P, ST, D + 1]) for u in range(CW)]
        more = Ahead(nc, ctx, "more", *[a.sb(f"in{u}", [P, ST * L + QT * D])[:] for u in range(2, CW)])
        ahead.e2T += more.e2T
        ahead.hb += more.hb
        ahead.loaded += more.loaded
        e2T, hb, loaded = ahead.e2T, ahead.hb, ahead.loaded
        res = [a.sb(f"res{u}", [P, QT, D]) for u in range(2)]
        rec = a.sb("rec", [P, 2 * QT])
        bank = [a.bank(f"bank{i}") for i in range(2 * QT)]
        ones_set = a.sem("ones_set")
        filled, freed = a.sem("filled"), a.sem("freed")
        rec_ready = a.sem("rec_ready")
        stored = [a.sem(f"stored{u}") for u in range(2)]
        block = ctx.enter_context(nc.Block())
        N_IN = 5
        ysv = ys_d.rearrange("(i u) (k t p) d -> u i k p t d", u=CW, k=2, p=P)

        def load_outputs(eng, u, i, k):
            eng.dma_start(ys[u][:, ST // 2 * k:ST // 2 * (k + 1), 0:D], ysv[u, i, k]).then_inc(loaded[u], 16)

        @block.sync
        def _(sp):
            for u in range(CW):
                load_outputs(sp, u, 0, 0)
                if u >= 2:
                    load_tokens(sp, ahead, e2_d, h2_d, u, 0)
            with sp.Fori(1, B // CW) as i:
                for u in range(CW):
                    sp.wait_ge(freed, QT * (CW * (i - 1) + u + 3))
                    for k in range(2):
                        load_outputs(sp, u, i, k)
                    load_tokens(sp, ahead, e2_d, h2_d, u, i)

        @block.scalar
        def _(act):
            for u in range(CW):
                load_outputs(act, u, 0, 1)
            ov = out.rearrange("(i u) l d -> u i l d", u=CW)
            with act.Fori(0, B // CW) as i:
                for u in range(CW):
                    act.wait_ge(freed, QT * (CW * i + u + 3))
                    act.dma_start(ov[u, i, 0:2 * P].rearrange("(t p) d -> p t d", p=P), res[u % 2][:, 0:2, :]
                                  ).then_inc(stored[u % 2], 16)
                    act.dma_start(ov[u, i, 2 * P:L], res[u % 2][0:LAST, 2, :]).then_inc(stored[u % 2], 16)
            for u in range(2):
                act.wait_ge(stored[u], 32 * (1 + B // 2))

        @block.tensor
        def _(pe):
            pe.wait_ge(ones_set, CW)
            with pe.Fori(0, B // CW) as i:
                for u in range(CW):
                    pe.wait_ge(loaded[u], 16 * N_IN * (i + 1))
                    for t in range(QT):
                        r = P if t < 2 else LAST
                        pe.wait_ge(freed, QT * (CW * i + u) + t + 1)
                        for st in range(ST):
                            mm = pe.matmul(bank[QT * (u % 2) + t][0:r, 0:D + 1], e2T[u][:, st, t * P:t * P + r], ys[u][:, st, :],
                                           start=(st == 0), stop=(st == ST - 1))
                        mm.then_inc(filled, 1)

        @block.vector
        def _(dve):
            dve.sem_inc(freed, 2 * QT)
            for u in range(2):
                dve.sem_inc(stored[u], 32)
            for u in range(CW):
                dve.memset(ys[u][:, :, D:D + 1], 1.0).then_inc(ones_set, 1)
            with dve.Fori(0, B // CW) as i:
                for u in range(CW):
                    dve.wait_ge(stored[u % 2], 32 * (CW // 2 * i + u // 2 + 1))
                    for t in range(QT):
                        r = P if t < 2 else LAST
                        o = bank[QT * (u % 2) + t]
                        rc = rec[0:r, QT * (u % 2) + t:QT * (u % 2) + t + 1]
                        dve.wait_ge(filled, QT * (CW * i + u) + t + 1)
                        dve.reciprocal(rc, o[0:r, D:D + 1]).then_inc(rec_ready, 1)
                        dve.wait_ge(rec_ready, QT * (CW * i + u) + t + 1)
                        dve.scalar_tensor_tensor(res[u % 2][0:r, t, :], o[0:r, 0:D], rc, hb[u][0:r, t, :],
                                                 ALU.mult, ALU.add).then_inc(freed, 1)


def fusion_kernel(nc, i, out):
    h_d = nc.dram_tensor("h_d", [B, L, D], F32, kind="Internal").ap()
    h2_d = nc.dram_tensor("h2_d", [B, L, D], F32, kind="Internal").ap()
    e2_d = nc.dram_tensor("e2_d", [B, P, ST * L], F32, kind="Internal").ap()
    ys_d = nc.dram_tensor("ys_d", [B, S, D], F32, kind="Internal").ap()
    tok = "L0_tok_"
    f = {n: i["L0_ffn_" + n] for n in ("phi", "ln_g", "ln_b", "w1", "b1", "w2", "b2")}
    with ExitStack() as phi_ctx:
        p = Alloc(nc, phi_ctx, "phi")
        ph = p.sb("parts", [P, 4, S])
        phis = [ph[0:r, k, :] for k, r in enumerate((P, P, P, DB))]
        with ExitStack() as ctx:
            a = Alloc(nc, ctx, "attn")
            attn = {
                "ident": a.sb("ident", [P, P]),
                "identb": a.sb("identb", [P, P], BF16),
                "identr": a.sb("identr", [P, P]),
                "mask": a.sb("mask", [P, 2, P], BF16),
                "rope": a.sb("rope", [P, QT, 2 * HD]),
                "wa": a.sb("wa", [P, 4, D]),
                "wb": a.sb("wb", [DB + 1, 4, D]),
            }
            attn_in = [i[n] for n in ("c_mask", "c_maskT", "c_rope")] \
                + [i["L0_attn_" + n] for n in ("Wq", "bq", "Wk", "bk", "Wv", "bv", "Wo", "bo")]
            patch_phase(nc, i["x"], i["txt"], i[tok + "freq_weight_h"], i[tok + "freq_weight_w"], i[tok + "proj_w"],
                        i[tok + "proj_b"], i[tok + "cls_token"], i[tok + "position_embeddings"], i["c_dft"],
                        i["c_selh"], i["c_selw"], i["c_ident"], h_d, f["phi"], phis, attn, attn_in)
            attention_phase(nc, h_d, attn, h2_d)
        with ExitStack() as ctx:
            xsTa = ctx.enter_context(nc.sbuf_tensor("xsTa", [P, N_EXP, EC1], F32))
            xsTb = ctx.enter_context(nc.sbuf_tensor("xsTb", [P, HALF, EC1], F32))
            dispatch_phase(nc, xsTa, xsTb, h2_d, phis, f["ln_g"], f["ln_b"], i["c_ident"], e2_d)
            ahead1 = ctx.enter_context(nc.sbuf_tensor("ahead1", [P, ST * L + QT * D], F32))
            ahead = Ahead(nc, ctx, "ahead", ph[:].rearrange("p k s -> p (k s)"), ahead1[:])
            expert_phase(nc, xsTa, xsTb, f["w1"], f["b1"], f["w2"], f["b2"], i["c_ident"], ys_d, ahead, e2_d, h2_d)
            combine_phase(nc, ahead, h2_d, e2_d, ys_d, out)


_INS = ["x", "txt", "L0_tok_freq_weight_h", "L0_tok_freq_weight_w", "L0_tok_proj_w", "L0_tok_proj_b",
        "L0_tok_cls_token", "L0_tok_position_embeddings", "L0_attn_Wq", "L0_attn_bq", "L0_attn_Wk", "L0_attn_bk",
        "L0_attn_Wv", "L0_attn_bv", "L0_attn_Wo", "L0_attn_bo", "L0_ffn_phi", "L0_ffn_ln_g", "L0_ffn_ln_b",
        "L0_ffn_w1", "L0_ffn_b1", "L0_ffn_w2", "L0_ffn_b2"]


def kernel(**inputs):
    import concourse.bacc as _bacc
    from concourse.bass_utils import run_bass_kernel_spmd as _run

    nc = _bacc.Bacc("TRN2", target_bir_lowering=False, num_devices=1)
    arrays, args = {}, {}
    for name, value in [(n, inputs[n]) for n in _INS] + list(shape_constants().items()):
        v = np.ascontiguousarray(value)
        arrays[f"in_{name}_dram"] = v
        args[name] = nc.dram_tensor(f"in_{name}_dram", v.shape, mybir.dt.from_np(v.dtype), kind="ExternalInput").ap()
    out = nc.dram_tensor("out_0_dram", (B, L, D), F32, kind="ExternalOutput").ap()
    fusion_kernel(nc, args, out)
    r = _run(nc, [arrays], core_ids=[0])
    return r.results[0]["out_0_dram"]
```
